# Optimizing a Trainium2 kernel written in Bass

```python
import numpy as np
import jax
import jax.numpy as jnp

def _softmax(x, axis=-1):
    return jax.nn.softmax(x, axis=axis)

def _gelu(x):
    return jax.nn.gelu(x, approximate=True)

def _silu(x):
    return jax.nn.silu(x)

def _sigmoid(x):
    return jax.nn.sigmoid(x)

def _layernorm(x, axis=-1, eps=1e-05):
    m = jnp.mean(x, axis=axis, keepdims=True)
    v = jnp.var(x, axis=axis, keepdims=True)
    return (x - m) / jnp.sqrt(v + eps)

def _scatter_add(tgt, idx, src, axis=0):
    return tgt.at[idx].add(src)

def _segment_sum(src, seg, n):
    return jax.ops.segment_sum(src, seg, n)
kernel_name = 'mk_gnn_ffn_d1_gnn_r8_e6a30b'

def setup_inputs(seed: int=0):
    np.random.seed(seed)
    _w = jnp.asarray

    def _rec_inputs():
        import jax
        import jax.numpy as jnp
        _gk = jax.random.key(seed)
        x = -0.0002117 + 1 * jax.random.normal(jax.random.fold_in(_gk, 1), (6250, 256), jnp.float32)
        src = jax.random.randint(jax.random.fold_in(_gk, 2), (200000,), 0, 6250, jnp.int32)
        dst = jnp.minimum((6250 * jax.random.uniform(jax.random.fold_in(_gk, 3), (200000,)) ** 2.0).astype(jnp.int32), 49999)
        _o = jnp.argsort(dst, stable=True)
        src = src[_o]
        dst = dst[_o]
        return (x, src, dst)
    x, src, dst = _rec_inputs()

    def _L0_gnn_setup():
        import jax, jax.numpy as jnp
        import numpy as np
        N_NODES = 12500
        N_EDGES = 200000
        D_IN = 256
        D_OUT = 256
        key = jax.random.key(seed)
        k1, k2, k3, k4 = jax.random.split(key, 4)
        x = jax.random.normal(k1, (N_NODES, D_IN), dtype=jnp.float32)
        edge_index = jax.random.randint(k2, (2, N_EDGES), 0, N_NODES, dtype=jnp.int64)
        W = jax.random.normal(k3, (D_OUT, D_IN), dtype=jnp.float32) * (1.0 / np.sqrt(D_IN))
        b = jax.random.normal(k4, (D_OUT,), dtype=jnp.float32) * 0.01
        return {'x': x, 'edge_index': edge_index, 'W': W, 'b': b}
    _L0_gnn_all = _L0_gnn_setup()
    _L0_gnn_in = {k: v for k, v in _L0_gnn_all.items() if k in ('W', 'b')}
    del _L0_gnn_all

    def _L0_ffn_setup():
        import jax, jax.numpy as jnp
        import numpy as np
        B, N, D = (16, 512, 256)
        NUM_EXPERTS, TOP_K, HEADS = (4, 2, 4)
        N_EDGES = 131072
        LN_EPS = 1e-05

        def _layernorm(x, g, b):
            mu = x.mean(-1, keepdims=True)
            var = ((x - mu) ** 2).mean(-1, keepdims=True)
            return (x - mu) * jax.lax.rsqrt(var + LN_EPS) * g + b

        def _forward(x, edge_index, W_gat, att_src, att_dst, b_gat, ln_gamma, ln_beta, W1, b1, W2, b2):
            Bc, Nc, Dc = x.shape
            M = Bc * Nc
            x_flat = x.reshape(M, Dc)
            h = (x_flat @ W_gat).reshape(M, HEADS, NUM_EXPERTS)
            loops = jnp.arange(M, dtype=edge_index.dtype)
            src = jnp.concatenate([edge_index[0], loops])
            dst = jnp.concatenate([edge_index[1], loops])
            a_src = (h * att_src).sum(-1)
            a_dst = (h * att_dst).sum(-1)
            e = jax.nn.leaky_relu(a_src[src] + a_dst[dst], negative_slope=0.2)
            e_max = jax.ops.segment_max(e, dst, num_segments=M)
            ee = jnp.exp(e - e_max[dst])
            denom = jax.ops.segment_sum(ee, dst, num_segments=M)
            alpha = ee / (denom[dst] + 1e-16)
            msg = h[src] * alpha[:, :, None]
            agg = jax.ops.segment_sum(msg, dst, num_segments=M).reshape(M, HEADS * NUM_EXPERTS) + b_gat
            scores = _layernorm(agg, ln_gamma, ln_beta).reshape(M, HEADS, NUM_EXPERTS).mean(1)
            scores = scores.reshape(Bc, Nc, NUM_EXPERTS)
            topk_s, topk_i = jax.lax.top_k(scores, TOP_K)
            w = jax.nn.softmax(topk_s, axis=-1)
            out = jnp.zeros_like(x)
            for ei in range(NUM_EXPERTS):
                g = jnp.where(topk_i == ei, w, 0.0).sum(-1)
                hh = jax.nn.gelu(x @ W1[ei] + b1[ei], approximate=False)
                out = out + g[..., None] * (hh @ W2[ei] + b2[ei])
            return out
        key = jax.random.key(seed)
        ks = jax.random.split(key, 8)
        s = 0.05
        return {'x': jax.random.normal(ks[0], (B, N, D), jnp.float32), 'W_gat': jax.random.normal(ks[1], (D, HEADS * NUM_EXPERTS), jnp.float32) * s, 'att_src': jax.random.normal(ks[2], (HEADS, NUM_EXPERTS), jnp.float32) * s, 'att_dst': jax.random.normal(ks[3], (HEADS, NUM_EXPERTS), jnp.float32) * s, 'b_gat': jnp.zeros((HEADS * NUM_EXPERTS,), jnp.float32), 'ln_gamma': jnp.ones((HEADS * NUM_EXPERTS,), jnp.float32), 'ln_beta': jnp.zeros((HEADS * NUM_EXPERTS,), jnp.float32), 'W1': jax.random.normal(ks[4], (NUM_EXPERTS, D, 2 * D), jnp.float32) * s, 'b1': jnp.zeros((NUM_EXPERTS, 2 * D), jnp.float32), 'W2': jax.random.normal(ks[5], (NUM_EXPERTS, 2 * D, D), jnp.float32) * s, 'b2': jnp.zeros((NUM_EXPERTS, D), jnp.float32), 'edge_index': jax.random.randint(ks[6], (2, N_EDGES), 0, B * N, jnp.int32)}
    _L0_ffn_all = _L0_ffn_setup()
    _L0_ffn_in = {k: v for k, v in _L0_ffn_all.items() if k in ('W_gat', 'att_src', 'att_dst', 'b_gat', 'ln_gamma', 'ln_beta', 'W1', 'b1', 'W2', 'b2', 'edge_index')}
    del _L0_ffn_all
    return {'x': x, 'src': src, 'dst': dst, 'L0_gnn_W': _L0_gnn_in['W'], 'L0_gnn_b': _L0_gnn_in['b'], 'L0_ffn_W_gat': _L0_ffn_in['W_gat'], 'L0_ffn_att_src': _L0_ffn_in['att_src'], 'L0_ffn_att_dst': _L0_ffn_in['att_dst'], 'L0_ffn_b_gat': _L0_ffn_in['b_gat'], 'L0_ffn_ln_gamma': _L0_ffn_in['ln_gamma'], 'L0_ffn_ln_beta': _L0_ffn_in['ln_beta'], 'L0_ffn_W1': _L0_ffn_in['W1'], 'L0_ffn_b1': _L0_ffn_in['b1'], 'L0_ffn_W2': _L0_ffn_in['W2'], 'L0_ffn_b2': _L0_ffn_in['b2'], 'L0_ffn_edge_index': _L0_ffn_in['edge_index']}

def reference(x, src, dst, L0_gnn_W, L0_gnn_b, L0_ffn_W_gat, L0_ffn_att_src, L0_ffn_att_dst, L0_ffn_b_gat, L0_ffn_ln_gamma, L0_ffn_ln_beta, L0_ffn_W1, L0_ffn_b1, L0_ffn_W2, L0_ffn_b2, L0_ffn_edge_index):
    import jax
    import jax.numpy as jnp

    def _L0_gnn_ref(x, edge_index, W, b):
        import jax, jax.numpy as jnp
        import numpy as np
        N_NODES = 12500
        N_EDGES = 200000
        D_IN = 256
        D_OUT = 256
        h = jnp.einsum('nd,od->no', x, W) + b
        row, col = (edge_index[0], edge_index[1])
        msgs = h[col]
        out = jax.ops.segment_sum(msgs, row, num_segments=h.shape[0])
        return out

    def _L0_ffn_ref(x, W_gat, att_src, att_dst, b_gat, ln_gamma, ln_beta, W1, b1, W2, b2, edge_index):
        import jax, jax.numpy as jnp
        import numpy as np
        B, N, D = (16, 512, 256)
        NUM_EXPERTS, TOP_K, HEADS = (4, 2, 4)
        N_EDGES = 131072
        LN_EPS = 1e-05

        def _layernorm(x, g, b):
            mu = x.mean(-1, keepdims=True)
            var = ((x - mu) ** 2).mean(-1, keepdims=True)
            return (x - mu) * jax.lax.rsqrt(var + LN_EPS) * g + b

        def _forward(x, edge_index, W_gat, att_src, att_dst, b_gat, ln_gamma, ln_beta, W1, b1, W2, b2):
            Bc, Nc, Dc = x.shape
            M = Bc * Nc
            x_flat = x.reshape(M, Dc)
            h = (x_flat @ W_gat).reshape(M, HEADS, NUM_EXPERTS)
            loops = jnp.arange(M, dtype=edge_index.dtype)
            src = jnp.concatenate([edge_index[0], loops])
            dst = jnp.concatenate([edge_index[1], loops])
            a_src = (h * att_src).sum(-1)
            a_dst = (h * att_dst).sum(-1)
            e = jax.nn.leaky_relu(a_src[src] + a_dst[dst], negative_slope=0.2)
            e_max = jax.ops.segment_max(e, dst, num_segments=M)
            ee = jnp.exp(e - e_max[dst])
            denom = jax.ops.segment_sum(ee, dst, num_segments=M)
            alpha = ee / (denom[dst] + 1e-16)
            msg = h[src] * alpha[:, :, None]
            agg = jax.ops.segment_sum(msg, dst, num_segments=M).reshape(M, HEADS * NUM_EXPERTS) + b_gat
            scores = _layernorm(agg, ln_gamma, ln_beta).reshape(M, HEADS, NUM_EXPERTS).mean(1)
            scores = scores.reshape(Bc, Nc, NUM_EXPERTS)
            topk_s, topk_i = jax.lax.top_k(scores, TOP_K)
            w = jax.nn.softmax(topk_s, axis=-1)
            out = jnp.zeros_like(x)
            for ei in range(NUM_EXPERTS):
                g = jnp.where(topk_i == ei, w, 0.0).sum(-1)
                hh = jax.nn.gelu(x @ W1[ei] + b1[ei], approximate=False)
                out = out + g[..., None] * (hh @ W2[ei] + b2[ei])
            return out
        return _forward(x, edge_index, W_gat, att_src, att_dst, b_gat, ln_gamma, ln_beta, W1, b1, W2, b2)
    edge_index = jnp.stack([src, dst])
    x = x + _L0_gnn_ref(_layernorm(x, axis=-1), edge_index, L0_gnn_W, L0_gnn_b)
    x = x + _L0_ffn_ref(_layernorm(x, axis=-1)[None], L0_ffn_W_gat, L0_ffn_att_src, L0_ffn_att_dst, L0_ffn_b_gat, L0_ffn_ln_gamma, L0_ffn_ln_beta, L0_ffn_W1, L0_ffn_b1, L0_ffn_W2, L0_ffn_b2, L0_ffn_edge_index)[0]
    return x

_drawn_inputs = setup_inputs


def setup_inputs(seed=0):
    import zlib

    import numpy as np

    out = dict(_drawn_inputs(seed))
    spreads = {'L0_ffn_b_gat': (0.0, 0.1),
     'L0_ffn_ln_gamma': (1.0, 0.2),
     'L0_ffn_ln_beta': (0.0, 0.437),
     'L0_ffn_b1': (0.0, 0.8),
     'L0_ffn_b2': (0.0, 0.657)}
    factors = {'L0_ffn_att_src': 4.83, 'L0_ffn_att_dst': 6.778}
    for name, (base, spread) in spreads.items():
        noise = np.random.default_rng([zlib.crc32(name.encode()), seed]).standard_normal(out[name].shape)
        drawn = base * np.exp(spread * noise) if base else spread * noise
        out[name] = jnp.asarray(drawn.astype(out[name].dtype))
    for name, factor in factors.items():
        out[name] = (out[name] * factor).astype(out[name].dtype)
    return out
```

```python
import concourse.bass as bass
from concourse import mybir
from concourse.alu_op_type import AluOpType as ALU
from contextlib import ExitStack

F32 = mybir.dt.float32
BF16 = mybir.dt.bfloat16
I32 = mybir.dt.int32
ACT = mybir.ActivationFunctionType
AX = mybir.AxisListType

P = 128
KEY_BIAS = 0x10000000
FIELD = 0x1FFF
SORT_W = 2048
SORT_BITS = 18
ROW_BITS = 11
EPS = 1e-5
NEG = -3.0e38


def sort_plan():
    steps, cur = [], 0

    def add(kind, *what):
        nonlocal cur
        steps.append((kind, cur, *what))
        cur ^= 1

    add("flip", 0, None)
    for k in range(1, ROW_BITS + 1):
        for j in range(k - 1, -1, -1):
            add("pair", 1 << j, j == k - 1)
    for k in range(ROW_BITS + 1, SORT_BITS + 1):
        add("flip", k - ROW_BITS - 1, k - ROW_BITS if k < SORT_BITS else None)
        add("turn")
        for j in range(k - ROW_BITS - 1, -1, -1):
            add("pair", 1 << j, False)
        add("turn")
        for j in range(ROW_BITS - 1, -1, -1):
            add("pair", 1 << j, False)
    return steps, cur


SORT_STEPS, SORTED_IN = sort_plan()
TURNS = [s[1] for s in SORT_STEPS if s[0] == "turn"]


def gnn_ffn_kernel(nc, x, src, dst, gnn_W, gnn_b, W_gat, att_src, att_dst, b_gat, ln_gamma, ln_beta,
                   W1, b1, W2, b2, edge_index, out):
    N, D = x.shape
    E1 = src.shape[0]
    E2 = edge_index.shape[1]
    EXP, _, HID = W1.shape
    HEADS = att_src.shape[0]
    FEAT = HEADS * EXP
    ROW = FEAT + 2 * HEADS
    KC = D // P
    FC = HID // P
    NB = -(-N // P)
    NBP = NB + 1
    TAIL = N - (NB - 1) * P
    E1_P, E1_W = 125, E1 // 125
    WIN = 2
    G = WIN * P
    RING = 8
    PRING = 4
    STEPS = -(-(E1 // G + 1 + NB) // RING) * RING
    ITERS = STEPS // RING
    E2_W = E2 // P
    HQ = -(-E2_W // ITERS)
    HCOLS = HQ * ITERS
    MARKS = NB
    GG, GQ = 3, 4
    TG = -(-(E2 + P * MARKS) // (P * GG * GQ)) * GG * GQ
    GITERS = TG // (GG * GQ)
    CHT = 4
    CH = CHT * P
    NCH = NB // CHT
    REST = NB - NCH * CHT

    ctx = ExitStack()
    with ctx:
        dram = lambda n, s, d=F32: nc.dram_tensor(n, s, d, kind="Internal").ap()
        pairs_d = dram("pairs_d", (P * SORT_W, 2))
        keys2_d = dram("keys2_d", (P * SORT_W,), I32)
        h_d = dram("h_d", (NBP * P, D))
        x1_d = dram("x1_d", (NBP * P, D))
        xT_d = dram("xT_d", (P, NBP, KC * P))
        tab_d = dram("tab_d", (NBP * P, ROW))
        y_d = dram("y_d", (NB * P, EXP, D))
        sums_d = dram("sums_d", (P * TG, ROW))

        def sb(name, shape, dt=F32):
            return ctx.enter_context(nc.sbuf_tensor(name, shape, dt))

        def sem(name):
            return ctx.enter_context(nc.semaphore(name))

        big = sb("big", [P, TG * ROW])
        nodes = big[:, 0:NBP * D]
        o = NBP * D
        sortbuf = [big[:, o:o + SORT_W], big[:, o + SORT_W:o + 2 * SORT_W]]
        o += 2 * SORT_W
        pairs = big[:, o:o + 2 * SORT_W].rearrange("p (t w) -> p t w", w=2)
        pairs_i = big[:, o:o + 2 * SORT_W].bitcast(I32).rearrange("p (t w) -> p t w", w=2)
        raw_a = big[:, o:o + SORT_W].bitcast(I32)
        raw_b = big[:, o + SORT_W:o + 2 * SORT_W].bitcast(I32)
        o += 2 * SORT_W
        rows_raw = big[0:E1_P, o:o + E1_W].bitcast(I32)
        o += E1_W
        dig_hi, dig_lo = big[:, o:o + HCOLS], big[:, o + HCOLS:o + 2 * HCOLS]
        o += 2 * HCOLS
        block_base = big[:, o:o + STEPS]
        o += STEPS
        assert o <= TG * ROW
        edges = big[:, :].rearrange("p (t f) -> p t f", f=ROW)

        gathered = sb("gathered", [P, RING, WIN, D])
        hidden = gathered[:, :, :, :].rearrange("p r t c -> p (r t c)").rearrange("p (s f c) -> p s f c", s=2, f=FC)
        mid = sb("mid", [P, RING * WIN * P])
        onehot = mid[:, :].rearrange("p (r t c) -> p r t c", r=RING, t=WIN)
        junk = mid[:, 0:E1_W // 2].bitcast(BF16)
        yst = mid[:, :].rearrange("p (s n c) -> p s n c", s=2, n=CHT)
        flat = gathered[:, :, :, :].rearrange("p r t c -> p (r t c)")
        step_iota, block_over = flat[:, 0:STEPS], flat[:, STEPS:2 * STEPS]
        mark_iota = sb("mark_iota", [P, MARKS], I32)
        node_iota = sb("node_iota", [P, 64])
        idx_slot = sb("idx_slot", [P, RING, WIN, 2])
        ident = sb("ident", [P, P])
        iota_c = sb("iota_c", [P, P])
        tri = sb("tri", [P, P])
        ones = sb("ones", [P, P])
        iota_i = sb("iota_i", [P, 8], I32)
        bits = sb("bits", [P, 8], I32)
        sign = sb("sign", [P, 8])
        thr = sb("thr", [P, NBP])
        signsum = sb("signsum", [P, NBP])
        zero_bf = sb("zero_bf", [P, P], BF16)
        iota_bf = sb("iota_bf", [P, P], BF16)
        oh_hi = sb("oh_hi", [P, HQ, 64], BF16)
        oh_lo = sb("oh_lo", [P, HQ, P], BF16)
        late = sb("late", [P, CHT * KC * P + NBP * ROW])
        step_tab = late[0:1, 0:2 * STEPS].bitcast(I32).rearrange("p (a k) -> p a k", a=2)
        xc = late[:, 0:CHT * KC * P].rearrange("p (n c) -> p n c", n=CHT)
        table = late[:, CHT * KC * P:].rearrange("p (n f) -> p n f", f=ROW)
        small = sb("small", [P, 16])
        small_i = sb("small_i", [P, 2], I32)
        end_idx = sb("end_idx", [P, 64], I32)
        histo = sb("histo", [P, 3, 64])
        key2 = flat[:, 2 * STEPS:2 * STEPS + TG + 1].bitcast(I32)
        edge_idx = sb("edge_idx", [P, TG], I32)
        starts = sb("starts", [P, TG + 1])
        inside = sb("inside", [P, TG + 1])
        gat_ring = sb("gat_ring", [P, GG, GQ, ROW])
        gat_slot = sb("gat_slot", [P, GG, GQ], I32)
        stats = sb("stats", [P, NBP, 6])
        mv = sb("mv", [P, NBP, 2])
        std = sb("std", [P, NBP])
        rstd = sb("rstd", [P, NBP])
        nmr = sb("nmr", [P, NBP])
        xn = sb("xn", [P, 2, D])
        xT = sb("xT", [P, 2, KC, P])
        hst = sb("hst", [P, 2, D])
        wt = sb("wt", [P, KC, D])
        wraw = sb("wraw", [P, KC, D])
        brow = sb("brow", [1, D])
        wg = sb("wg", [P, KC, FEAT])
        att = sb("att", [P, 2, FEAT])
        gpar = sb("gpar", [P, 3, FEAT])
        weights = sb("weights", [P, EXP * (KC * HID + FC * D)])
        w1s = weights[:, 0:EXP * KC * HID].rearrange("p (e k f) -> p e k f", e=EXP, k=KC)
        w2s = weights[:, EXP * KC * HID:].rearrange("p (e k f) -> p e k f", e=EXP, k=FC)
        top4 = weights[:, 0:HEADS * TG].rearrange("p (h t) -> p h t", h=HEADS)
        scratch = weights[:, HEADS * TG:(HEADS + 1) * TG]
        b1s = sb("b1s", [P, EXP, FC])
        b2s = sb("b2s", [1, EXP, D])
        carry_t = sb("carry_t", [P, FEAT + HEADS])
        carry_f = sb("carry_f", [P, FEAT + HEADS])
        carry_in = sb("carry_in", [P, FEAT + HEADS])
        carry_r = weights[0:FEAT + HEADS, (HEADS + 1) * TG:(HEADS + 1) * TG + 4 * P].rearrange("p (a c) -> p a c", a=2)
        gate = sb("gate", [P, EXP, NB])

        ps = ctx.enter_context(nc.psum_tensor("ps", [P, 8 * 512], F32))
        bank = lambda b: ps[:, b * 512:(b + 1) * 512]
        ps_sort = ps[:, 0:SORT_W]
        ps_step = [bank(j)[:, 0:D] for j in range(PRING)]
        ps_hist = bank(6)[:, 0:64]
        ps_tab = bank(7)

        S = {}

        def s(name):
            if name not in S:
                S[name] = sem(name)
            return S[name]

        raw_in, x_in, w_in, w2_in = s("raw_in"), s("x_in"), s("w_in"), s("w2_in")
        raw2_in = s("raw2_in")
        consts = s("consts")
        vec = s("vec")
        sort_ready, turned, turn_copied = s("sort_ready"), s("turned"), s("turn_copied")
        var_ready, std_ready, norm1_ready = s("var_ready"), s("std_ready"), s("norm1_ready")
        wt_turned, wt_copied = s("wt_turned"), s("wt_copied")
        xn_ready, xn_turned, xT_ready, h_done, h_copied = (s("xn_ready"), s("xn_turned"), s("xT_ready"),
                                                           s("h_done"), s("h_copied"))
        h_stored = [s("h_stored0"), s("h_stored1")]
        sums_ready, count_done, steps_ready, steps_done, tab_ready = (
            s("sums_ready"), s("count_done"), s("steps_ready"), s("steps_done"), s("tab_ready"))
        pairs_ready, pairs_stored = s("pairs_ready"), s("pairs_stored")
        idx_in = [s(f"idx_in{j}") for j in range(RING)]
        rows_in = [s(f"rows_in{j}") for j in range(RING)]
        onehot_ready, step_done, step_added = s("onehot_ready"), s("step_done"), s("step_added")
        digit_ready, digit_done = s("digit_ready"), s("digit_done")
        keys2_ready, keys2_stored, keys2_in = s("keys2_ready"), s("keys2_stored"), s("keys2_in")
        hist_copied, hist_summed = s("hist_copied"), s("hist_summed")
        x1_ready, x1_stored = s("x1_ready"), s("x1_stored")
        xn2_ready, xn2_turned, xT2_ready, g_done, g_copied = (s("xn2_ready"), s("xn2_turned"), s("xT2_ready"),
                                                              s("g_done"), s("g_copied"))
        xT_stored = [s("xT_stored0"), s("xT_stored1")]
        table_ready, table_stored = s("table_ready"), s("table_stored")
        slot_ready, gathers_begun = s("slot_ready"), s("gathers_begun")
        gat_in = [s(f"gat_in{g}") for g in range(GG)]
        xc_in, up_done, act_done, down_done, y_copied = (s("xc_in"), s("up_done"), s("act_done"),
                                                         s("down_done"), s("y_copied"))
        y_stored = [s("y_stored0"), s("y_stored1")]
        tails_ready, tails_turned, carry_ready, carry_turned = (s("tails_ready"), s("tails_turned"),
                                                                s("carry_ready"), s("carry_turned"))
        logit_ready, exp_ready = s("logit_ready"), s("exp_ready")
        edge_sums_ready, edge_sums_stored, node_sums_in = (s("edge_sums_ready"), s("edge_sums_stored"),
                                                           s("node_sums_in"))
        rvar_ready, rstd_in, d_ready, dexp_ready = s("rvar_ready"), s("rstd_in"), s("d_ready"), s("dexp_ready")
        FR = 3
        fin_in = [s(f"fin_in{j}") for j in range(FR)]
        fin_ready, fin_step, stats_in = s("fin_ready"), s("fin_step"), s("stats_in")
        fin_out = [s(f"fin_out{j}") for j in range(FR)]

        finy = big[:, 0:FR * (EXP + 1) * D].rearrange("p (r e c) -> p r e c", r=FR, e=EXP + 1)
        fino = big[:, FR * (EXP + 1) * D:FR * (EXP + 2) * D].rearrange("p (r c) -> p r c", r=FR)
        o2 = FR * (EXP + 2) * D
        nsum = big[:, o2:o2 + NB * ROW].rearrange("p (n f) -> p n f", f=ROW)
        o2 += NB * ROW
        nw = [big[:, o2 + q * NB * FEAT:o2 + (q + 1) * NB * FEAT] for q in range(3)]
        o2 += 3 * NB * FEAT
        nv = [big[:, o2 + q * NB:o2 + (q + 1) * NB] for q in range(14)]
        o2 += 14 * NB
        score = [big[:, o2 + q * NB:o2 + (q + 1) * NB] for q in range(EXP)]
        o2 += EXP * NB
        rank = [big[:, o2 + q * NB:o2 + (q + 1) * NB] for q in range(EXP)]
        o2 += EXP * NB
        den = big[:, o2:o2 + NB * HEADS].rearrange("p (n h) -> p n h", h=HEADS)

        NTURN = len(TURNS)
        block = ctx.enter_context(nc.Block())

        @block.sync
        def _(sp):
            sp.dma_start(rows_raw, src.rearrange("(p t) -> p t", p=E1_P)).then_inc(raw_in, 16)
            sp.dma_start(raw_b[0:E1_P, 0:E1_W], dst.rearrange("(p t) -> p t", p=E1_P)).then_inc(raw_in, 16)
            sp.wait_ge(consts, 1)
            n3 = nodes.rearrange("p (n c) -> p n c", c=D)
            sp.dma_start(n3[:, 0:NB - 1, :], x[0:(NB - 1) * P, :].rearrange("(n p) c -> p n c", p=P)).then_inc(x_in, 16)
            sp.dma_start(n3[0:TAIL, NB - 1, :], x[(NB - 1) * P:N, :]).then_inc(x_in, 16)
            sp.dma_start(wraw[:, :, :], gnn_W.rearrange("(k p) c -> p k c", p=P)).then_inc(w_in, 16)
            sp.dma_start(brow[:, :], gnn_b.rearrange("(a c) -> a c", a=1)).then_inc(w_in, 16)
            sp.dma_start(wg[:, :, :], W_gat.rearrange("(k p) f -> p k f", p=P)).then_inc(w2_in, 16)
            for q, a in enumerate((att_src, att_dst)):
                sp.dma_start(att[:, q, :], a.rearrange("(o h) e -> o (h e)", o=1).to_broadcast([P, FEAT])).then_inc(w2_in, 16)
            for q, a in enumerate((b_gat, ln_gamma, ln_beta)):
                sp.dma_start(gpar[:, q, :], a.rearrange("(o f) -> o f", o=1).to_broadcast([P, FEAT])).then_inc(w2_in, 16)
            for e in range(EXP):
                sp.dma_start(w1s[:, e, :, :], W1[e].rearrange("(k p) f -> p k f", p=P)).then_inc(w2_in, 16)
                sp.dma_start(w2s[:, e, :, :], W2[e].rearrange("(k p) f -> p k f", p=P)).then_inc(w2_in, 16)
                sp.dma_start(b1s[:, e, :], b1[e].rearrange("(f p) -> p f", p=P), allow_slow_non_contiguous=True).then_inc(w2_in, 16)
            sp.dma_start(b2s[:, :, :], b2.rearrange("(o e) c -> o e c", o=1)).then_inc(w2_in, 16)
            with sp.Fori(0, NBP // 2) as i:
                for t in range(2):
                    sp.wait_ge(h_copied, 2 * i + t + 1)
                    sp.dma_start(h_d[bass.ds((2 * i + t) * P, P), :], hst[:, t, :]).then_inc(h_stored[t], 16)
            sp.wait_ge(pairs_ready, 1)
            sp.dma_start(pairs_d.rearrange("(p t) w -> p (t w)", p=P), pairs.rearrange("p t w -> p (t w)")).then_inc(pairs_stored, 16)
            sp.wait_ge(pairs_stored, 16)
            e2 = edge_index.rearrange("a (p t) -> a p t", p=P)
            sp.dma_start(raw_a[:, 0:E2_W], e2[0]).then_inc(raw2_in, 16)
            sp.dma_start(raw_b[:, 0:E2_W], e2[1]).then_inc(raw2_in, 16)
            sp.wait_ge(keys2_ready, 1)
            sp.dma_start(keys2_d.rearrange("(p t) -> p t", p=P), sortbuf[SORTED_IN].bitcast(I32)).then_inc(keys2_stored, 16)
            sp.wait_ge(keys2_stored, 16)
            halo = bass.AP(tensor=keys2_d.tensor, offset=0, ap=[[TG, P], [1, TG + 1]])
            sp.dma_start(key2[:, :], halo).then_inc(keys2_in, 16)
            sp.wait_ge(tab_ready, 1)

            def load_step(i, j, first):
                if not first:
                    sp.wait_ge(step_done, i * RING + j + 1 - RING)
                at = sp.value_load(step_tab[0:1, 0, bass.ds(i * RING + j, 1)], min_val=0, max_val=P * SORT_W - G)
                sp.dma_start(idx_slot[:, j, :, :], pairs_d[bass.ds(at, G), :].rearrange("(p t) w -> p t w", p=P)).then_inc(idx_in[j], 16)

            for j in range(RING):
                load_step(0, j, True)
            with sp.Fori(1, ITERS) as i:
                for j in range(RING):
                    load_step(i, j, False)
            sp.wait_ge(x1_ready, 1)
            sp.dma_start(x1_d.rearrange("(n p) c -> p n c", p=P), n3).then_inc(x1_stored, 16)
            with sp.Fori(0, NBP // 2) as i:
                for t in range(2):
                    sp.wait_ge(xT2_ready, 2 * i + t + 1)
                    sp.dma_start(xT_d[:, bass.ds(2 * i + t, 1), :], xT[:, t, :, :].rearrange("p (o k) c -> p o (k c)", o=1)).then_inc(xT_stored[t], 16)
            sp.wait_ge(table_ready, 1)
            sp.dma_start(tab_d.rearrange("(n p) f -> p n f", p=P), table[:, :, :]).then_inc(table_stored, 16)
            for t in range(2):
                sp.wait_ge(xT_stored[t], 16 * (NBP // 2))

            def load_chunk(start, tiles):
                sp.dma_start(xc[:, 0:tiles, :], xT_d[:, bass.ds(start, tiles), :]).then_inc(xc_in, 16)

            def store_chunk(i, start, tiles, next_tiles):
                for e in range(EXP):
                    if e == EXP - 1 and next_tiles:
                        sp.wait_ge(up_done, (i + 1) * EXP * FC)
                        load_chunk((i + 1) * CHT, next_tiles)
                    sp.wait_ge(y_copied, EXP * i + e + 1)
                    sp.dma_start(y_d[bass.ds(start * P, tiles * P), e, :].rearrange("(n p) c -> p n c", p=P),
                                 yst[:, e % 2, 0:tiles, :]).then_inc(y_stored[e % 2], 16)

            load_chunk(0, CHT)
            with sp.Fori(0, NCH - 1) as i:
                store_chunk(i, i * CHT, CHT, CHT)
            store_chunk(NCH - 1, (NCH - 1) * CHT, CHT, REST)
            store_chunk(NCH, NCH * CHT, REST, 0)
            sp.wait_ge(edge_sums_ready, 1)
            sp.dma_start(sums_d.rearrange("(p t) f -> p (t f)", p=P), big[:, :]).then_inc(edge_sums_stored, 16)
            sp.wait_ge(edge_sums_stored, 16)
            sp.wait_ge(x1_stored, 16)
            for e in range(2):
                sp.wait_ge(y_stored[e], 16 * (NCH + 1) * EXP // 2)

            def load_final(n, j, rows):
                sp.dma_start(finy[0:rows, j, 0:EXP, :], y_d[bass.ds(n * P, rows), :, :]).then_inc(fin_in[j], 16)
                sp.dma_start(finy[0:rows, j, EXP, :], x1_d[bass.ds(n * P, rows), :]).then_inc(fin_in[j], 16)

            def store_final(n, j, rows):
                sp.wait_ge(fin_ready, n + 1)
                sp.dma_start(out[bass.ds(n * P, rows), :], fino[0:rows, j, :]).then_inc(fin_out[j], 16)

            LOOP = (NB - 1) // FR
            for j in range(FR):
                load_final(j, j, P)
            with sp.Fori(0, LOOP - 1) as i:
                for j in range(FR):
                    store_final(i * FR + j, j, P)
                    load_final((i + 1) * FR + j, j, P)
            for j in range(FR):
                store_final((LOOP - 1) * FR + j, j, P)
                if j == 0:
                    load_final(NB - 1, 0, TAIL)
            store_final(NB - 1, 0, TAIL)
            for j in range(FR):
                sp.wait_ge(fin_out[j], 16 * (LOOP + (j == 0)))

        @block.gpsimd
        def _(pool):
            nc.gpsimd.memset(nodes[:, (NB - 1) * D:NBP * D], 0.0).then_inc(consts, 1)
            nc.gpsimd.memset(ident[:, :], 0.0).then_inc(consts, 1)
            nc.gpsimd.memset(tri[:, :], 1.0).then_inc(consts, 1)
            pool.wait_ge(consts, 3)
            nc.gpsimd.affine_select(out=ident[:, :], in_=ident[:, :], compare_op=ALU.not_equal, fill=1.0, base=0,
                                    pattern=[[-1, P]], channel_multiplier=1).then_inc(consts, 1)
            nc.gpsimd.affine_select(out=tri[:, :], in_=tri[:, :], compare_op=ALU.is_ge, fill=0.0, base=0,
                                    pattern=[[1, P]], channel_multiplier=-1).then_inc(consts, 1)
            nc.gpsimd.memset(ones[:, :], 1.0).then_inc(consts, 1)
            nc.gpsimd.memset(zero_bf[:, :], 0.0).then_inc(consts, 1)
            nc.gpsimd.iota(iota_i[:, :], [[0, 8]], base=0, channel_multiplier=1).then_inc(consts, 1)
            nc.gpsimd.iota(iota_c[:, :], [[1, P]], base=0, channel_multiplier=0,
                           allow_small_or_imprecise_dtypes=True).then_inc(consts, 1)
            nc.gpsimd.iota(iota_bf[:, :], [[1, P]], base=0, channel_multiplier=0,
                           allow_small_or_imprecise_dtypes=True).then_inc(consts, 1)
            nc.gpsimd.iota(thr[:, :], [[-P, NBP]], base=0, channel_multiplier=0,
                           allow_small_or_imprecise_dtypes=True).then_inc(consts, 1)
            nc.gpsimd.iota(step_iota, [[1, STEPS]], base=0, channel_multiplier=0,
                           allow_small_or_imprecise_dtypes=True).then_inc(consts, 1)
            nc.gpsimd.iota(mark_iota[:, :], [[1, MARKS]], base=0, channel_multiplier=MARKS).then_inc(consts, 1)
            nc.gpsimd.iota(node_iota[:, :], [[P, 64]], base=0, channel_multiplier=1,
                           allow_small_or_imprecise_dtypes=True).then_inc(consts, 1)
            for t in range(2):
                pool.wait_ge(h_stored[t], 16 * (NBP // 2))

            def gather_step(i, j, first):
                pool.wait_ge(idx_in[j], 16 * i + 16)
                if not first:
                    pool.wait_ge(step_done, i * RING + j + 1 - RING)
                pool.sem_inc(gathers_begun, 1)
                for t in range(WIN):
                    nc.gpsimd.indirect_dma_start(
                        gathered[:, j, t, :], None, h_d[:, :],
                        bass.IndirectOffsetOnAxis(ap=idx_slot[:, j, t, 1:2].bitcast(I32), axis=0)).then_inc(rows_in[j], 16)

            for j in range(RING):
                gather_step(0, j, True)
            with pool.Fori(1, ITERS) as i:
                for j in range(RING):
                    gather_step(i, j, False)
            pool.wait_ge(table_stored, 16)
            with pool.Fori(0, GITERS) as i:
                for g in range(GG):
                    pool.wait_ge(slot_ready, GG * i + g + 1)
                    pool.sem_inc(gathers_begun, 1)
                    for q in range(GQ):
                        nc.gpsimd.indirect_dma_start(
                            gat_ring[:, g, q, :], None, tab_d[:, :],
                            bass.IndirectOffsetOnAxis(ap=gat_slot[:, g, q:q + 1], axis=0)).then_inc(gat_in[g], 16)
            pool.wait_ge(edge_sums_stored, 16)
            for n in range(NB):
                nc.gpsimd.indirect_dma_start(
                    nsum[:, n, :], None, sums_d[:, :],
                    bass.IndirectOffsetOnAxis(ap=end_idx[:, n:n + 1], axis=0)).then_inc(node_sums_in, 16)

        @block.scalar
        def _(act):
            act.wait_ge(wt_turned, 1)
            nc.scalar.activation(wt[:, :, :].rearrange("p k c -> p (k c)"), bank(7), ACT.Copy).then_inc(wt_copied, 1)
            act.wait_ge(var_ready, 1)
            nc.scalar.activation(std[:, :], mv[:, :, 1], ACT.Sqrt).then_inc(std_ready, 1)
            act.wait_ge(norm1_ready, 1)

            def layer_one(i, first):
                for t in range(2):
                    if not first:
                        act.wait_ge(xn_turned, 2 * i + t - 1)
                    nc.scalar.activation(xn[:, t, :], nodes[:, bass.ds((2 * i + t) * D, D)], ACT.Identity,
                                         scale=rstd[:, bass.ds(2 * i + t, 1)],
                                         bias=nmr[:, bass.ds(2 * i + t, 1)]).then_inc(xn_ready, 1)
                for t in range(2):
                    act.wait_ge(xn_turned, 2 * i + t + 1)
                    if not first:
                        act.wait_ge(h_done, 2 * i + t - 1)
                    nc.scalar.activation(xT[:, t, :, :].rearrange("p k c -> p (k c)"), bank(4 + t)[:, 0:D],
                                         ACT.Copy).then_inc(xT_ready, 1)
                for t in range(2):
                    act.wait_ge(h_done, 2 * i + t + 1)
                    if not first:
                        act.wait_ge(h_stored[t], 16 * i)
                    nc.scalar.activation(hst[:, t, :], bank(4 + t)[:, D:2 * D], ACT.Copy).then_inc(h_copied, 1)

            layer_one(0, True)
            with act.Fori(1, NBP // 2) as i:
                layer_one(i, False)

            def turn_copies(n):
                to = sortbuf[1 - TURNS[n % NTURN]]
                for b in range(2):
                    act.wait_ge(turned, 4 * n + b + 1)
                    nc.scalar.activation(to[:, b * 512:(b + 1) * 512], bank(b), ACT.Copy).then_inc(turn_copied, 1)

            act.wait_ge(consts, 15)
            act.wait_ge(raw_in, 32)
            per = -(-NBP // NTURN)
            for n in range(NTURN):
                turn_copies(n)
                for b in range(n * per, min((n + 1) * per, NBP)):
                    if b:
                        act.wait_ge(sums_ready, b)
                    nc.scalar.activation(junk[0:E1_P, :], rows_raw, ACT.Sign, bias=thr[0:E1_P, b:b + 1],
                                         accum_out=signsum[0:E1_P, b:b + 1]).then_inc(sums_ready, 1)
            for n in range(NTURN, 2 * NTURN):
                turn_copies(n)
            act.wait_ge(var_ready, 2)
            nc.scalar.activation(std[:, :], mv[:, :, 1], ACT.Sqrt).then_inc(std_ready, 1)

            def layer_two(i, first):
                for t in range(2):
                    act.wait_ge(xn2_turned, 2 * i + t + 1)
                    if not first:
                        act.wait_ge(g_done, 2 * i + t - 1)
                        act.wait_ge(xT_stored[t], 16 * i)
                    nc.scalar.activation(xT[:, t, :, :].rearrange("p k c -> p (k c)"), bank(4 + t)[:, 0:D],
                                         ACT.Copy).then_inc(xT2_ready, 1)

            layer_two(0, True)
            with act.Fori(1, NBP // 2) as i:
                layer_two(i, False)

            def expert_chunk(i, tiles, first):
                for e in range(EXP):
                    for f in range(FC):
                        act.wait_ge(up_done, (i * EXP + e) * FC + f + 1)
                        if not (first and e < 2):
                            act.wait_ge(down_done, i * EXP + e - 1)
                        nc.scalar.activation(hidden[:, e % 2, f, 0:tiles * P], bank(f % 2)[:, 0:tiles * P], ACT.Gelu,
                                             bias=b1s[:, e, f:f + 1]).then_inc(act_done, 1)
                    act.wait_ge(down_done, i * EXP + e + 1)
                    if not (first and e < 2):
                        act.wait_ge(y_stored[e % 2], 16 * (2 * i + e // 2))
                    nc.scalar.activation(yst[:, e % 2, 0:tiles, :].rearrange("p n c -> p (n c)"),
                                         ps[:, 1024:1024 + tiles * D], ACT.Copy).then_inc(y_copied, 1)

            expert_chunk(0, CHT, True)
            with act.Fori(1, NCH) as i:
                expert_chunk(i, CHT, False)
            expert_chunk(NCH, REST, False)
            act.wait_ge(logit_ready, 1)
            nc.scalar.activation(edges[:, :, FEAT:FEAT + HEADS], edges[:, :, FEAT:FEAT + HEADS], ACT.Exp).then_inc(exp_ready, 1)
            act.wait_ge(rvar_ready, 1)
            nc.scalar.activation(nv[1], nv[1], ACT.Sqrt).then_inc(rstd_in, 1)
            act.wait_ge(d_ready, 1)
            nc.scalar.activation(nv[13], nv[12], ACT.Exp).then_inc(dexp_ready, 1)

        @block.tensor
        def _(pe):
            pe.wait_ge(consts, 4)
            pe.wait_ge(w_in, 32)
            for k in range(KC):
                for m in range(KC):
                    last = nc.tensor.transpose(bank(7)[:, (k * KC + m) * P:(k * KC + m + 1) * P],
                                               wraw[:, m, k * P:(k + 1) * P], ident[:, :])
            last.then_inc(wt_turned, 1)
            pe.wait_ge(wt_copied, 1)
            pe.wait_ge(consts, 6)

            def layer_one(i, first):
                for t in range(2):
                    pe.wait_ge(xn_ready, 2 * i + t + 1)
                    if not first:
                        pe.wait_ge(h_copied, 2 * i + t - 1)
                    for k in range(KC):
                        last = nc.tensor.transpose(bank(4 + t)[:, k * P:(k + 1) * P], xn[:, t, k * P:(k + 1) * P], ident[:, :])
                    last.then_inc(xn_turned, 1)
                for t in range(2):
                    pe.wait_ge(xT_ready, 2 * i + t + 1)
                    for k in range(KC):
                        nc.tensor.matmul(bank(4 + t)[:, D:2 * D], xT[:, t, k, :], wt[:, k, :], start=(k == 0), stop=False)
                    nc.tensor.matmul(bank(4 + t)[:, D:2 * D], ones[0:1, :], brow[0:1, :], start=False, stop=True).then_inc(h_done, 1)

            layer_one(0, True)
            with pe.Fori(1, NBP // 2) as i:
                layer_one(i, False)

            def turn(n):
                pe.wait_ge(sort_ready, n + 1)
                frm = sortbuf[TURNS[n % NTURN]]
                for b in range(4):
                    for q in range(4):
                        at = (4 * b + q) * P
                        last = nc.tensor.transpose(ps_sort[:, at:at + P], frm[:, at:at + P], ident[:, :])
                    last.then_inc(turned, 1)

            for n in range(NTURN):
                turn(n)
            pe.wait_ge(sums_ready, NBP)
            nc.tensor.matmul(ps_tab[0:NB, 0:1], signsum[0:E1_P, 0:NB], ones[0:E1_P, 0:1], start=True, stop=True)
            nc.tensor.matmul(ps_tab[0:NB, 1:2], signsum[0:E1_P, 1:NBP], ones[0:E1_P, 0:1], start=True, stop=True).then_inc(count_done, 1)
            pe.wait_ge(steps_ready, 1)
            nc.tensor.matmul(ps_tab[0:NB, 2:3], tri[0:NB, 0:NB], small[0:NB, 3:4], start=True, stop=True).then_inc(count_done, 1)
            pe.wait_ge(steps_ready, 2)
            mask = block_over
            pe.wait_ge(h_copied, NBP)
            H = STEPS // 2
            for half in range(2):
                nc.tensor.matmul(bank(4 + half)[:, 0:H], ones[0:NB, :], mask[0:NB, half * H:(half + 1) * H], start=True, stop=True)
            for half in range(2):
                last = nc.tensor.matmul(bank(6 + half)[0:1, 0:H], small[0:NB, 5:6], mask[0:NB, half * H:(half + 1) * H], start=True, stop=True)
            last.then_inc(steps_done, 1)
            for n in range(NTURN, 2 * NTURN):
                turn(n)
            pe.wait_ge(tab_ready, 1)
            pe.wait_ge(consts, 7)
            nc.tensor.matmul(ps_hist, zero_bf[:, :], zero_bf[:, 0:64], start=True, stop=False)

            def step(i, j, first):
                pe.wait_ge(onehot_ready, i * RING + j + 1)
                pe.wait_ge(rows_in[j], 32 * i + 32)
                if not (first and j < PRING):
                    pe.wait_ge(step_added, i * RING + j + 1 - PRING)
                for t in range(WIN):
                    last = nc.tensor.matmul(ps_step[j % PRING], onehot[:, j, t, :], gathered[:, j, t, :],
                                            start=(t == 0), stop=(t == WIN - 1))
                last.then_inc(step_done, 1)

            def digits(i):
                for q in range(HQ):
                    pe.wait_ge(digit_ready, i * HQ + q + 1)
                    nc.tensor.matmul(ps_hist, oh_lo[:, q, :], oh_hi[:, q, :], start=False, stop=False).then_inc(digit_done, 1)

            for j in range(RING):
                step(0, j, True)
            digits(0)
            with pe.Fori(1, ITERS) as i:
                for j in range(RING):
                    step(i, j, False)
                digits(i)
            nc.tensor.matmul(ps_hist, zero_bf[:, :], zero_bf[:, 0:64], start=False, stop=True).then_inc(digit_done, 1)
            pe.wait_ge(hist_copied, 1)
            nc.tensor.matmul(ps_tab[:, 0:64], tri[:, :], histo[:, 0, :], start=True, stop=True)
            nc.tensor.matmul(ps_tab[:, 64:128], ones[:, :], histo[:, 0, :], start=True, stop=True).then_inc(hist_summed, 1)
            pe.wait_ge(w2_in, 16 * (7 + 3 * EXP))

            def layer_two(i, first):
                for t in range(2):
                    pe.wait_ge(xn2_ready, 2 * i + t + 1)
                    if not first:
                        pe.wait_ge(g_copied, 2 * i + t - 1)
                    for k in range(KC):
                        last = nc.tensor.transpose(bank(4 + t)[:, k * P:(k + 1) * P], xn[:, t, k * P:(k + 1) * P], ident[:, :])
                    last.then_inc(xn2_turned, 1)
                for t in range(2):
                    pe.wait_ge(xT2_ready, 2 * i + t + 1)
                    for k in range(KC):
                        last = nc.tensor.matmul(bank(4 + t)[:, D:D + FEAT], xT[:, t, k, :], wg[:, k, :], start=(k == 0), stop=(k == KC - 1))
                    last.then_inc(g_done, 1)

            layer_two(0, True)
            with pe.Fori(1, NBP // 2) as i:
                layer_two(i, False)

            def expert_chunk(i, tiles, first):
                T = tiles * P
                pe.wait_ge(xc_in, 16 * i + 16)
                for e in range(EXP):
                    for f in range(FC):
                        if not (first and e == 0 and f < 2):
                            pe.wait_ge(act_done, (i * EXP + e) * FC + f - 1)
                        for k in range(KC):
                            last = nc.tensor.matmul(bank(f % 2)[:, 0:T], w1s[:, e, k, f * P:(f + 1) * P],
                                                    xc[:, 0:tiles, k * P:(k + 1) * P], start=(k == 0), stop=(k == KC - 1))
                        last.then_inc(up_done, 1)
                    pe.wait_ge(act_done, (i * EXP + e + 1) * FC)
                    if not (first and e == 0):
                        pe.wait_ge(y_copied, i * EXP + e)
                    for n in range(tiles):
                        y = ps[:, 1024 + n * D:1024 + (n + 1) * D]
                        for f in range(FC):
                            nc.tensor.matmul(y, hidden[:, e % 2, f, n * P:(n + 1) * P], w2s[:, e, f, :], start=(f == 0), stop=False)
                        last = nc.tensor.matmul(y, ones[0:1, :], b2s[0:1, e, :], start=False, stop=True)
                    last.then_inc(down_done, 1)

            expert_chunk(0, CHT, True)
            with pe.Fori(1, NCH) as i:
                expert_chunk(i, CHT, False)
            expert_chunk(NCH, REST, False)
            for r, (nf, at) in enumerate(((HEADS, 0), (HEADS, 0), (HEADS, 1), (FEAT + HEADS, 0))):
                pe.wait_ge(tails_ready, r + 1)
                nc.tensor.transpose(bank(4)[0:nf, 0:P], carry_t[:, 0:nf], ident[:, :])
                nc.tensor.transpose(bank(4)[0:nf, P:2 * P], carry_f[:, 0:nf], ident[:, :]).then_inc(tails_turned, 1)
                pe.wait_ge(carry_ready, r + 1)
                nc.tensor.transpose(bank(5)[:, 0:nf], carry_r[0:nf, 1, at:at + P], ident[0:nf, 0:nf]).then_inc(carry_turned, 1)

        @block.vector
        def _(dve):
            V = nc.vector
            n = [0]

            def done(ins):
                n[0] += 1
                ins.then_inc(vec, 1)
                dve.wait_ge(vec, n[0])

            def sort_step(which, turn_no):
                kind, cur, *what = which
                frm, to = sortbuf[cur], sortbuf[1 - cur]
                if kind == "flip":
                    a, b = what
                    if b is None:
                        done(V.tensor_scalar(to, frm, sign[:, a:a + 1], None, ALU.mult))
                    else:
                        done(V.tensor_scalar(to, frm, sign[:, a:a + 1], sign[:, b:b + 1], ALU.mult, ALU.mult))
                elif kind == "pair":
                    d, mirror = what
                    f4 = frm.rearrange("p (b s d) -> p b s d", s=2, d=d)
                    t4 = to.rearrange("p (b s d) -> p b s d", s=2, d=d)
                    lo, hi, tlo, thi = f4[:, :, 0, :], f4[:, :, 1, :], t4[:, :, 0, :], t4[:, :, 1, :]
                    if mirror:
                        hi, thi = hi[:, :, ::-1], thi[:, :, ::-1]
                    V.tensor_tensor(tlo, lo, hi, ALU.min)
                    done(V.tensor_tensor(thi, lo, hi, ALU.max))
                else:
                    dve.sem_inc(sort_ready, 1)
                    for b in (2, 3):
                        dve.wait_ge(turned, 4 * turn_no + b + 1)
                        last = V.tensor_copy(to[:, b * 512:(b + 1) * 512], bank(b))
                    done(last)
                    dve.wait_ge(turn_copied, 2 * turn_no + 2)

            def layer_stats(call):
                with dve.Fori(0, NBP) as i:
                    V.bn_stats(stats[:, bass.ds(i, 1), :].rearrange("p o s -> p (o s)"), nodes[:, bass.ds(i * D, D)]).then_inc(stats_in, 1)
                dve.wait_ge(stats_in, call * NBP)
                for b in range(NBP):
                    last = V.bn_aggr(mv[:, b, :], stats[:, b, :])
                done(last)
                done(V.tensor_scalar_add(mv[:, :, 1], mv[:, :, 1], EPS))
                dve.sem_inc(var_ready, 1)

            dve.wait_ge(raw_in, 32)
            dve.wait_ge(consts, 14)
            for k in range(7):
                V.tensor_scalar(bits[:, k:k + 1], iota_i[:, k:k + 1], k, 1, ALU.logical_shift_right, ALU.bitwise_and)
            done(V.memset(bits[:, 7:8], 0))
            V.tensor_scalar(sign[:, :], bits[:, :], -2.0, 1.0, ALU.mult, ALU.add)
            V.tensor_scalar_add(thr[:, :], thr[:, :], 0.5).then_inc(consts, 1)
            s0, s1 = sortbuf[0].bitcast(I32), sortbuf[1].bitcast(I32)
            V.memset(s0, KEY_BIAS | 0x63FFE000)
            done(V.scalar_tensor_tensor(out=raw_a[0:E1_P, 0:E1_W], in0=rows_raw, scalar=13, in1=raw_b[0:E1_P, 0:E1_W],
                                        op0=ALU.logical_shift_left, op1=ALU.bitwise_or))
            done(V.tensor_scalar(s0[0:E1_P, 0:E1_W], raw_a[0:E1_P, 0:E1_W], KEY_BIAS, None, ALU.bitwise_or))
            turn_no = 0
            for at, which in enumerate(SORT_STEPS):
                if at == 22:
                    dve.wait_ge(x_in, 32)
                    layer_stats(1)
                    dve.wait_ge(std_ready, 1)
                    done(V.reciprocal(rstd[:, :], std[:, :]))
                    V.scalar_tensor_tensor(out=nmr[:, :], in0=mv[:, :, 0], scalar=-1.0, in1=rstd[:, :],
                                           op0=ALU.mult, op1=ALU.mult).then_inc(norm1_ready, 1)
                sort_step(which, turn_no)
                turn_no += which[0] == "turn"
            srt = sortbuf[SORTED_IN].bitcast(I32)
            oth = sortbuf[1 - SORTED_IN].bitcast(I32)
            done(V.tensor_scalar(oth, srt, 13, FIELD, ALU.logical_shift_right, ALU.bitwise_and))
            V.tensor_copy(pairs[:, :, 0], oth)
            done(V.tensor_scalar(srt, srt, FIELD, None, ALU.bitwise_and))
            V.tensor_scalar_min(pairs_i[:, :, 1], srt, N - 1).then_inc(pairs_ready, 1)

            dve.wait_ge(count_done, 1)
            done(V.tensor_scalar(small[0:NB, 0:2], ps_tab[0:NB, 0:2], -0.5, 0.5 * E1, ALU.mult, ALU.add))
            done(V.tensor_tensor(small[0:NB, 2:3], small[0:NB, 1:2], small[0:NB, 0:1], ALU.subtract))
            done(V.tensor_scalar_add(small_i[0:NB, 0:1], small[0:NB, 2:3], float(G - 1)))
            done(V.tensor_scalar(small_i[0:NB, 1:2], small_i[0:NB, 0:1], G.bit_length() - 1, None, ALU.logical_shift_right))
            done(V.tensor_copy(small[0:NB, 3:4], small_i[0:NB, 1:2]))
            dve.sem_inc(steps_ready, 1)
            done(V.scalar_tensor_tensor(out=small[0:NB, 5:6], in0=small[0:NB, 3:4], scalar=-float(G), in1=small[0:NB, 2:3],
                                        op0=ALU.mult, op1=ALU.add))
            dve.wait_ge(count_done, 2)
            done(V.tensor_copy(small[0:NB, 4:5], ps_tab[0:NB, 2:3]))
            done(V.tensor_scalar(block_over[0:NB, :], step_iota[0:NB, :], small[0:NB, 4:5], None, ALU.is_ge))
            dve.sem_inc(steps_ready, 1)
            dve.wait_ge(steps_done, 1)
            H = STEPS // 2
            for half in range(2):
                c = slice(half * H, (half + 1) * H)
                V.tensor_scalar(block_base[:, c], bank(4 + half)[:, 0:H], float(P), None, ALU.mult)
                V.tensor_scalar(step_tab[0:1, 1, c], bank(4 + half)[0:1, 0:H], float(D), None, ALU.mult)
                last = V.scalar_tensor_tensor(out=step_tab[0:1, 0, c], in0=step_iota[0:1, c], scalar=float(G),
                                              in1=bank(6 + half)[0:1, 0:H], op0=ALU.mult, op1=ALU.add)
            done(last)
            dve.wait_ge(raw2_in, 32)
            V.memset(s0, KEY_BIAS | 0x63FFDFFF)
            V.tensor_scalar(dig_hi[:, 0:E2_W].bitcast(I32), raw_b[:, 0:E2_W], 7, None, ALU.logical_shift_right)
            V.tensor_scalar(dig_lo[:, 0:E2_W].bitcast(I32), raw_b[:, 0:E2_W], P - 1, None, ALU.bitwise_and)
            V.memset(dig_hi[:, E2_W:HCOLS], -1.0)
            done(V.memset(dig_lo[:, E2_W:HCOLS], -1.0))
            V.tensor_copy(dig_hi[:, 0:E2_W], dig_hi[:, 0:E2_W].bitcast(I32))
            V.tensor_copy(dig_lo[:, 0:E2_W], dig_lo[:, 0:E2_W].bitcast(I32))
            done(V.scalar_tensor_tensor(out=raw_a[:, 0:E2_W], in0=raw_b[:, 0:E2_W], scalar=14, in1=raw_a[:, 0:E2_W],
                                        op0=ALU.logical_shift_left, op1=ALU.bitwise_or))
            V.tensor_scalar(s0[:, 0:E2_W], raw_a[:, 0:E2_W], KEY_BIAS | 0x2000, None, ALU.bitwise_or)
            done(V.scalar_tensor_tensor(out=raw_b[:, 0:MARKS], in0=mark_iota[:, :], scalar=14, in1=mark_iota[:, :],
                                        op0=ALU.logical_shift_left, op1=ALU.bitwise_or))
            done(V.tensor_scalar(s0[:, E2_W:E2_W + MARKS], raw_b[:, 0:MARKS], KEY_BIAS, None, ALU.bitwise_or))
            for which in SORT_STEPS:
                sort_step(which, turn_no)
                turn_no += which[0] == "turn"
            dve.sem_inc(keys2_ready, 1)
            dve.wait_ge(keys2_in, 16)
            done(V.tensor_scalar(edge_idx[:, :], key2[:, 0:TG], FIELD, None, ALU.bitwise_and))
            V.tensor_scalar_min(edge_idx[:, :], edge_idx[:, :], N - 1)
            done(V.tensor_scalar(key2[:, :], key2[:, :], 13, 1, ALU.logical_shift_right, ALU.bitwise_and))
            V.tensor_copy(inside[:, :], key2[:, :])
            done(V.tensor_scalar(starts[:, :], key2[:, :], -1.0, 1.0, ALU.mult, ALU.add))
            dve.sem_inc(tab_ready, 1)

            def spread(i, j, first):
                dve.wait_ge(idx_in[j], 16 * i + 16)
                if not first:
                    dve.wait_ge(step_done, i * RING + j + 1 - RING)
                for t in range(WIN):
                    last = V.tensor_scalar(onehot[:, j, t, :], iota_c[:, :], block_base[:, bass.ds(i * RING + j, 1)],
                                           idx_slot[:, j, t, 0:1], ALU.add, ALU.is_equal)
                last.then_inc(onehot_ready, 1)

            def add_step(k, j, first):
                dve.wait_ge(step_done, k + 1)
                if not first:
                    dve.wait_ge(step_added, k)
                col = dve.value_load(step_tab[0:1, 1, bass.ds(k, 1)], min_val=0, max_val=NB * D)
                V.tensor_tensor(nodes[:, bass.ds(col, D)], nodes[:, bass.ds(col, D)], ps_step[j % PRING], ALU.add).then_inc(step_added, 1)

            def digits(i, first):
                for q in range(HQ):
                    if not first:
                        dve.wait_ge(digit_done, (i - 1) * HQ + q + 1)
                    V.tensor_scalar(oh_hi[:, q, :], iota_bf[:, 0:64], dig_hi[:, bass.ds(i * HQ + q, 1)], None, ALU.is_equal)
                    V.tensor_scalar(oh_lo[:, q, :], iota_bf[:, :], dig_lo[:, bass.ds(i * HQ + q, 1)], None, ALU.is_equal).then_inc(digit_ready, 1)

            for j in range(RING):
                spread(0, j, True)
                if j >= PRING:
                    add_step(j - PRING, j, j == PRING)
            digits(0, True)
            with dve.Fori(1, ITERS) as i:
                for j in range(RING):
                    spread(i, j, False)
                    add_step(i * RING + j - PRING, j, False)
                digits(i, False)
            for k in range(STEPS - PRING, STEPS):
                add_step(k, k % PRING, False)
            dve.wait_ge(step_added, STEPS)
            dve.sem_inc(x1_ready, 1)
            layer_stats(2)
            dve.wait_ge(digit_done, HCOLS + 1)
            V.tensor_copy(histo[:, 0, :], ps_hist).then_inc(hist_copied, 1)
            dve.wait_ge(hist_summed, 1)
            V.tensor_copy(histo[:, 1, :], ps_tab[:, 0:64])
            done(V.tensor_copy(histo[:, 2, :], ps_tab[:, 64:128]))
            done(V.tensor_tensor(histo[:, 1, :], histo[:, 1, :], histo[:, 2, :], ALU.subtract))
            done(V.tensor_tensor_scan(histo[:, 0, :], ones[:, 0:64], histo[:, 2, :], 0.0, ALU.mult, ALU.add))
            done(V.tensor_tensor(histo[:, 1, :], histo[:, 1, :], histo[:, 0, :], ALU.add))
            V.tensor_tensor(end_idx[:, :], histo[:, 1, :], node_iota[:, :], ALU.add)
            dve.wait_ge(std_ready, 2)
            done(V.reciprocal(rstd[:, :], std[:, :]))

            def layer_two(i, first):
                for t in range(2):
                    if not first:
                        dve.wait_ge(xn2_turned, 2 * i + t - 1)
                    V.tensor_scalar(xn[:, t, :], nodes[:, bass.ds((2 * i + t) * D, D)],
                                    mv[:, bass.ds(2 * i + t, 1), 0:1].rearrange("p a b -> p (a b)"),
                                    rstd[:, bass.ds(2 * i + t, 1)], ALU.subtract, ALU.mult).then_inc(xn2_ready, 1)
                for t in range(2):
                    dve.wait_ge(g_done, 2 * i + t + 1)
                    V.tensor_copy(table[:, bass.ds(2 * i + t, 1), 0:FEAT].rearrange("p o f -> p (o f)"),
                                  bank(4 + t)[:, D:D + FEAT]).then_inc(g_copied, 1)

            layer_two(0, True)
            with dve.Fori(1, NBP // 2) as i:
                layer_two(i, False)
            dve.wait_ge(g_copied, NBP)
            wide = xn[:, :, :].rearrange("p a b -> p (a b)")
            for q in range(2):
                for half in range(2):
                    nn = NBP // 2
                    rows = slice(half * nn, (half + 1) * nn)
                    prod = wide[:, 0:nn * FEAT].rearrange("p (n h e) -> p n h e", h=HEADS, e=EXP)
                    done(V.tensor_tensor(prod.rearrange("p n h e -> p n (h e)"), table[:, rows, 0:FEAT],
                                         att[:, q, :].unsqueeze(1).to_broadcast([P, nn, FEAT]), ALU.mult))
                    done(V.tensor_reduce(table[:, rows, FEAT + q * HEADS:FEAT + (q + 1) * HEADS], prod, axis=AX.X, op=ALU.add))
            dve.sem_inc(table_ready, 1)

            dve.wait_ge(x1_stored, 16)
            per = GG * GQ

            def fill(i, g, first):
                if not first:
                    dve.wait_ge(gat_in[g], 16 * GQ * i)
                    V.tensor_copy(edges[:, bass.ds((i - 1) * per + g * GQ, GQ), :], gat_ring[:, g, :, :])
                V.tensor_copy(gat_slot[:, g, :], edge_idx[:, bass.ds(i * per + g * GQ, GQ)]).then_inc(slot_ready, 1)

            for g in range(GG):
                fill(0, g, True)
            with dve.Fori(1, GITERS) as i:
                for g in range(GG):
                    fill(i, g, False)
            for g in range(GG):
                dve.wait_ge(gat_in[g], 16 * GQ * GITERS)
                last = V.tensor_copy(edges[:, TG - per + g * GQ:TG - per + (g + 1) * GQ, :], gat_ring[:, g, :, :])
            done(last)

            f_dst = lambda h: edges[:, :, FEAT + HEADS + h]
            first = starts[:, 0:TG]
            ends = starts[:, 1:TG + 1]
            in_row = inside[:, 0:TG]
            not_end = inside[:, 1:TG + 1]
            a_src = edges[:, :, FEAT:FEAT + HEADS]
            a_dst = edges[:, :, FEAT + HEADS:ROW]
            top = top4[:, :, :].rearrange("p h t -> p t h")
            over_heads = lambda a: a.unsqueeze(2).to_broadcast([P, TG, HEADS])

            V.tensor_reduce(small[:, 0:1], first, axis=AX.X, op=ALU.max)
            done(V.tensor_reduce(small[:, 1:2], ends, axis=AX.X, op=ALU.max))
            V.tensor_scalar(small[:, 4:5], small[:, 0:1], NEG, None, ALU.mult)
            done(V.tensor_scalar(small[:, 2:4], small[:, 0:2], -1.0, 1.0, ALU.mult, ALU.add))

            def carry(r, nf, flag, init, op0, op1, backward):
                done(V.tensor_copy(carry_f[:, 0:nf], flag.to_broadcast([P, nf])))
                dve.sem_inc(tails_ready, 1)
                done(V.memset(carry_r[0:nf, 1, :], init))
                dve.wait_ge(tails_turned, r + 1)
                done(V.tensor_copy(carry_r[0:nf, 0, :], bank(4)[0:nf, 0:2 * P]))
                tails, flags = carry_r[0:nf, 0, 0:P], carry_r[0:nf, 0, P:2 * P]
                state = carry_r[0:nf, 1, 0:P] if backward else carry_r[0:nf, 1, 1:P + 1]
                if backward:
                    tails, flags, state = tails[:, ::-1], flags[:, ::-1], state[:, ::-1]
                done(V.tensor_tensor_scan(state, flags, tails, init, op0, op1))
                dve.sem_inc(carry_ready, 1)
                dve.wait_ge(carry_turned, r + 1)
                done(V.tensor_copy(carry_in[:, 0:nf], bank(5)[:, 0:nf]))

            dve.wait_ge(down_done, EXP * (NCH + 1))
            done(V.tensor_tensor(a_dst, a_dst, over_heads(first), ALU.mult))
            for h in range(HEADS):
                last = V.tensor_tensor_scan(top4[:, h, :], in_row, f_dst(h), 0.0, ALU.mult, ALU.add)
            done(last)
            done(V.tensor_copy(carry_t[:, 0:HEADS], top4[:, :, TG - 1]))
            carry(0, HEADS, small[:, 2:3], 0.0, ALU.mult, ALU.add, False)
            for h in range(HEADS):
                V.tensor_tensor_scan(f_dst(h), in_row, f_dst(h), carry_in[:, h:h + 1], ALU.mult, ALU.add)
            done(V.tensor_scalar(scratch[:, :], first, NEG, None, ALU.mult))
            for h in range(HEADS):
                last = V.tensor_tensor_scan(top4[:, h, :], scratch[:, :], edges[:, :, FEAT + h], NEG, ALU.add, ALU.max)
            done(last)
            done(V.tensor_copy(carry_t[:, 0:HEADS], top4[:, :, TG - 1]))
            carry(1, HEADS, small[:, 4:5], NEG, ALU.add, ALU.max, False)
            for h in range(HEADS):
                last = V.tensor_tensor_scan(top4[:, h, :], scratch[:, :], edges[:, :, FEAT + h], carry_in[:, h:h + 1], ALU.add, ALU.max)
            done(last)
            done(V.tensor_tensor(top4[:, :, :], top4[:, :, :], ends.unsqueeze(1).to_broadcast([P, HEADS, TG]), ALU.mult))
            for h in range(HEADS):
                done(V.tensor_tensor_scan(scratch[:, ::-1], not_end[:, ::-1], top4[:, h, ::-1], 0.0, ALU.mult, ALU.add))
                done(V.tensor_copy(carry_t[:, h:h + 1], scratch[:, 0:1]))
            carry(2, HEADS, small[:, 3:4], 0.0, ALU.mult, ALU.add, True)
            for h in range(HEADS):
                last = V.tensor_tensor_scan(top4[:, h, ::-1], not_end[:, ::-1], top4[:, h, ::-1], carry_in[:, h:h + 1], ALU.mult, ALU.add)
            done(last)
            V.tensor_tensor(a_src, a_src, a_dst, ALU.add)
            done(V.tensor_tensor(top, top, a_dst, ALU.add))
            V.scalar_tensor_tensor(out=a_src, in0=a_src, scalar=0.2, in1=a_src, op0=ALU.mult, op1=ALU.max)
            done(V.scalar_tensor_tensor(out=top, in0=top, scalar=0.2, in1=top, op0=ALU.mult, op1=ALU.max))
            V.tensor_tensor(a_src, a_src, top, ALU.subtract).then_inc(logit_ready, 1)
            dve.wait_ge(exp_ready, 1)
            for h in range(HEADS):
                last = V.tensor_tensor(edges[:, :, h * EXP:(h + 1) * EXP], edges[:, :, h * EXP:(h + 1) * EXP],
                                       edges[:, :, FEAT + h].unsqueeze(2).to_broadcast([P, TG, EXP]), ALU.mult)
            done(last)
            NS = FEAT + HEADS
            for f in range(NS):
                done(V.tensor_tensor_scan(scratch[:, :], in_row, edges[:, :, f], 0.0, ALU.mult, ALU.add))
                done(V.tensor_copy(carry_t[:, f:f + 1], scratch[:, TG - 1:TG]))
            carry(3, NS, small[:, 2:3], 0.0, ALU.mult, ALU.add, False)
            for f in range(NS):
                last = V.tensor_tensor_scan(edges[:, :, f], in_row, edges[:, :, f], carry_in[:, f:f + 1], ALU.mult, ALU.add)
            done(last)
            dve.sem_inc(edge_sums_ready, 1)

            dve.wait_ge(node_sums_in, 16 * NB)
            dve.wait_ge(w2_in, 16 * (7 + 3 * EXP))
            n4 = lambda a: a.rearrange("p (n h e) -> p n h e", h=HEADS, e=EXP)
            n3 = lambda a: a.rearrange("p (n f) -> p n f", f=FEAT)
            over_n = lambda a: a.unsqueeze(1).to_broadcast([P, NB, FEAT])
            over_f = lambda a: a.unsqueeze(2).to_broadcast([P, NB, FEAT])
            done(V.tensor_scalar_add(den, nsum[:, :, FEAT:NS], 1e-16))
            done(V.reciprocal(den, den))
            for h in range(HEADS):
                last = V.tensor_tensor(n4(nw[0])[:, :, h, :], nsum[:, :, h * EXP:(h + 1) * EXP],
                                       den[:, :, h].unsqueeze(2).to_broadcast([P, NB, EXP]), ALU.mult)
            done(last)
            done(V.tensor_tensor(n3(nw[0]), n3(nw[0]), over_n(gpar[:, 0, :]), ALU.add))
            done(V.tensor_reduce(nv[0], n3(nw[0]), axis=AX.X, op=ALU.add))
            done(V.tensor_scalar(nv[0], nv[0], 1.0 / FEAT, None, ALU.mult))
            done(V.tensor_tensor(n3(nw[1]), n3(nw[0]), over_f(nv[0]), ALU.subtract))
            done(V.tensor_tensor(nw[2], nw[1], nw[1], ALU.mult))
            done(V.tensor_reduce(nv[1], n3(nw[2]), axis=AX.X, op=ALU.add))
            V.tensor_scalar(nv[1], nv[1], 1.0 / FEAT, EPS, ALU.mult, ALU.add).then_inc(rvar_ready, 1)
            dve.wait_ge(rstd_in, 1)
            done(V.reciprocal(nv[2], nv[1]))
            done(V.tensor_tensor(n3(nw[1]), n3(nw[1]), over_f(nv[2]), ALU.mult))
            done(V.tensor_tensor(n3(nw[1]), n3(nw[1]), over_n(gpar[:, 1, :]), ALU.mult))
            done(V.tensor_tensor(n3(nw[1]), n3(nw[1]), over_n(gpar[:, 2, :]), ALU.add))
            for e in range(EXP):
                last = V.tensor_reduce(score[e], n4(nw[1])[:, :, :, e], axis=AX.X, op=ALU.add)
            done(last)
            for e in range(EXP):
                V.tensor_scalar(score[e], score[e], 1.0 / HEADS, None, ALU.mult)
                last = V.memset(rank[e], float(EXP - 1 - e))
            done(last)
            for a in range(EXP):
                for b in range(a + 1, EXP):
                    done(V.tensor_tensor(nv[0], score[a], score[b], ALU.is_ge))
                    V.tensor_tensor(rank[b], rank[b], nv[0], ALU.add)
                    done(V.tensor_tensor(rank[a], rank[a], nv[0], ALU.subtract))
            V.tensor_tensor(nv[0], score[0], score[1], ALU.max)
            done(V.tensor_tensor(nv[1], score[2], score[3], ALU.max))
            done(V.tensor_tensor(nv[0], nv[0], nv[1], ALU.max))
            done(V.scalar_tensor_tensor(out=nv[12], in0=rank[0], scalar=1.0, in1=score[0], op0=ALU.is_equal, op1=ALU.mult))
            for e in range(1, EXP):
                done(V.scalar_tensor_tensor(out=nv[1], in0=rank[e], scalar=1.0, in1=score[e], op0=ALU.is_equal, op1=ALU.mult))
                done(V.tensor_tensor(nv[12], nv[12], nv[1], ALU.add))
            V.tensor_tensor(nv[12], nv[12], nv[0], ALU.subtract).then_inc(d_ready, 1)
            dve.wait_ge(dexp_ready, 1)
            done(V.tensor_scalar_add(nv[0], nv[13], 1.0))
            done(V.reciprocal(nv[0], nv[0]))
            done(V.tensor_tensor(nv[1], nv[13], nv[0], ALU.mult))
            for e in range(EXP):
                done(V.scalar_tensor_tensor(out=nv[2], in0=rank[e], scalar=0.0, in1=nv[0], op0=ALU.is_equal, op1=ALU.mult))
                done(V.scalar_tensor_tensor(out=gate[:, e, :], in0=rank[e], scalar=1.0, in1=nv[1], op0=ALU.is_equal, op1=ALU.mult))
                done(V.tensor_tensor(gate[:, e, :], gate[:, e, :], nv[2], ALU.add))

            def combine(k, j, n_in, first):
                rows = P if j is not None else TAIL
                j = j or 0
                dve.wait_ge(fin_in[j], 32 * n_in)
                if not first:
                    dve.wait_ge(fin_out[j], 16 * (n_in - 1))
                for e in range(EXP):
                    if e:
                        dve.wait_ge(fin_step, k * EXP + e)
                    add = finy[0:rows, j, EXP, :] if e == 0 else fino[0:rows, j, :]
                    last = V.scalar_tensor_tensor(out=fino[0:rows, j, :], in0=finy[0:rows, j, e, :],
                                                  scalar=gate[0:rows, e, bass.ds(k, 1)], in1=add, op0=ALU.mult, op1=ALU.add)
                    last.then_inc(fin_step, 1)
                dve.wait_ge(fin_step, k * EXP + EXP)
                dve.sem_inc(fin_ready, 1)

            LOOP = (NB - 1) // FR
            for j in range(FR):
                combine(j, j, 1, True)
            with dve.Fori(1, LOOP) as i:
                for j in range(FR):
                    combine(i * FR + j, j, i + 1, False)
            combine(NB - 1, None, LOOP + 1, False)


_INS = ["x", "src", "dst", "L0_gnn_W", "L0_gnn_b", "L0_ffn_W_gat", "L0_ffn_att_src", "L0_ffn_att_dst", "L0_ffn_b_gat",
        "L0_ffn_ln_gamma", "L0_ffn_ln_beta", "L0_ffn_W1", "L0_ffn_b1", "L0_ffn_W2", "L0_ffn_b2", "L0_ffn_edge_index"]


def kernel(**inputs):
    import numpy as _np
    import concourse.bacc as _bacc
    from concourse import mybir as _mybir
    from concourse.bass_utils import run_bass_kernel_spmd as _run

    nc = _bacc.Bacc("TRN2", target_bir_lowering=False, num_devices=1)
    arrays, args = {}, []
    for name in _INS:
        a = _np.ascontiguousarray(inputs[name])
        arrays[f"in_{name}"] = a
        args.append(nc.dram_tensor(f"in_{name}", a.shape, _mybir.dt.from_np(a.dtype), kind="ExternalInput").ap())
    shape = inputs["x"].shape
    out = nc.dram_tensor("out_0", shape, _mybir.dt.float32, kind="ExternalOutput").ap()
    gnn_ffn_kernel(nc, *args, out)
    r = _run(nc, [arrays], core_ids=[0])
    return r.results[0]["out_0"]
```

```python
import concourse.bass as bass
from concourse import mybir
from concourse.alu_op_type import AluOpType as ALU
from contextlib import ExitStack

F32 = mybir.dt.float32
BF16 = mybir.dt.bfloat16
I32 = mybir.dt.int32
ACT = mybir.ActivationFunctionType
AX = mybir.AxisListType

P = 128
KEY_BIAS = 0x10000000
FIELD = 0x1FFF
CHUNK_W, CHUNK_ROW_BITS = 1024, 10
ROUTE_W, ROUTE_ROW_BITS = 2048, 11
PART_BITS = 7
EPS = 1e-5
NEG = -3.0e38


def sort_plan(row_bits):
    steps, cur = [], 0

    def add(kind, *what):
        nonlocal cur
        steps.append((kind, cur, *what))
        cur ^= 1

    add("flip", 0, None)
    for k in range(1, row_bits + 1):
        for j in range(k - 1, -1, -1):
            add("pair", 1 << j, j == k - 1)
    for k in range(row_bits + 1, row_bits + PART_BITS + 1):
        add("flip", k - row_bits - 1, k - row_bits if k < row_bits + PART_BITS else None)
        add("turn")
        for j in range(k - row_bits - 1, -1, -1):
            add("pair", 1 << j, False)
        add("turn")
        for j in range(row_bits - 1, -1, -1):
            add("pair", 1 << j, False)
    return steps, cur


CHUNK_STEPS, CHUNK_IN = sort_plan(CHUNK_ROW_BITS)
ROUTE_STEPS, ROUTE_IN = sort_plan(ROUTE_ROW_BITS)
TURN_OF = {name: [s[1] for s in steps if s[0] == "turn"] for name, steps in (("chunk", CHUNK_STEPS), ("route", ROUTE_STEPS))}


def gnn_ffn_kernel(nc, x, src, dst, gnn_W, gnn_b, W_gat, att_src, att_dst, b_gat, ln_gamma, ln_beta,
                   W1, b1, W2, b2, edge_index, out):
    N, D = x.shape
    E1 = src.shape[0]
    E2 = edge_index.shape[1]
    EXP, _, HID = W1.shape
    HEADS = att_src.shape[0]
    FEAT = HEADS * EXP
    ROW = FEAT + 2 * HEADS
    KC = D // P
    FC = HID // P
    NB = -(-N // P)
    NBP = NB + 1
    TAIL = N - (NB - 1) * P
    CHUNKS = 2
    E1_P, E1_W = 125, E1 // 125
    C_W = E1_W // CHUNKS
    C_E = E1_P * C_W
    WIN = 2
    G = WIN * P
    RING = 8
    PRING = 4
    C_STEPS = -(-((C_E + NB * (G - 1)) // G) // RING) * RING
    C_ITERS = C_STEPS // RING
    STEPS = CHUNKS * C_STEPS
    ITERS = CHUNKS * C_ITERS
    E2_W = E2 // P
    HQ = -(-E2_W // ITERS)
    HCOLS = HQ * ITERS
    MARKS = NB
    GG, GQ = 3, 4
    TG = -(-(E2 + P * MARKS) // (P * GG * GQ)) * GG * GQ
    GITERS = TG // (GG * GQ)
    CHT = 4
    CH = CHT * P
    NCH = NB // CHT
    REST = NB - NCH * CHT

    ctx = ExitStack()
    with ctx:
        dram = lambda n, s, d=F32: nc.dram_tensor(n, s, d, kind="Internal").ap()
        pairs_d = dram("pairs_d", (CHUNKS * P * CHUNK_W, 2))
        keys2_d = dram("keys2_d", (P * ROUTE_W,), I32)
        h_d = dram("h_d", (NBP * P, D))
        x1_d = dram("x1_d", (NBP * P, D))
        xT_d = dram("xT_d", (P, NBP, KC * P))
        tab_d = dram("tab_d", (NBP * P, ROW))
        y_d = dram("y_d", (NB * P, EXP, D))
        sums_d = dram("sums_d", (P * TG, ROW))

        def sb(name, shape, dt=F32):
            return ctx.enter_context(nc.sbuf_tensor(name, shape, dt))

        def sem(name):
            return ctx.enter_context(nc.semaphore(name))

        big = sb("big", [P, TG * ROW])
        nodes = big[:, 0:NBP * D]
        o = NBP * D
        chunkbuf = [big[:, o:o + CHUNK_W], big[:, o + CHUNK_W:o + 2 * CHUNK_W]]
        routebuf = [big[:, o:o + ROUTE_W], big[:, o + ROUTE_W:o + 2 * ROUTE_W]]
        block_over = big[:, o:o + C_STEPS]
        r_src = big[:, o + ROUTE_W:o + ROUTE_W + E2_W].bitcast(I32)
        r_dst = big[:, o + ROUTE_W + E2_W:o + ROUTE_W + 2 * E2_W].bitcast(I32)
        o += 2 * ROUTE_W
        pairs = big[:, o:o + 2 * CHUNK_W].rearrange("p (t w) -> p t w", w=2)
        pairs_i = big[:, o:o + 2 * CHUNK_W].bitcast(I32).rearrange("p (t w) -> p t w", w=2)
        key2 = big[:, o:o + TG + 1].bitcast(I32)
        mark_tmp = big[:, o + TG + 1:o + TG + 1 + MARKS].bitcast(I32)
        o += 2 * CHUNK_W
        rows_raw = big[0:E1_P, o:o + E1_W].bitcast(I32)
        cols_raw = big[0:E1_P, o + E1_W:o + 2 * E1_W].bitcast(I32)
        o += 2 * E1_W
        dig_hi, dig_lo = big[:, o:o + HCOLS], big[:, o + HCOLS:o + 2 * HCOLS]
        o += 2 * HCOLS
        block_base = big[:, o:o + STEPS]
        o += STEPS
        assert o <= TG * ROW
        edges = big[:, :].rearrange("p (t f) -> p t f", f=ROW)

        gathered = sb("gathered", [P, RING, WIN, D])
        hidden = gathered[:, :, :, :].rearrange("p r t c -> p (r t c)").rearrange("p (s f c) -> p s f c", s=2, f=FC)
        mid = sb("mid", [P, RING * WIN * P])
        onehot = mid[:, :].rearrange("p (r t c) -> p r t c", r=RING, t=WIN)
        junk = sb("junk", [P, C_W], BF16)
        yst = mid[:, :].rearrange("p (s n c) -> p s n c", s=2, n=CHT)
        flat = gathered[:, :, :, :].rearrange("p r t c -> p (r t c)")
        step_iota = sb("step_iota", [P, C_STEPS])
        xn = flat[:, 0:4 * D].rearrange("p (u c) -> p u c", u=2)
        xT = flat[:, 4 * D:8 * D].rearrange("p (u c) -> p u c", u=2)
        wraw = flat[:, 12 * D:14 * D].rearrange("p (k c) -> p k c", k=KC)
        wt = flat[:, 14 * D:16 * D].rearrange("p (k c) -> p k c", k=KC)
        hst = flat[:, 8 * D:12 * D].rearrange("p (u c) -> p u c", u=2)
        mark_iota = sb("mark_iota", [P, MARKS], I32)
        node_iota = sb("node_iota", [P, 64])
        idx_slot = sb("idx_slot", [P, RING, WIN, 2])
        ident = sb("ident", [P, P])
        iota_c = sb("iota_c", [P, P])
        tri = sb("tri", [P, P])
        ones = sb("ones", [P, P])
        iota_i = sb("iota_i", [P, 8], I32)
        bits = sb("bits", [P, 8], I32)
        sign = sb("sign", [P, 8])
        thr = sb("thr", [P, NBP])
        signsum = sb("signsum", [P, CHUNKS, NBP])
        zero_bf = sb("zero_bf", [P, P], BF16)
        oh_hi = sb("oh_hi", [P, HQ, 64], BF16)
        oh_lo = sb("oh_lo", [P, HQ, P], BF16)
        late = sb("late", [P, CHT * KC * P + NBP * ROW])
        step_tab = late[0:1, 0:2 * STEPS].bitcast(I32).rearrange("p (a k) -> p a k", a=2)
        small_row = late[0:1, 2 * STEPS:2 * STEPS + C_STEPS]
        xc = late[:, 0:CHT * KC * P].rearrange("p (n c) -> p n c", n=CHT)
        table = late[:, CHT * KC * P:].rearrange("p (n f) -> p n f", f=ROW)
        small = sb("small", [P, 16])
        small_i = sb("small_i", [P, 2], I32)
        end_idx = sb("end_idx", [P, 64], I32)
        histo = sb("histo", [P, 3, 65])
        digit_axis = sb("digit_axis", [P, P])
        last_row = sb("last_row", [P, P])
        edge_idx = sb("edge_idx", [P, TG], I32)
        starts = sb("starts", [P, TG + 1])
        inside = sb("inside", [P, TG + 1])
        gat_ring = sb("gat_ring", [P, GG, GQ, ROW])
        gat_slot = sb("gat_slot", [P, GG, GQ], I32)
        stats = sb("stats", [P, NBP, 6])
        mv = sb("mv", [P, NBP, 2])
        std = sb("std", [P, NBP])
        rstd = sb("rstd", [P, NBP])
        nmr = sb("nmr", [P, NBP])
        brow = sb("brow", [1, D])
        wg = sb("wg", [P, KC, FEAT])
        att = sb("att", [P, 2, FEAT])
        gpar = sb("gpar", [P, 3, FEAT])
        weights = sb("weights", [P, EXP * (KC * HID + FC * D)])
        w1s = weights[:, 0:EXP * KC * HID].rearrange("p (e k f) -> p e k f", e=EXP, k=KC)
        w2s = weights[:, EXP * KC * HID:].rearrange("p (e k f) -> p e k f", e=EXP, k=FC)
        top4 = weights[:, 0:HEADS * TG].rearrange("p (h t) -> p h t", h=HEADS)
        scratch = weights[:, HEADS * TG:(HEADS + 1) * TG]
        b1s = sb("b1s", [P, EXP, FC])
        b2s = sb("b2s", [1, EXP, D])
        carry_t = sb("carry_t", [P, HEADS])
        carry_f = sb("carry_f", [P, HEADS])
        carry_in = sb("carry_in", [P, HEADS])
        carry_r = weights[0:HEADS, (HEADS + 1) * TG:(HEADS + 1) * TG + 4 * P].rearrange("p (a c) -> p a c", a=2)
        gate = sb("gate", [P, EXP, NB])
        NS = FEAT + HEADS
        SPILL_HALVES = ((0, NB // 2 + 1), (NB // 2 + 1, NB))
        spill_lo = mid[:, 0:P]
        spill_hi = mid[:, P:P + NB * NS]
        last_node = sb("last_node", [P, 2])
        last_i = sb("last_i", [P, 2], I32)

        ps = ctx.enter_context(nc.psum_tensor("ps", [P, 8 * 512], F32))
        bank = lambda b: ps[:, b * 512:(b + 1) * 512]
        ps_step = [bank(2 + j)[:, 0:D] for j in range(PRING)]
        ps_hist = bank(6)[:, 0:64]
        ps_tab = bank(7)

        S = {}

        def s(name):
            if name not in S:
                S[name] = sem(name)
            return S[name]

        raw_in, x_in, w_in, w2_in = s("raw_in"), s("x_in"), s("w_in"), s("w2_in")
        raw2_in = s("raw2_in")
        consts = s("consts")
        vec = s("vec")
        sort_ready, turned, turn_copied = s("sort_ready"), s("turned"), s("turn_copied")
        half_copied, digits_in = s("half_copied"), s("digits_in")
        var_ready, std_ready, norm1_ready = s("var_ready"), s("std_ready"), s("norm1_ready")
        wt_turned, wt_copied = s("wt_turned"), s("wt_copied")
        xn_ready, xn_turned, xT_ready, h_done, h_copied = (s("xn_ready"), s("xn_turned"), s("xT_ready"),
                                                           s("h_done"), s("h_copied"))
        h_stored = [s("h_stored0"), s("h_stored1")]
        sums_ready, count_done, steps_ready, steps_done, tab_ready = (
            s("sums_ready"), s("count_done"), s("steps_ready"), s("steps_done"), s("tab_ready"))
        pairs_ready, pairs_stored = s("pairs_ready"), s("pairs_stored")
        idx_in = [s(f"idx_in{j}") for j in range(RING)]
        rows_in = [s(f"rows_in{j}") for j in range(RING)]
        onehot_ready, step_done, step_added = s("onehot_ready"), s("step_done"), s("step_added")
        digit_ready, digit_done = s("digit_ready"), s("digit_done")
        keys2_ready, keys2_stored, keys2_in = s("keys2_ready"), s("keys2_stored"), s("keys2_in")
        hist_copied, hist_summed = s("hist_copied"), s("hist_summed")
        x1_ready, x1_stored = s("x1_ready"), s("x1_stored")
        xn2_ready, xn2_turned, xT2_ready, g_done, g_copied = (s("xn2_ready"), s("xn2_turned"), s("xT2_ready"),
                                                              s("g_done"), s("g_copied"))
        xT_stored = [s("xT_stored0"), s("xT_stored1")]
        table_ready, table_stored = s("table_ready"), s("table_stored")
        slot_ready, gathers_begun = s("slot_ready"), s("gathers_begun")
        gat_in = [s(f"gat_in{g}") for g in range(GG)]
        xc_in, up_done, act_done, down_done, y_copied = (s("xc_in"), s("up_done"), s("act_done"),
                                                         s("down_done"), s("y_copied"))
        y_stored = [s("y_stored0"), s("y_stored1")]
        tails_ready, tails_turned, carry_ready, carry_turned = (s("tails_ready"), s("tails_turned"),
                                                                s("carry_ready"), s("carry_turned"))
        spill_ready, spill_done = s("spill_ready"), s("spill_done")
        logit_ready, exp_ready = s("logit_ready"), s("exp_ready")
        edge_sums_ready, edge_sums_stored, node_sums_in = (s("edge_sums_ready"), s("edge_sums_stored"),
                                                           s("node_sums_in"))
        rvar_ready, rstd_in, d_ready, dexp_ready = s("rvar_ready"), s("rstd_in"), s("d_ready"), s("dexp_ready")
        FR = 12
        fin_in = [s(f"fin_in{j}") for j in range(FR)]
        fin_ready, fin_step, stats_in = s("fin_ready"), s("fin_step"), s("stats_in")
        fin_out = [s(f"fin_out{j}") for j in range(FR)]

        finy = big[:, 0:FR * (EXP + 1) * D].rearrange("p (r e c) -> p r e c", r=FR, e=EXP + 1)
        fino = big[:, FR * (EXP + 1) * D:FR * (EXP + 2) * D].rearrange("p (r c) -> p r c", r=FR)
        o2 = FR * (EXP + 2) * D
        nsum = big[:, o2:o2 + NB * ROW].rearrange("p (n f) -> p n f", f=ROW)
        o2 += NB * ROW
        nw = [big[:, o2 + q * NB * FEAT:o2 + (q + 1) * NB * FEAT] for q in range(3)]
        o2 += 3 * NB * FEAT
        nv = [big[:, o2 + q * NB:o2 + (q + 1) * NB] for q in range(14)]
        o2 += 14 * NB
        score = [big[:, o2 + q * NB:o2 + (q + 1) * NB] for q in range(EXP)]
        o2 += EXP * NB
        rank = [big[:, o2 + q * NB:o2 + (q + 1) * NB] for q in range(EXP)]
        o2 += EXP * NB
        den = big[:, o2:o2 + NB * HEADS].rearrange("p (n h) -> p n h", h=HEADS)

        UNITS = NBP // 2
        C_TURNS, R_TURNS = len(TURN_OF["chunk"]), len(TURN_OF["route"])
        side = ([("chunk", st) for st in CHUNK_STEPS] + [("lay", None)] + [("keys", None)]
                + [("route", st) for st in ROUTE_STEPS] + [("flags", None)])
        weight = {"chunk": 1.2, "lay": 12.0, "keys": 6.0, "route": 2.3, "flags": 8.0}
        ROUND_PAIRS = [(c * C_ITERS + a, c * C_ITERS + min(a + 2, C_ITERS)) for c in range(CHUNKS) for a in range(1, C_ITERS, 2)]
        share = sum(weight[kind] for kind, _ in side) / (len(ROUND_PAIRS) - 3)
        assert sum(weight[kind] for kind, _ in side[:len(CHUNK_STEPS) + 1]) < share * (len(ROUND_PAIRS) // 2 - 1)
        BURSTS, at = [], 0
        for n, (a, b) in enumerate(ROUND_PAIRS):
            take, spent = at, 0.0
            while take < len(side) and (spent < share or n == len(ROUND_PAIRS) - 1):
                spent += weight[side[take][0]]
                take += 1
            BURSTS.append((side[at:take], a, b))
            at = take
        assert at == len(side)

        block = ctx.enter_context(nc.Block())

        @block.sync
        def _(sp):
            sp.dma_start(rows_raw, src.rearrange("(p t) -> p t", p=E1_P)).then_inc(raw_in, 16)
            sp.dma_start(cols_raw, dst.rearrange("(p t) -> p t", p=E1_P)).then_inc(raw_in, 16)
            sp.wait_ge(consts, 1)
            n3 = nodes.rearrange("p (n c) -> p n c", c=D)
            sp.dma_start(n3[:, 0:NB - 1, :], x[0:(NB - 1) * P, :].rearrange("(n p) c -> p n c", p=P)).then_inc(x_in, 16)
            sp.dma_start(n3[0:TAIL, NB - 1, :], x[(NB - 1) * P:N, :]).then_inc(x_in, 16)
            sp.dma_start(wraw[:, :, :], gnn_W.rearrange("(k p) c -> p k c", p=P)).then_inc(w_in, 16)
            sp.dma_start(brow[:, :], gnn_b.rearrange("(a c) -> a c", a=1)).then_inc(w_in, 16)
            e2 = edge_index.rearrange("a (p t) -> a p t", p=P)
            sp.dma_start(r_src, e2[0]).then_inc(raw2_in, 16)
            sp.dma_start(r_dst, e2[1]).then_inc(raw2_in, 16)
            sp.dma_start(wg[:, :, :], W_gat.rearrange("(k p) f -> p k f", p=P)).then_inc(w2_in, 16)
            for q, a in enumerate((att_src, att_dst)):
                sp.dma_start(att[:, q, :], a.rearrange("(o h) e -> o (h e)", o=1).to_broadcast([P, FEAT])).then_inc(w2_in, 16)
            for q, a in enumerate((b_gat, ln_gamma, ln_beta)):
                sp.dma_start(gpar[:, q, :], a.rearrange("(o f) -> o f", o=1).to_broadcast([P, FEAT])).then_inc(w2_in, 16)
            for e in range(EXP):
                sp.dma_start(w1s[:, e, :, :], W1[e].rearrange("(k p) f -> p k f", p=P)).then_inc(w2_in, 16)
                sp.dma_start(w2s[:, e, :, :], W2[e].rearrange("(k p) f -> p k f", p=P)).then_inc(w2_in, 16)
                sp.dma_start(b1s[:, e, :], b1[e].rearrange("(f p) -> p f", p=P), allow_slow_non_contiguous=True).then_inc(w2_in, 16)
            sp.dma_start(b2s[:, :, :], b2.rearrange("(o e) c -> o e c", o=1)).then_inc(w2_in, 16)
            h_u = h_d.rearrange("(u t p) c -> p u t c", t=2, p=P)

            def store_h(u, par):
                sp.wait_ge(h_copied, u + 1)
                sp.dma_start(h_u[:, bass.ds(u, 1), :, :].rearrange("p o t c -> p (o t) c"),
                             hst[:, par, :].rearrange("p (t c) -> p t c", t=2)).then_inc(h_stored[par], 16)

            with sp.Fori(0, UNITS // 2) as i:
                for par in range(2):
                    store_h(2 * i + par, par)
            store_h(UNITS - 1, 0)
            sp.wait_ge(pairs_stored, 16)
            sp.wait_ge(tab_ready, 1)

            def load_step(i, j, first):
                if not first:
                    sp.wait_ge(step_done, i * RING + j + 1 - RING)
                at = sp.value_load(step_tab[0:1, 0, bass.ds(i * RING + j, 1)], min_val=0, max_val=CHUNKS * P * CHUNK_W - G)
                sp.dma_start(idx_slot[:, j, :, :], pairs_d[bass.ds(at, G), :].rearrange("(p t) w -> p t w", p=P)).then_inc(idx_in[j], 16)

            for j in range(RING):
                load_step(0, j, True)
            with sp.Fori(1, C_ITERS) as i:
                for j in range(RING):
                    load_step(i, j, False)
            sp.wait_ge(pairs_stored, 32)
            sp.wait_ge(tab_ready, 2)
            with sp.Fori(C_ITERS, ITERS) as i:
                for j in range(RING):
                    load_step(i, j, False)
            sp.wait_ge(x1_ready, 1)
            sp.dma_start(x1_d.rearrange("(n p) c -> p n c", p=P), n3).then_inc(x1_stored, 16)

            def store_xT(u, par):
                sp.wait_ge(xT2_ready, u + 1)
                sp.dma_start(xT_d[:, bass.ds(2 * u, 2), :], xT[:, par, :].rearrange("p (t c) -> p t c", t=2)).then_inc(xT_stored[par], 16)

            with sp.Fori(0, UNITS // 2) as i:
                for par in range(2):
                    store_xT(2 * i + par, par)
            store_xT(UNITS - 1, 0)
            sp.wait_ge(table_ready, 1)
            sp.dma_start(tab_d.rearrange("(n p) f -> p n f", p=P), table[:, :, :]).then_inc(table_stored, 16)
            for par in range(2):
                sp.wait_ge(xT_stored[par], 16 * (UNITS // 2 + 1 - par))

            def load_chunk(start, tiles):
                sp.dma_start(xc[:, 0:tiles, :], xT_d[:, bass.ds(start, tiles), :]).then_inc(xc_in, 16)

            def store_chunk(i, start, tiles, next_tiles):
                for e in range(EXP):
                    if e == EXP - 1 and next_tiles:
                        sp.wait_ge(up_done, (i + 1) * EXP * FC)
                        load_chunk((i + 1) * CHT, next_tiles)
                    sp.wait_ge(y_copied, EXP * i + e + 1)
                    sp.dma_start(y_d[bass.ds(start * P, tiles * P), e, :].rearrange("(n p) c -> p n c", p=P),
                                 yst[:, e % 2, 0:tiles, :]).then_inc(y_stored[e % 2], 16)

            load_chunk(0, CHT)
            with sp.Fori(0, NCH - 1) as i:
                store_chunk(i, i * CHT, CHT, CHT)
            store_chunk(NCH - 1, (NCH - 1) * CHT, CHT, REST)
            store_chunk(NCH, NCH * CHT, REST, 0)
            sp.wait_ge(edge_sums_ready, 1)
            sp.dma_start(sums_d.rearrange("(p t) f -> p (t f)", p=P), big[:, :]).then_inc(edge_sums_stored, 16)
            sp.wait_ge(edge_sums_stored, 16)
            sp.wait_ge(x1_stored, 16)
            for e in range(2):
                sp.wait_ge(y_stored[e], 16 * (NCH + 1) * EXP // 2)

            def load_final(n, j, rows):
                sp.dma_start(finy[0:rows, j, 0:EXP, :], y_d[bass.ds(n * P, rows), :, :]).then_inc(fin_in[j], 16)
                sp.dma_start(finy[0:rows, j, EXP, :], x1_d[bass.ds(n * P, rows), :]).then_inc(fin_in[j], 16)

            def store_final(n, j, rows):
                sp.wait_ge(fin_ready, n + 1)
                sp.dma_start(out[bass.ds(n * P, rows), :], fino[0:rows, j, :]).then_inc(fin_out[j], 16)

            LOOP = (NB - 1) // FR
            for j in range(FR):
                load_final(j, j, P)
            with sp.Fori(0, LOOP - 1) as i:
                for j in range(FR):
                    store_final(i * FR + j, j, P)
                    load_final((i + 1) * FR + j, j, P)
            for j in range(FR):
                store_final((LOOP - 1) * FR + j, j, P)
                if j == 0:
                    load_final(NB - 1, 0, TAIL)
            store_final(NB - 1, 0, TAIL)
            for j in range(FR):
                sp.wait_ge(fin_out[j], 16 * (LOOP + (j == 0)))

        @block.gpsimd
        def _(pool):
            nc.gpsimd.memset(nodes[:, (NB - 1) * D:NBP * D], 0.0).then_inc(consts, 1)
            nc.gpsimd.memset(ident[:, :], 0.0).then_inc(consts, 1)
            nc.gpsimd.memset(tri[:, :], 1.0).then_inc(consts, 1)
            pool.wait_ge(consts, 3)
            nc.gpsimd.affine_select(out=ident[:, :], in_=ident[:, :], compare_op=ALU.not_equal, fill=1.0, base=0,
                                    pattern=[[-1, P]], channel_multiplier=1).then_inc(consts, 1)
            nc.gpsimd.affine_select(out=tri[:, :], in_=tri[:, :], compare_op=ALU.is_ge, fill=0.0, base=0,
                                    pattern=[[1, P]], channel_multiplier=-1).then_inc(consts, 1)
            nc.gpsimd.memset(ones[:, :], 1.0).then_inc(consts, 1)
            nc.gpsimd.memset(zero_bf[:, :], 0.0).then_inc(consts, 1)
            nc.gpsimd.iota(iota_i[:, :], [[0, 8]], base=0, channel_multiplier=1).then_inc(consts, 1)
            nc.gpsimd.iota(iota_c[:, :], [[1, P]], base=0, channel_multiplier=0,
                           allow_small_or_imprecise_dtypes=True).then_inc(consts, 1)
            nc.gpsimd.iota(thr[:, :], [[-P, NBP]], base=0, channel_multiplier=0,
                           allow_small_or_imprecise_dtypes=True).then_inc(consts, 1)
            nc.gpsimd.iota(step_iota[:, :], [[1, C_STEPS]], base=0, channel_multiplier=0,
                           allow_small_or_imprecise_dtypes=True).then_inc(consts, 1)
            nc.gpsimd.iota(mark_iota[:, :], [[1, MARKS]], base=0, channel_multiplier=MARKS).then_inc(consts, 1)
            nc.gpsimd.iota(node_iota[:, :], [[P, 64]], base=0, channel_multiplier=1,
                           allow_small_or_imprecise_dtypes=True).then_inc(consts, 1)
            for t in range(2):
                pool.wait_ge(h_stored[t], 16 * (UNITS // 2 + 1 - t))

            def gather_step(i, j, first):
                pool.wait_ge(idx_in[j], 16 * i + 16)
                if not first:
                    pool.wait_ge(step_done, i * RING + j + 1 - RING)
                pool.sem_inc(gathers_begun, 1)
                for t in range(WIN):
                    nc.gpsimd.indirect_dma_start(
                        gathered[:, j, t, :], None, h_d[:, :],
                        bass.IndirectOffsetOnAxis(ap=idx_slot[:, j, t, 1:2].bitcast(I32), axis=0)).then_inc(rows_in[j], 16)

            for j in range(RING):
                gather_step(0, j, True)
            with pool.Fori(1, ITERS) as i:
                for j in range(RING):
                    gather_step(i, j, False)
            pool.wait_ge(table_stored, 16)
            with pool.Fori(0, GITERS) as i:
                for g in range(GG):
                    pool.wait_ge(slot_ready, GG * i + g + 1)
                    pool.sem_inc(gathers_begun, 1)
                    for q in range(GQ):
                        nc.gpsimd.indirect_dma_start(
                            gat_ring[:, g, q, :], None, tab_d[:, :],
                            bass.IndirectOffsetOnAxis(ap=gat_slot[:, g, q:q + 1], axis=0)).then_inc(gat_in[g], 16)
            pool.wait_ge(edge_sums_stored, 16)
            for n in range(NB):
                nc.gpsimd.indirect_dma_start(
                    nsum[:, n, :], None, sums_d[:, :],
                    bass.IndirectOffsetOnAxis(ap=end_idx[:, n:n + 1], axis=0)).then_inc(node_sums_in, 16)

        @block.scalar
        def _(act):
            act.wait_ge(wt_turned, 1)
            nc.scalar.activation(wt.rearrange("p k c -> p (k c)"), bank(7), ACT.Copy).then_inc(wt_copied, 1)
            act.wait_ge(var_ready, 1)
            nc.scalar.activation(std[:, :], mv[:, :, 1], ACT.Sqrt).then_inc(std_ready, 1)
            act.wait_ge(norm1_ready, 1)

            def normalise(u, par, first):
                if not first:
                    act.wait_ge(xn_turned, u - 1)
                for t in range(2):
                    last = nc.scalar.activation(xn[:, par, t * D:(t + 1) * D], nodes[:, bass.ds((2 * u + t) * D, D)],
                                                ACT.Identity, scale=rstd[:, bass.ds(2 * u + t, 1)],
                                                bias=nmr[:, bass.ds(2 * u + t, 1)])
                last.then_inc(xn_ready, 1)

            def copy_xT(u, par, first):
                act.wait_ge(xn_turned, u + 1)
                if not first:
                    act.wait_ge(h_done, u - 1)
                nc.scalar.activation(xT[:, par, :], bank(4 + par), ACT.Copy).then_inc(xT_ready, 1)

            def copy_h(u, par, first):
                act.wait_ge(h_done, u + 1)
                if not first:
                    act.wait_ge(h_stored[par], 16 * (u - par) // 2 if isinstance(u, int) else 8 * (u - par))
                nc.scalar.activation(hst[:, par, :], bank(6 + par), ACT.Copy).then_inc(h_copied, 1)

            normalise(0, 0, True)
            normalise(1, 1, True)
            copy_xT(0, 0, True)
            normalise(2, 0, False)
            copy_xT(1, 1, True)
            copy_h(0, 0, True)
            normalise(3, 1, False)
            copy_xT(2, 0, False)
            copy_h(1, 1, True)
            with act.Fori(2, UNITS // 2) as i:
                for par in range(2):
                    u = 2 * i + par
                    normalise(u, par, False)
                    copy_xT(u - 1, 1 - par, False)
                    copy_h(u - 2, par, False)
            normalise(UNITS - 1, 0, False)
            copy_xT(UNITS - 2, 1, False)
            copy_h(UNITS - 3, 0, False)
            copy_xT(UNITS - 1, 0, False)
            copy_h(UNITS - 2, 1, False)
            copy_h(UNITS - 1, 0, False)

            turns_done = [0, 0]

            def turn_copies(net):
                bufs, halves = (chunkbuf, 1) if net == "chunk" else (routebuf, 2)
                of = TURN_OF[net]
                to = bufs[1 - of[turns_done[0] % len(of) if net == "chunk" else turns_done[0] - CHUNKS * C_TURNS]]
                turns_done[0] += 1
                for b in range(halves):
                    act.wait_ge(turned, turns_done[1] + 1)
                    nc.scalar.activation(to[:, b * 1024:b * 1024 + 512], bank(0), ACT.Copy).then_inc(turn_copied, 1)
                    turns_done[1] += 2

            act.wait_ge(raw_in, 32)
            act.wait_ge(consts, 14)
            def count_signs(q):
                c, b = divmod(q, NBP)
                if q:
                    act.wait_ge(sums_ready, q)
                nc.scalar.activation(junk[0:E1_P, :], rows_raw[:, c * C_W:(c + 1) * C_W], ACT.Sign,
                                     bias=thr[0:E1_P, b:b + 1],
                                     accum_out=signsum[0:E1_P, c, b:b + 1]).then_inc(sums_ready, 1)

            def store_pairs(c):
                act.wait_ge(pairs_ready, c + 1)
                act.dma_start(pairs_d[c * P * CHUNK_W:(c + 1) * P * CHUNK_W, :].rearrange("(p t) w -> p (t w)", p=P),
                              pairs.rearrange("p t w -> p (t w)")).then_inc(pairs_stored, 16)

            def reload_keys():
                act.wait_ge(keys2_ready, 1)
                act.dma_start(keys2_d.rearrange("(p t) -> p t", p=P), routebuf[ROUTE_IN].bitcast(I32)).then_inc(keys2_stored, 16)
                act.wait_ge(keys2_stored, 16)
                halo = bass.AP(tensor=keys2_d.tensor, offset=0, ap=[[TG, P], [1, TG + 1]])
                act.dma_start(key2, halo).then_inc(keys2_in, 16)

            def digits(i, first):
                for q in range(HQ):
                    if not first:
                        act.wait_ge(digit_done, (i - 1) * HQ + q + 1)
                    nc.scalar.activation(oh_hi[:, q, :], digit_axis[:, 0:64], ACT.Sign, bias=dig_hi[:, bass.ds(i * HQ + q, 1)])
                    nc.scalar.activation(oh_lo[:, q, :], digit_axis[:, :], ACT.Sign, bias=dig_lo[:, bass.ds(i * HQ + q, 1)]).then_inc(digit_ready, 1)

            per = -(-NBP // C_TURNS)
            for n in range(C_TURNS):
                turn_copies("chunk")
                for q in range(n * per, min((n + 1) * per, NBP)):
                    count_signs(q)
            store_pairs(0)
            act.wait_ge(digits_in, 1)
            digits(0, True)
            for q in range(NBP, 2 * NBP):
                count_signs(q)
            for entries, a, b in BURSTS:
                if a == C_ITERS + 1:
                    digits(C_ITERS, False)
                for kind, entry in entries:
                    if kind == "lay":
                        store_pairs(1)
                    elif kind == "flags":
                        reload_keys()
                    elif entry and entry[0] == "turn":
                        turn_copies(kind)
                with act.Fori(a, b) as i:
                    digits(i, False)
            act.wait_ge(var_ready, 2)
            nc.scalar.activation(std[:, :], mv[:, :, 1], ACT.Sqrt).then_inc(std_ready, 1)

            def copy_xT2(u, par, first):
                act.wait_ge(xn2_turned, u + 1)
                if not first:
                    act.wait_ge(g_done, u - 1)
                    act.wait_ge(xT_stored[par], 16 * (u - par) // 2 if isinstance(u, int) else 8 * (u - par))
                nc.scalar.activation(xT[:, par, :], bank(4 + par), ACT.Copy).then_inc(xT2_ready, 1)

            for par in range(2):
                copy_xT2(par, par, True)
            with act.Fori(1, UNITS // 2) as i:
                for par in range(2):
                    copy_xT2(2 * i + par, par, False)
            copy_xT2(UNITS - 1, 0, False)

            def expert_chunk(i, tiles, first):
                for e in range(EXP):
                    for f in range(FC):
                        act.wait_ge(up_done, (i * EXP + e) * FC + f + 1)
                        if not (first and e < 2):
                            act.wait_ge(down_done, i * EXP + e - 1)
                        nc.scalar.activation(hidden[:, e % 2, f, 0:tiles * P], bank(f % 2)[:, 0:tiles * P], ACT.Gelu,
                                             bias=b1s[:, e, f:f + 1]).then_inc(act_done, 1)
                    act.wait_ge(down_done, i * EXP + e + 1)
                    if not (first and e < 2):
                        act.wait_ge(y_stored[e % 2], 16 * (2 * i + e // 2))
                    nc.scalar.activation(yst[:, e % 2, 0:tiles, :].rearrange("p n c -> p (n c)"),
                                         ps[:, 1024:1024 + tiles * D], ACT.Copy).then_inc(y_copied, 1)

            expert_chunk(0, CHT, True)
            with act.Fori(1, NCH) as i:
                expert_chunk(i, CHT, False)
            expert_chunk(NCH, REST, False)
            act.wait_ge(logit_ready, 1)
            nc.scalar.activation(edges[:, :, FEAT:FEAT + HEADS], edges[:, :, FEAT:FEAT + HEADS], ACT.Exp).then_inc(exp_ready, 1)
            act.wait_ge(rvar_ready, 1)
            nc.scalar.activation(nv[1], nv[1], ACT.Sqrt).then_inc(rstd_in, 1)
            act.wait_ge(d_ready, 1)
            nc.scalar.activation(nv[13], nv[12], ACT.Exp).then_inc(dexp_ready, 1)

        @block.tensor
        def _(pe):
            pe.wait_ge(consts, 4)
            pe.wait_ge(w_in, 32)
            for k in range(KC):
                for m in range(KC):
                    last = nc.tensor.transpose(bank(7)[:, (k * KC + m) * P:(k * KC + m + 1) * P],
                                               wraw[:, m, k * P:(k + 1) * P], ident[:, :])
            last.then_inc(wt_turned, 1)
            pe.wait_ge(wt_copied, 1)
            pe.wait_ge(consts, 6)

            def turn_x(u, par, ready, turned_x, first, until):
                pe.wait_ge(ready, u + 1)
                if not first:
                    pe.wait_ge(until, u - 1)
                for t in range(2 * KC):
                    last = nc.tensor.transpose(bank(4 + par)[:, t * P:(t + 1) * P], xn[:, par, t * P:(t + 1) * P], ident[:, :])
                last.then_inc(turned_x, 1)

            def multiply_h(u, par, first):
                pe.wait_ge(xT_ready, u + 1)
                if not first:
                    pe.wait_ge(h_copied, u - 1)
                for t in range(2):
                    o = bank(6 + par)[:, t * D:(t + 1) * D]
                    for k in range(KC):
                        at = (t * KC + k) * P
                        nc.tensor.matmul(o, xT[:, par, at:at + P], wt[:, k, :], start=(k == 0), stop=False)
                    last = nc.tensor.matmul(o, ones[0:1, :], brow[0:1, :], start=False, stop=True)
                last.then_inc(h_done, 1)

            turn_x(0, 0, xn_ready, xn_turned, True, None)
            turn_x(1, 1, xn_ready, xn_turned, True, None)
            multiply_h(0, 0, True)
            turn_x(2, 0, xn_ready, xn_turned, False, xT_ready)
            multiply_h(1, 1, True)
            turn_x(3, 1, xn_ready, xn_turned, False, xT_ready)
            multiply_h(2, 0, False)
            with pe.Fori(2, UNITS // 2) as i:
                for par in range(2):
                    u = 2 * i + par
                    turn_x(u, par, xn_ready, xn_turned, False, xT_ready)
                    multiply_h(u - 1, 1 - par, False)
            turn_x(UNITS - 1, 0, xn_ready, xn_turned, False, xT_ready)
            multiply_h(UNITS - 2, 1, False)
            multiply_h(UNITS - 1, 0, False)

            turns_done = [0]
            copies_done = [0, 0]

            def turn(net):
                bufs, halves = (chunkbuf, 1) if net == "chunk" else (routebuf, 2)
                of = TURN_OF[net]
                frm = bufs[of[turns_done[0] % len(of) if net == "chunk" else turns_done[0] - CHUNKS * C_TURNS]]
                turns_done[0] += 1
                pe.wait_ge(sort_ready, turns_done[0])
                for half in range(halves):
                    for b in range(2):
                        if half and b == 0:
                            pe.wait_ge(turn_copied, copies_done[0] + 1)
                        if half and b == 1:
                            pe.wait_ge(half_copied, copies_done[1] + 1)
                        for q in range(4):
                            at = (8 * half + 4 * b + q) * P
                            last = nc.tensor.transpose(bank(b)[:, q * P:(q + 1) * P], frm[:, at:at + P], ident[:, :])
                        last.then_inc(turned, 1)
                copies_done[0] += halves
                copies_done[1] += halves - 1

            def lay_steps(c):
                pe.wait_ge(sums_ready, CHUNKS * NBP)
                nc.tensor.matmul(ps_tab[0:NB, 0:1], signsum[0:E1_P, c, 0:NB], ones[0:E1_P, 0:1], start=True, stop=True)
                nc.tensor.matmul(ps_tab[0:NB, 1:2], signsum[0:E1_P, c, 1:NBP], ones[0:E1_P, 0:1], start=True, stop=True).then_inc(count_done, 1)
                pe.wait_ge(steps_ready, 3 * c + 1)
                nc.tensor.matmul(ps_tab[0:NB, 2:3], tri[0:NB, 0:NB], small[0:NB, 3:4], start=True, stop=True).then_inc(count_done, 1)
                pe.wait_ge(steps_ready, 3 * c + 2)
                nc.tensor.matmul(ps_tab[:, 0:C_STEPS], ones[0:NB, :], block_over[0:NB, :], start=True, stop=True).then_inc(steps_done, 1)
                pe.wait_ge(steps_ready, 3 * c + 3)
                nc.tensor.matmul(ps_tab[0:1, 0:C_STEPS], small[0:NB, 5:6], block_over[0:NB, :], start=True, stop=True).then_inc(steps_done, 1)

            for n in range(C_TURNS):
                turn("chunk")
            pe.wait_ge(h_copied, UNITS)
            lay_steps(0)
            pe.wait_ge(consts, 7)
            nc.tensor.matmul(ps_hist, zero_bf[:, :], zero_bf[:, 0:64], start=True, stop=False)

            def step(i, j, first):
                pe.wait_ge(onehot_ready, i * RING + j + 1)
                pe.wait_ge(rows_in[j], 32 * i + 32)
                if not (first and j < PRING):
                    pe.wait_ge(step_added, i * RING + j + 1 - PRING)
                for t in range(WIN):
                    last = nc.tensor.matmul(ps_step[j % PRING], onehot[:, j, t, :], gathered[:, j, t, :],
                                            start=(t == 0), stop=(t == WIN - 1))
                last.then_inc(step_done, 1)

            def digits(i):
                for q in range(HQ):
                    pe.wait_ge(digit_ready, i * HQ + q + 1)
                    nc.tensor.matmul(ps_hist, oh_lo[:, q, :], oh_hi[:, q, :], start=False, stop=False).then_inc(digit_done, 1)

            for j in range(RING):
                step(0, j, True)
            digits(0)
            for entries, a, b in BURSTS:
                if a == C_ITERS + 1:
                    for j in range(RING):
                        step(C_ITERS, j, False)
                    digits(C_ITERS)
                for kind, entry in entries:
                    if kind == "lay":
                        lay_steps(1)
                    elif entry and entry[0] == "turn":
                        turn(kind)
                with pe.Fori(a, b) as i:
                    for j in range(RING):
                        step(i, j, False)
                    digits(i)
            nc.tensor.matmul(ps_hist, zero_bf[:, :], zero_bf[:, 0:64], start=False, stop=True).then_inc(digit_done, 1)
            pe.wait_ge(hist_copied, 1)
            nc.tensor.matmul(ps_tab[:, 0:64], last_row[:, :], histo[:, 0, 1:65], start=True, stop=True).then_inc(hist_summed, 1)
            pe.wait_ge(w2_in, 16 * (7 + 3 * EXP))

            def multiply_g(u, par, first):
                pe.wait_ge(xT2_ready, u + 1)
                if not first:
                    pe.wait_ge(g_copied, u - 1)
                for t in range(2):
                    for k in range(KC):
                        at = (t * KC + k) * P
                        last = nc.tensor.matmul(bank(6 + par)[:, t * FEAT:(t + 1) * FEAT], xT[:, par, at:at + P], wg[:, k, :],
                                                start=(k == 0), stop=(k == KC - 1))
                last.then_inc(g_done, 1)

            turn_x(0, 0, xn2_ready, xn2_turned, True, None)
            turn_x(1, 1, xn2_ready, xn2_turned, True, None)
            multiply_g(0, 0, True)
            turn_x(2, 0, xn2_ready, xn2_turned, False, xT2_ready)
            multiply_g(1, 1, True)
            turn_x(3, 1, xn2_ready, xn2_turned, False, xT2_ready)
            multiply_g(2, 0, False)
            with pe.Fori(2, UNITS // 2) as i:
                for par in range(2):
                    u = 2 * i + par
                    turn_x(u, par, xn2_ready, xn2_turned, False, xT2_ready)
                    multiply_g(u - 1, 1 - par, False)
            turn_x(UNITS - 1, 0, xn2_ready, xn2_turned, False, xT2_ready)
            multiply_g(UNITS - 2, 1, False)
            multiply_g(UNITS - 1, 0, False)

            def expert_chunk(i, tiles, first):
                T = tiles * P
                pe.wait_ge(xc_in, 16 * i + 16)
                for e in range(EXP):
                    for f in range(FC):
                        if not (first and e == 0 and f < 2):
                            pe.wait_ge(act_done, (i * EXP + e) * FC + f - 1)
                        for k in range(KC):
                            last = nc.tensor.matmul(bank(f % 2)[:, 0:T], w1s[:, e, k, f * P:(f + 1) * P],
                                                    xc[:, 0:tiles, k * P:(k + 1) * P], start=(k == 0), stop=(k == KC - 1))
                        last.then_inc(up_done, 1)
                    pe.wait_ge(act_done, (i * EXP + e + 1) * FC)
                    if not (first and e == 0):
                        pe.wait_ge(y_copied, i * EXP + e)
                    for n in range(tiles):
                        y = ps[:, 1024 + n * D:1024 + (n + 1) * D]
                        for f in range(FC):
                            nc.tensor.matmul(y, hidden[:, e % 2, f, n * P:(n + 1) * P], w2s[:, e, f, :], start=(f == 0), stop=False)
                        last = nc.tensor.matmul(y, ones[0:1, :], b2s[0:1, e, :], start=False, stop=True)
                    last.then_inc(down_done, 1)

            expert_chunk(0, CHT, True)
            with pe.Fori(1, NCH) as i:
                expert_chunk(i, CHT, False)
            expert_chunk(NCH, REST, False)
            for r, (nf, at) in enumerate(((HEADS, 0), (HEADS, 0), (HEADS, 1))):
                pe.wait_ge(tails_ready, r + 1)
                nc.tensor.transpose(bank(4)[0:nf, 0:P], carry_t[:, 0:nf], ident[:, :])
                nc.tensor.transpose(bank(4)[0:nf, P:2 * P], carry_f[:, 0:nf], ident[:, :]).then_inc(tails_turned, 1)
                pe.wait_ge(carry_ready, r + 1)
                nc.tensor.transpose(bank(5)[:, 0:nf], carry_r[0:nf, 1, at:at + P], ident[0:nf, 0:nf]).then_inc(carry_turned, 1)
            pe.wait_ge(spill_ready, 1)
            for half, (a, b) in enumerate(SPILL_HALVES):
                last = nc.tensor.matmul(bank(6 + half)[:, 0:(b - a) * NS], spill_lo, spill_hi[:, a * NS:b * NS], start=True, stop=True)
            last.then_inc(spill_done, 1)

        @block.vector
        def _(dve):
            V = nc.vector
            n = [0]

            def done(ins):
                n[0] += 1
                ins.then_inc(vec, 1)
                dve.wait_ge(vec, n[0])

            turns_done = [0, 0]

            def sort_step(net, which):
                kind, cur, *what = which
                bufs = chunkbuf if net == "chunk" else routebuf
                frm, to = bufs[cur], bufs[1 - cur]
                if kind == "flip":
                    a, b = what
                    if b is None:
                        done(V.tensor_scalar(to, frm, sign[:, a:a + 1], None, ALU.mult))
                    else:
                        done(V.tensor_scalar(to, frm, sign[:, a:a + 1], sign[:, b:b + 1], ALU.mult, ALU.mult))
                elif kind == "pair":
                    d, mirror = what
                    f4 = frm.rearrange("p (b s d) -> p b s d", s=2, d=d)
                    t4 = to.rearrange("p (b s d) -> p b s d", s=2, d=d)
                    lo, hi, tlo, thi = f4[:, :, 0, :], f4[:, :, 1, :], t4[:, :, 0, :], t4[:, :, 1, :]
                    if mirror:
                        hi, thi = hi[:, :, ::-1], thi[:, :, ::-1]
                    V.tensor_tensor(tlo, lo, hi, ALU.min)
                    done(V.tensor_tensor(thi, lo, hi, ALU.max))
                else:
                    halves = 1 if net == "chunk" else 2
                    dve.sem_inc(sort_ready, 1)
                    for half in range(halves):
                        dve.wait_ge(turned, turns_done[0] + 2)
                        turns_done[0] += 2
                        last = V.tensor_copy(to[:, half * 1024 + 512:(half + 1) * 1024], bank(1))
                        if half < halves - 1:
                            last.then_inc(half_copied, 1)
                    done(last)
                    turns_done[1] += halves
                    dve.wait_ge(turn_copied, turns_done[1])

            def layer_stats(call):
                with dve.Fori(0, NBP) as i:
                    V.bn_stats(stats[:, bass.ds(i, 1), :].rearrange("p o s -> p (o s)"), nodes[:, bass.ds(i * D, D)]).then_inc(stats_in, 1)
                dve.wait_ge(stats_in, call * NBP)
                for b in range(NBP):
                    last = V.bn_aggr(mv[:, b, :], stats[:, b, :])
                done(last)
                done(V.tensor_scalar_add(mv[:, :, 1], mv[:, :, 1], EPS))
                dve.sem_inc(var_ready, 1)

            dve.wait_ge(raw_in, 32)
            dve.wait_ge(consts, 13)
            for k in range(7):
                V.tensor_scalar(bits[:, k:k + 1], iota_i[:, k:k + 1], k, 1, ALU.logical_shift_right, ALU.bitwise_and)
            done(V.memset(bits[:, 7:8], 0))
            V.tensor_scalar(sign[:, :], bits[:, :], -2.0, 1.0, ALU.mult, ALU.add)
            V.tensor_scalar_add(thr[:, :], thr[:, :], 0.5).then_inc(consts, 1)

            def chunk_keys(c):
                k0, k1 = chunkbuf[0].bitcast(I32), chunkbuf[1].bitcast(I32)
                cols = slice(c * C_W, (c + 1) * C_W)
                V.memset(k0, KEY_BIAS | 0x63FFE000)
                done(V.scalar_tensor_tensor(out=k1[0:E1_P, 0:C_W], in0=rows_raw[:, cols], scalar=13, in1=cols_raw[:, cols],
                                            op0=ALU.logical_shift_left, op1=ALU.bitwise_or))
                done(V.tensor_scalar(k0[0:E1_P, 0:C_W], k1[0:E1_P, 0:C_W], KEY_BIAS, None, ALU.bitwise_or))

            def chunk_pairs(c):
                srt, oth = chunkbuf[CHUNK_IN].bitcast(I32), chunkbuf[1 - CHUNK_IN].bitcast(I32)
                if c:
                    dve.wait_ge(pairs_stored, 16 * c)
                done(V.tensor_scalar(oth, srt, 13, FIELD, ALU.logical_shift_right, ALU.bitwise_and))
                V.tensor_copy(pairs[:, :, 0], oth)
                done(V.tensor_scalar(srt, srt, FIELD, None, ALU.bitwise_and))
                done(V.tensor_scalar_min(pairs_i[:, :, 1], srt, N - 1))
                dve.sem_inc(pairs_ready, 1)

            def lay_steps(c):
                dve.wait_ge(count_done, 2 * c + 1)
                done(V.tensor_scalar(small[0:NB, 0:2], ps_tab[0:NB, 0:2], -0.5, 0.5 * C_E, ALU.mult, ALU.add))
                done(V.tensor_tensor(small[0:NB, 2:3], small[0:NB, 1:2], small[0:NB, 0:1], ALU.subtract))
                done(V.tensor_scalar_add(small_i[0:NB, 0:1], small[0:NB, 2:3], float(G - 1)))
                done(V.tensor_scalar(small_i[0:NB, 1:2], small_i[0:NB, 0:1], G.bit_length() - 1, None, ALU.logical_shift_right))
                done(V.tensor_copy(small[0:NB, 3:4], small_i[0:NB, 1:2]))
                dve.sem_inc(steps_ready, 1)
                done(V.scalar_tensor_tensor(out=small[0:NB, 5:6], in0=small[0:NB, 3:4], scalar=-float(G), in1=small[0:NB, 2:3],
                                            op0=ALU.mult, op1=ALU.add))
                dve.wait_ge(count_done, 2 * c + 2)
                done(V.tensor_copy(small[0:NB, 4:5], ps_tab[0:NB, 2:3]))
                done(V.tensor_scalar(block_over[0:NB, :], step_iota[0:NB, :], small[0:NB, 4:5], None, ALU.is_ge))
                dve.sem_inc(steps_ready, 1)
                dve.wait_ge(steps_done, 2 * c + 1)
                k = slice(c * C_STEPS, (c + 1) * C_STEPS)
                V.tensor_scalar(block_base[:, k], ps_tab[:, 0:C_STEPS], float(P), None, ALU.mult)
                done(V.tensor_scalar(step_tab[0:1, 1, k], ps_tab[0:1, 0:C_STEPS], float(D), None, ALU.mult))
                dve.sem_inc(steps_ready, 1)
                dve.wait_ge(steps_done, 2 * c + 2)
                done(V.scalar_tensor_tensor(out=small_row, in0=step_iota[0:1, :], scalar=float(G),
                                            in1=ps_tab[0:1, 0:C_STEPS], op0=ALU.mult, op1=ALU.add))
                done(V.tensor_scalar_add(step_tab[0:1, 0, k], small_row, float(c * P * CHUNK_W)))
                dve.sem_inc(tab_ready, 1)

            chunk_keys(0)
            for at, which in enumerate(CHUNK_STEPS):
                if at == 22:
                    dve.wait_ge(x_in, 32)
                    layer_stats(1)
                    dve.wait_ge(std_ready, 1)
                    done(V.reciprocal(rstd[:, :], std[:, :]))
                    V.scalar_tensor_tensor(out=nmr[:, :], in0=mv[:, :, 0], scalar=-1.0, in1=rstd[:, :],
                                           op0=ALU.mult, op1=ALU.mult).then_inc(norm1_ready, 1)
                if at == 60:
                    dve.wait_ge(raw2_in, 32)
                    V.tensor_scalar(dig_hi[:, 0:E2_W].bitcast(I32), r_dst, 7, None, ALU.logical_shift_right)
                    V.tensor_scalar(dig_lo[:, 0:E2_W].bitcast(I32), r_dst, P - 1, None, ALU.bitwise_and)
                    V.memset(dig_hi[:, E2_W:HCOLS], -63.0)
                    done(V.memset(dig_lo[:, E2_W:HCOLS], -float(P - 1)))
                    V.tensor_scalar(dig_hi[:, 0:E2_W], dig_hi[:, 0:E2_W].bitcast(I32), -1.0, None, ALU.mult)
                    V.tensor_scalar(dig_lo[:, 0:E2_W], dig_lo[:, 0:E2_W].bitcast(I32), -1.0, None, ALU.mult)
                    V.tensor_scalar(last_row[:, :], ones[:, :], ident[:, P - 1:P], None, ALU.mult)
                    V.tensor_scalar_add(digit_axis[:, :], iota_c[:, :], 0.5).then_inc(digits_in, 1)
                sort_step("chunk", which)
            chunk_pairs(0)
            lay_steps(0)

            def route_keys():
                s0 = routebuf[0].bitcast(I32)
                V.memset(s0, KEY_BIAS | 0x63FFDFFF)
                done(V.scalar_tensor_tensor(out=r_src, in0=r_dst, scalar=14, in1=r_src,
                                            op0=ALU.logical_shift_left, op1=ALU.bitwise_or))
                V.tensor_scalar(s0[:, 0:E2_W], r_src, KEY_BIAS | 0x2000, None, ALU.bitwise_or)
                dve.wait_ge(pairs_stored, 16 * CHUNKS)
                done(V.scalar_tensor_tensor(out=mark_tmp, in0=mark_iota[:, :], scalar=14, in1=mark_iota[:, :],
                                            op0=ALU.logical_shift_left, op1=ALU.bitwise_or))
                done(V.tensor_scalar(s0[:, E2_W:E2_W + MARKS], mark_tmp, KEY_BIAS, None, ALU.bitwise_or))

            def route_flags():
                dve.sem_inc(keys2_ready, 1)
                dve.wait_ge(keys2_in, 16)
                V.tensor_scalar(last_i[:, 0:1], key2[:, TG - 1:TG], 14 + 7, 63, ALU.logical_shift_right, ALU.bitwise_and)
                V.tensor_scalar(last_i[:, 1:2], key2[:, TG - 1:TG], 14, P - 1, ALU.logical_shift_right, ALU.bitwise_and)
                done(V.tensor_scalar(edge_idx[:, :], key2[:, 0:TG], FIELD, None, ALU.bitwise_and))
                V.tensor_copy(last_node[:, :], last_i[:, :])
                V.tensor_scalar_min(edge_idx[:, :], edge_idx[:, :], N - 1)
                done(V.tensor_scalar(key2, key2, 13, 1, ALU.logical_shift_right, ALU.bitwise_and))
                V.tensor_copy(inside[:, :], key2)
                done(V.tensor_scalar(starts[:, :], key2, -1.0, 1.0, ALU.mult, ALU.add))

            def spread(i, j, first):
                dve.wait_ge(idx_in[j], 16 * i + 16)
                if not first:
                    dve.wait_ge(step_done, i * RING + j + 1 - RING)
                V.scalar_tensor_tensor(out=onehot[:, j, :, :], in0=iota_c[:, :].unsqueeze(1).to_broadcast([P, WIN, P]),
                                       scalar=block_base[:, bass.ds(i * RING + j, 1)],
                                       in1=idx_slot[:, j, :, 0].unsqueeze(2).to_broadcast([P, WIN, P]),
                                       op0=ALU.add, op1=ALU.is_equal).then_inc(onehot_ready, 1)

            def add_step(k, j, first):
                dve.wait_ge(step_done, k + 1)
                if not first:
                    dve.wait_ge(step_added, k)
                col = dve.value_load(step_tab[0:1, 1, bass.ds(k, 1)], min_val=0, max_val=NB * D)
                V.tensor_tensor(nodes[:, bass.ds(col, D)], nodes[:, bass.ds(col, D)], ps_step[j % PRING], ALU.add).then_inc(step_added, 1)

            for j in range(RING):
                spread(0, j, True)
                if j >= PRING:
                    add_step(j - PRING, j, j == PRING)
            chunk_keys(1)
            for entries, a, b in BURSTS:
                if a == C_ITERS + 1:
                    for j in range(RING):
                        spread(C_ITERS, j, False)
                        add_step(C_STEPS + j - PRING, j, False)
                for kind, entry in entries:
                    if kind == "lay":
                        chunk_pairs(1)
                        lay_steps(1)
                    elif kind == "keys":
                        route_keys()
                    elif kind == "flags":
                        route_flags()
                    else:
                        sort_step(kind, entry)
                with dve.Fori(a, b) as i:
                    for j in range(RING):
                        spread(i, j, False)
                        add_step(i * RING + j - PRING, j, False)
            for k in range(STEPS - PRING, STEPS):
                add_step(k, k % PRING, False)
            dve.wait_ge(step_added, STEPS)
            dve.sem_inc(x1_ready, 1)
            layer_stats(2)
            dve.wait_ge(digit_done, HCOLS + 1)
            counts, last_counts, ends_at = histo[:, 0, :], histo[:, 1, :], histo[:, 2, 0:64]
            done(V.tensor_copy(counts[:, 1:65], ps_hist))
            V.tensor_scalar(counts[:, 0:1], counts[:, 64:65], -1.0, None, ALU.mult).then_inc(hist_copied, 1)
            dve.wait_ge(hist_summed, 1)
            done(V.tensor_copy(last_counts[:, 1:65], ps_tab[:, 0:64]))
            done(V.tensor_scalar(last_counts[:, 0:1], last_counts[:, 64:65], -1.0, None, ALU.mult))
            done(V.tensor_tensor(counts, counts, last_counts, ALU.add))
            done(V.tensor_tensor(ends_at, counts[:, 1:65], counts[:, 0:64], ALU.subtract))
            done(V.tensor_scalar(last_counts, last_counts, last_counts[:, 64:65], 0.5, ALU.add, ALU.mult))
            done(V.scalar_tensor_tensor(out=ends_at, in0=ends_at, scalar=0.25, in1=last_counts[:, 0:64], op0=ALU.mult, op1=ALU.add))
            V.tensor_tensor(end_idx[:, :], ends_at, node_iota[:, :], ALU.add)
            dve.wait_ge(std_ready, 2)
            done(V.reciprocal(rstd[:, :], std[:, :]))

            def normalise(u, par, first):
                if not first:
                    dve.wait_ge(xn2_turned, u - 1)
                for t in range(2):
                    last = V.tensor_scalar(xn[:, par, t * D:(t + 1) * D], nodes[:, bass.ds((2 * u + t) * D, D)],
                                           mv[:, bass.ds(2 * u + t, 1), 0:1].rearrange("p a b -> p (a b)"),
                                           rstd[:, bass.ds(2 * u + t, 1)], ALU.subtract, ALU.mult)
                last.then_inc(xn2_ready, 1)

            def copy_g(u, par):
                dve.wait_ge(g_done, u + 1)
                V.tensor_copy(table[:, bass.ds(2 * u, 2), 0:FEAT],
                              bank(6 + par)[:, 0:2 * FEAT].rearrange("p (t f) -> p t f", t=2)).then_inc(g_copied, 1)

            normalise(0, 0, True)
            normalise(1, 1, True)
            normalise(2, 0, False)
            copy_g(0, 0)
            normalise(3, 1, False)
            copy_g(1, 1)
            with dve.Fori(2, UNITS // 2) as i:
                for par in range(2):
                    normalise(2 * i + par, par, False)
                    copy_g(2 * i + par - 2, par)
            normalise(UNITS - 1, 0, False)
            copy_g(UNITS - 3, 0)
            copy_g(UNITS - 2, 1)
            copy_g(UNITS - 1, 0)
            dve.wait_ge(g_copied, UNITS)
            wide = flat[:, 0:2 * D]
            for q in range(2):
                for half in range(2):
                    nn = NBP // 2
                    rows = slice(half * nn, (half + 1) * nn)
                    prod = wide[:, 0:nn * FEAT].rearrange("p (n h e) -> p n h e", h=HEADS, e=EXP)
                    done(V.tensor_tensor(prod.rearrange("p n h e -> p n (h e)"), table[:, rows, 0:FEAT],
                                         att[:, q, :].unsqueeze(1).to_broadcast([P, nn, FEAT]), ALU.mult))
                    done(V.tensor_reduce(table[:, rows, FEAT + q * HEADS:FEAT + (q + 1) * HEADS], prod, axis=AX.X, op=ALU.add))
            dve.sem_inc(table_ready, 1)

            dve.wait_ge(x1_stored, 16)
            per = GG * GQ

            def fill(i, g, first):
                if not first:
                    dve.wait_ge(gat_in[g], 16 * GQ * i)
                    V.tensor_copy(edges[:, bass.ds((i - 1) * per + g * GQ, GQ), :], gat_ring[:, g, :, :])
                V.tensor_copy(gat_slot[:, g, :], edge_idx[:, bass.ds(i * per + g * GQ, GQ)]).then_inc(slot_ready, 1)

            for g in range(GG):
                fill(0, g, True)
            with dve.Fori(1, GITERS) as i:
                for g in range(GG):
                    fill(i, g, False)
            for g in range(GG):
                dve.wait_ge(gat_in[g], 16 * GQ * GITERS)
                last = V.tensor_copy(edges[:, TG - per + g * GQ:TG - per + (g + 1) * GQ, :], gat_ring[:, g, :, :])
            done(last)

            f_dst = lambda h: edges[:, :, FEAT + HEADS + h]
            first = starts[:, 0:TG]
            ends = starts[:, 1:TG + 1]
            in_row = inside[:, 0:TG]
            not_end = inside[:, 1:TG + 1]
            a_src = edges[:, :, FEAT:FEAT + HEADS]
            a_dst = edges[:, :, FEAT + HEADS:ROW]
            top = top4[:, :, :].rearrange("p h t -> p t h")
            over_heads = lambda a: a.unsqueeze(2).to_broadcast([P, TG, HEADS])

            V.tensor_reduce(small[:, 0:1], first, axis=AX.X, op=ALU.max)
            done(V.tensor_reduce(small[:, 1:2], ends, axis=AX.X, op=ALU.max))
            V.tensor_scalar(small[:, 4:5], small[:, 0:1], NEG, None, ALU.mult)
            done(V.tensor_scalar(small[:, 2:4], small[:, 0:2], -1.0, 1.0, ALU.mult, ALU.add))

            def carry(r, nf, flag, init, op0, op1, backward):
                done(V.tensor_copy(carry_f[:, 0:nf], flag.to_broadcast([P, nf])))
                dve.sem_inc(tails_ready, 1)
                done(V.memset(carry_r[0:nf, 1, :], init))
                dve.wait_ge(tails_turned, r + 1)
                done(V.tensor_copy(carry_r[0:nf, 0, :], bank(4)[0:nf, 0:2 * P]))
                tails, flags = carry_r[0:nf, 0, 0:P], carry_r[0:nf, 0, P:2 * P]
                state = carry_r[0:nf, 1, 0:P] if backward else carry_r[0:nf, 1, 1:P + 1]
                if backward:
                    tails, flags, state = tails[:, ::-1], flags[:, ::-1], state[:, ::-1]
                done(V.tensor_tensor_scan(state, flags, tails, init, op0, op1))
                dve.sem_inc(carry_ready, 1)
                dve.wait_ge(carry_turned, r + 1)
                done(V.tensor_copy(carry_in[:, 0:nf], bank(5)[:, 0:nf]))

            dve.wait_ge(down_done, EXP * (NCH + 1))
            done(V.tensor_tensor(a_dst, a_dst, over_heads(first), ALU.mult))
            for h in range(HEADS):
                last = V.tensor_tensor_scan(top4[:, h, :], in_row, f_dst(h), 0.0, ALU.mult, ALU.add)
            done(last)
            done(V.tensor_copy(carry_t[:, 0:HEADS], top4[:, :, TG - 1]))
            carry(0, HEADS, small[:, 2:3], 0.0, ALU.mult, ALU.add, False)
            for h in range(HEADS):
                V.tensor_tensor_scan(f_dst(h), in_row, f_dst(h), carry_in[:, h:h + 1], ALU.mult, ALU.add)
            done(V.tensor_scalar(scratch[:, :], first, NEG, None, ALU.mult))
            for h in range(HEADS):
                last = V.tensor_tensor_scan(top4[:, h, :], scratch[:, :], edges[:, :, FEAT + h], NEG, ALU.add, ALU.max)
            done(last)
            done(V.tensor_copy(carry_t[:, 0:HEADS], top4[:, :, TG - 1]))
            carry(1, HEADS, small[:, 4:5], NEG, ALU.add, ALU.max, False)
            for h in range(HEADS):
                last = V.tensor_tensor_scan(top4[:, h, :], scratch[:, :], edges[:, :, FEAT + h], carry_in[:, h:h + 1], ALU.add, ALU.max)
            done(last)
            done(V.tensor_tensor(top4[:, :, :], top4[:, :, :], ends.unsqueeze(1).to_broadcast([P, HEADS, TG]), ALU.mult))
            for h in range(HEADS):
                done(V.tensor_tensor_scan(scratch[:, ::-1], not_end[:, ::-1], top4[:, h, ::-1], 0.0, ALU.mult, ALU.add))
                done(V.tensor_copy(carry_t[:, h:h + 1], scratch[:, 0:1]))
            carry(2, HEADS, small[:, 3:4], 0.0, ALU.mult, ALU.add, True)
            for h in range(HEADS):
                last = V.tensor_tensor_scan(top4[:, h, ::-1], not_end[:, ::-1], top4[:, h, ::-1], carry_in[:, h:h + 1], ALU.mult, ALU.add)
            done(last)
            V.tensor_tensor(a_src, a_src, a_dst, ALU.add)
            done(V.tensor_tensor(top, top, a_dst, ALU.add))
            V.scalar_tensor_tensor(out=a_src, in0=a_src, scalar=0.2, in1=a_src, op0=ALU.mult, op1=ALU.max)
            done(V.scalar_tensor_tensor(out=top, in0=top, scalar=0.2, in1=top, op0=ALU.mult, op1=ALU.max))
            V.tensor_tensor(a_src, a_src, top, ALU.subtract).then_inc(logit_ready, 1)
            dve.wait_ge(exp_ready, 1)
            for h in range(HEADS):
                last = V.tensor_tensor(edges[:, :, h * EXP:(h + 1) * EXP], edges[:, :, h * EXP:(h + 1) * EXP],
                                       edges[:, :, FEAT + h].unsqueeze(2).to_broadcast([P, TG, EXP]), ALU.mult)
            done(last)
            for f in range(NS):
                last = V.tensor_tensor_scan(edges[:, :, f], in_row, edges[:, :, f], 0.0, ALU.mult, ALU.add)
            done(last)
            dve.sem_inc(edge_sums_ready, 1)
            for e in range(2):
                dve.wait_ge(y_stored[e], 16 * (NCH + 1) * EXP // 2)
            V.tensor_scalar(spill_lo, iota_c[:, :], last_node[:, 1:2], not_end[:, TG - 1:TG], ALU.is_equal, ALU.mult)
            V.scalar_tensor_tensor(out=spill_hi.rearrange("p (n f) -> p n f", f=NS),
                                   in0=iota_c[:, 0:NB].unsqueeze(2).to_broadcast([P, NB, NS]), scalar=last_node[:, 0:1],
                                   in1=edges[:, TG - 1, 0:NS].unsqueeze(1).to_broadcast([P, NB, NS]),
                                   op0=ALU.is_equal, op1=ALU.mult).then_inc(spill_ready, 1)

            dve.wait_ge(node_sums_in, 16 * NB)
            dve.wait_ge(w2_in, 16 * (7 + 3 * EXP))
            n4 = lambda a: a.rearrange("p (n h e) -> p n h e", h=HEADS, e=EXP)
            n3 = lambda a: a.rearrange("p (n f) -> p n f", f=FEAT)
            over_n = lambda a: a.unsqueeze(1).to_broadcast([P, NB, FEAT])
            over_f = lambda a: a.unsqueeze(2).to_broadcast([P, NB, FEAT])
            dve.wait_ge(spill_done, 1)
            for half, (a, b) in enumerate(SPILL_HALVES):
                last = V.tensor_tensor(nsum[:, a:b, 0:NS], nsum[:, a:b, 0:NS],
                                       bank(6 + half)[:, 0:(b - a) * NS].rearrange("p (n f) -> p n f", f=NS), ALU.add)
            done(last)
            done(V.tensor_scalar_add(den, nsum[:, :, FEAT:NS], 1e-16))
            done(V.reciprocal(den, den))
            for h in range(HEADS):
                last = V.tensor_tensor(n4(nw[0])[:, :, h, :], nsum[:, :, h * EXP:(h + 1) * EXP],
                                       den[:, :, h].unsqueeze(2).to_broadcast([P, NB, EXP]), ALU.mult)
            done(last)
            done(V.tensor_tensor(n3(nw[0]), n3(nw[0]), over_n(gpar[:, 0, :]), ALU.add))
            done(V.tensor_reduce(nv[0], n3(nw[0]), axis=AX.X, op=ALU.add))
            done(V.tensor_scalar(nv[0], nv[0], 1.0 / FEAT, None, ALU.mult))
            done(V.tensor_tensor(n3(nw[1]), n3(nw[0]), over_f(nv[0]), ALU.subtract))
            done(V.tensor_tensor(nw[2], nw[1], nw[1], ALU.mult))
            done(V.tensor_reduce(nv[1], n3(nw[2]), axis=AX.X, op=ALU.add))
            V.tensor_scalar(nv[1], nv[1], 1.0 / FEAT, EPS, ALU.mult, ALU.add).then_inc(rvar_ready, 1)
            dve.wait_ge(rstd_in, 1)
            done(V.reciprocal(nv[2], nv[1]))
            done(V.tensor_tensor(n3(nw[1]), n3(nw[1]), over_f(nv[2]), ALU.mult))
            done(V.tensor_tensor(n3(nw[1]), n3(nw[1]), over_n(gpar[:, 1, :]), ALU.mult))
            done(V.tensor_tensor(n3(nw[1]), n3(nw[1]), over_n(gpar[:, 2, :]), ALU.add))
            for e in range(EXP):
                last = V.tensor_reduce(score[e], n4(nw[1])[:, :, :, e], axis=AX.X, op=ALU.add)
            done(last)
            for e in range(EXP):
                V.tensor_scalar(score[e], score[e], 1.0 / HEADS, None, ALU.mult)
                last = V.memset(rank[e], float(EXP - 1 - e))
            done(last)
            for a in range(EXP):
                for b in range(a + 1, EXP):
                    done(V.tensor_tensor(nv[0], score[a], score[b], ALU.is_ge))
                    V.tensor_tensor(rank[b], rank[b], nv[0], ALU.add)
                    done(V.tensor_tensor(rank[a], rank[a], nv[0], ALU.subtract))
            V.tensor_tensor(nv[0], score[0], score[1], ALU.max)
            done(V.tensor_tensor(nv[1], score[2], score[3], ALU.max))
            done(V.tensor_tensor(nv[0], nv[0], nv[1], ALU.max))
            done(V.scalar_tensor_tensor(out=nv[12], in0=rank[0], scalar=1.0, in1=score[0], op0=ALU.is_equal, op1=ALU.mult))
            for e in range(1, EXP):
                done(V.scalar_tensor_tensor(out=nv[1], in0=rank[e], scalar=1.0, in1=score[e], op0=ALU.is_equal, op1=ALU.mult))
                done(V.tensor_tensor(nv[12], nv[12], nv[1], ALU.add))
            V.tensor_tensor(nv[12], nv[12], nv[0], ALU.subtract).then_inc(d_ready, 1)
            dve.wait_ge(dexp_ready, 1)
            done(V.tensor_scalar_add(nv[0], nv[13], 1.0))
            done(V.reciprocal(nv[0], nv[0]))
            done(V.tensor_tensor(nv[1], nv[13], nv[0], ALU.mult))
            for e in range(EXP):
                done(V.scalar_tensor_tensor(out=nv[2], in0=rank[e], scalar=0.0, in1=nv[0], op0=ALU.is_equal, op1=ALU.mult))
                done(V.scalar_tensor_tensor(out=gate[:, e, :], in0=rank[e], scalar=1.0, in1=nv[1], op0=ALU.is_equal, op1=ALU.mult))
                done(V.tensor_tensor(gate[:, e, :], gate[:, e, :], nv[2], ALU.add))

            def combine(k, j, n_in, first):
                rows = P if j is not None else TAIL
                j = j or 0
                dve.wait_ge(fin_in[j], 32 * n_in)
                if not first:
                    dve.wait_ge(fin_out[j], 16 * (n_in - 1))
                for e in range(EXP):
                    if e:
                        dve.wait_ge(fin_step, k * EXP + e)
                    add = finy[0:rows, j, EXP, :] if e == 0 else fino[0:rows, j, :]
                    last = V.scalar_tensor_tensor(out=fino[0:rows, j, :], in0=finy[0:rows, j, e, :],
                                                  scalar=gate[0:rows, e, bass.ds(k, 1)], in1=add, op0=ALU.mult, op1=ALU.add)
                    last.then_inc(fin_step, 1)
                dve.wait_ge(fin_step, k * EXP + EXP)
                dve.sem_inc(fin_ready, 1)

            LOOP = (NB - 1) // FR
            for j in range(FR):
                combine(j, j, 1, True)
            with dve.Fori(1, LOOP) as i:
                for j in range(FR):
                    combine(i * FR + j, j, i + 1, False)
            combine(NB - 1, None, LOOP + 1, False)


_INS = ["x", "src", "dst", "L0_gnn_W", "L0_gnn_b", "L0_ffn_W_gat", "L0_ffn_att_src", "L0_ffn_att_dst", "L0_ffn_b_gat",
        "L0_ffn_ln_gamma", "L0_ffn_ln_beta", "L0_ffn_W1", "L0_ffn_b1", "L0_ffn_W2", "L0_ffn_b2", "L0_ffn_edge_index"]


def kernel(**inputs):
    import numpy as _np
    import concourse.bacc as _bacc
    from concourse import mybir as _mybir
    from concourse.bass_utils import run_bass_kernel_spmd as _run

    nc = _bacc.Bacc("TRN2", target_bir_lowering=False, num_devices=1)
    arrays, args = {}, []
    for name in _INS:
        a = _np.ascontiguousarray(inputs[name])
        arrays[f"in_{name}"] = a
        args.append(nc.dram_tensor(f"in_{name}", a.shape, _mybir.dt.from_np(a.dtype), kind="ExternalInput").ap())
    shape = inputs["x"].shape
    out = nc.dram_tensor("out_0", shape, _mybir.dt.float32, kind="ExternalOutput").ap()
    gnn_ffn_kernel(nc, *args, out)
    r = _run(nc, [arrays], core_ids=[0])
    return r.results[0]["out_0"]
```

```python
import concourse.bass as bass
from concourse import mybir
from concourse.alu_op_type import AluOpType as ALU
from contextlib import ExitStack

F32 = mybir.dt.float32
BF16 = mybir.dt.bfloat16
I32 = mybir.dt.int32
ACT = mybir.ActivationFunctionType
AX = mybir.AxisListType

P = 128
KEY_BIAS = 0x10000000
FIELD = 0x1FFF
CHUNK_W, CHUNK_ROW_BITS = 1024, 10
ROUTE_W, ROUTE_ROW_BITS = 2048, 11
PART_BITS = 7
EPS = 1e-5
NEG = -3.0e38


def sort_plan(row_bits):
    steps, cur = [], 0

    def add(kind, *what):
        nonlocal cur
        steps.append((kind, cur, *what))
        cur ^= 1

    add("flip", 0, None)
    for k in range(1, row_bits + 1):
        for j in range(k - 1, -1, -1):
            add("pair", 1 << j, j == k - 1)
    for k in range(row_bits + 1, row_bits + PART_BITS + 1):
        add("flip", k - row_bits - 1, k - row_bits if k < row_bits + PART_BITS else None)
        add("turn")
        for j in range(k - row_bits - 1, -1, -1):
            add("pair", 1 << j, False)
        add("turn")
        for j in range(row_bits - 1, -1, -1):
            add("pair", 1 << j, False)
    return steps, cur


CHUNK_STEPS, CHUNK_IN = sort_plan(CHUNK_ROW_BITS)
ROUTE_STEPS, ROUTE_IN = sort_plan(ROUTE_ROW_BITS)
TURN_OF = {name: [s[1] for s in steps if s[0] == "turn"] for name, steps in (("chunk", CHUNK_STEPS), ("route", ROUTE_STEPS))}


def gnn_ffn_kernel(nc, x, src, dst, gnn_W, gnn_b, W_gat, att_src, att_dst, b_gat, ln_gamma, ln_beta,
                   W1, b1, W2, b2, edge_index, out):
    N, D = x.shape
    E1 = src.shape[0]
    E2 = edge_index.shape[1]
    EXP, _, HID = W1.shape
    HEADS = att_src.shape[0]
    FEAT = HEADS * EXP
    ROW = FEAT + 2 * HEADS
    KC = D // P
    FC = HID // P
    NB = -(-N // P)
    NBP = NB + 1
    TAIL = N - (NB - 1) * P
    CHUNKS = 2
    E1_P, E1_W = 125, E1 // 125
    C_W = E1_W // CHUNKS
    C_E = E1_P * C_W
    WIN = 2
    G = WIN * P
    RING = 8
    PRING = 4
    C_STEPS = -(-((C_E + NB * (G - 1)) // G) // RING) * RING
    C_ITERS = C_STEPS // RING
    STEPS = CHUNKS * C_STEPS
    ITERS = CHUNKS * C_ITERS
    E2_W = E2 // P
    HQ = -(-E2_W // ITERS)
    HCOLS = HQ * ITERS
    MARKS = NB
    GG = EXP - 1
    CHT = 4
    NCH = NB // CHT
    REST = NB - NCH * CHT
    GW = -(-(E2 + P * MARKS) // (P * GG * NCH))
    TG = GW * GG * NCH
    BLOCK_WAITS = 9
    NS = FEAT + HEADS
    NC = NS + HEADS + 1

    ctx = ExitStack()
    with ctx:
        dram = lambda n, s, d=F32: nc.dram_tensor(n, s, d, kind="Internal").ap()
        pairs_d = dram("pairs_d", (CHUNKS * P * CHUNK_W, 2))
        keys2_d = dram("keys2_d", (P * ROUTE_W,), I32)
        h_d = dram("h_d", (NBP * P, D))
        xT_d = dram("xT_d", (P, NBP, KC * P))
        tab_d = dram("tab_d", (NBP * P, ROW))
        y_d = dram("y_d", (NB * P, EXP, D))
        sums_d = dram("sums_d", (P * TG, ROW))

        def sb(name, shape, dt=F32):
            return ctx.enter_context(nc.sbuf_tensor(name, shape, dt))

        def sem(name):
            return ctx.enter_context(nc.semaphore(name))

        SORT_AREA = 2 * ROUTE_W + 2 * CHUNK_W + 2 * E1_W + 2 * HCOLS + STEPS
        big = sb("big", [P, NBP * D + SORT_AREA])
        nodes = big[:, 0:NBP * D]
        o = NBP * D
        chunkbuf = [big[:, o:o + CHUNK_W], big[:, o + CHUNK_W:o + 2 * CHUNK_W]]
        routebuf = [big[:, o:o + ROUTE_W], big[:, o + ROUTE_W:o + 2 * ROUTE_W]]
        r_src = big[:, o + ROUTE_W:o + ROUTE_W + E2_W].bitcast(I32)
        r_dst = big[:, o + ROUTE_W + E2_W:o + ROUTE_W + 2 * E2_W].bitcast(I32)
        o += 2 * ROUTE_W
        pairs = big[:, o:o + 2 * CHUNK_W].rearrange("p (t w) -> p t w", w=2)
        pairs_i = big[:, o:o + 2 * CHUNK_W].bitcast(I32).rearrange("p (t w) -> p t w", w=2)
        block_over = big[:, o:o + C_STEPS]
        key2 = big[:, o:o + TG + 1].bitcast(I32)
        mark_tmp = big[:, o + TG + 1:o + TG + 1 + MARKS].bitcast(I32)
        o += 2 * CHUNK_W
        rows_raw = big[0:E1_P, o:o + E1_W].bitcast(I32)
        cols_raw = big[0:E1_P, o + E1_W:o + 2 * E1_W].bitcast(I32)
        o += 2 * E1_W
        dig_hi, dig_lo = big[:, o:o + HCOLS], big[:, o + HCOLS:o + 2 * HCOLS]
        o += 2 * HCOLS
        block_base = big[:, o:o + STEPS]
        o += STEPS
        assert o == NBP * D + SORT_AREA

        area = [NBP * D]

        def over(*shape):
            size = 1
            for d in shape:
                size *= d
            columns = big[:, area[0]:area[0] + size]
            area[0] += size
            if len(shape) == 1:
                return columns
            if len(shape) == 2:
                return columns.rearrange("p (a b) -> p a b", a=shape[0])
            return columns.rearrange("p (a b c) -> p a b c", a=shape[0], b=shape[1])

        edge_ring = over(GG, GW, ROW)
        head_row = over(ROW)
        gat_slot = over(GG, GW).bitcast(I32)
        b_first, b_in, b_reset = over(GW), over(GW), over(GW)
        e_blk = over(GW, HEADS)
        m_run = over(GW + 1, HEADS)
        expo = over(GW, 2 * HEADS)
        keep = over(GW, HEADS)
        carry_dst, carry_sum = over(HEADS), over(NS)
        tails = over(4, NS)
        spill_lo = over(P)
        spill_hi = over(NB, NC)
        carried = over(NB, NC)
        m_carried, m_node = over(NB, HEADS), over(NB, HEADS)
        shares = over(2, NB, HEADS)
        row_vals = over(NC)
        nsum = over(NB, ROW)
        nw = [over(NB * FEAT) for _ in range(3)]
        nv = [over(NB) for _ in range(14)]
        score = [over(NB) for _ in range(EXP)]
        rank = [over(NB) for _ in range(EXP)]
        den = over(NB, HEADS)
        assert area[0] <= NBP * D + SORT_AREA

        gathered = sb("gathered", [P, RING, WIN, D])
        hidden = gathered[:, :, :, :].rearrange("p r t c -> p (r t c)").rearrange("p (s f c) -> p s f c", s=2, f=FC)
        mid = sb("mid", [P, RING * WIN * P])
        onehot = mid[:, :].rearrange("p (r t c) -> p r t c", r=RING, t=WIN)
        junk = sb("junk", [P, C_W], BF16)
        yst = mid[:, :].rearrange("p (s n c) -> p s n c", s=2, n=CHT)
        flat = gathered[:, :, :, :].rearrange("p r t c -> p (r t c)")
        step_iota = sb("step_iota", [P, C_STEPS])
        xn = flat[:, 0:4 * D].rearrange("p (u c) -> p u c", u=2)
        xT = flat[:, 4 * D:8 * D].rearrange("p (u c) -> p u c", u=2)
        wraw = flat[:, 12 * D:14 * D].rearrange("p (k c) -> p k c", k=KC)
        wt = flat[:, 14 * D:16 * D].rearrange("p (k c) -> p k c", k=KC)
        hst = flat[:, 8 * D:12 * D].rearrange("p (u c) -> p u c", u=2)
        mark_iota = sb("mark_iota", [P, MARKS], I32)
        node_iota = sb("node_iota", [P, 64])
        idx_slot = sb("idx_slot", [P, RING, WIN, 2])
        ident = sb("ident", [P, P])
        iota_c = sb("iota_c", [P, P])
        tri = sb("tri", [P, P])
        ones = sb("ones", [P, P])
        iota_i = sb("iota_i", [P, 8], I32)
        bits = sb("bits", [P, 8], I32)
        sign = sb("sign", [P, 8])
        thr = sb("thr", [P, NBP])
        signsum = sb("signsum", [P, CHUNKS, NBP])
        zero_bf = sb("zero_bf", [P, P], BF16)
        oh_hi = sb("oh_hi", [P, HQ, 64], BF16)
        oh_lo = sb("oh_lo", [P, HQ, P], BF16)
        late = sb("late", [P, CHT * KC * P + NBP * ROW])
        unread = late[:, 0:2 * D].rearrange("p (a c) -> p a c", a=2)
        step_tab = late[0:1, 0:2 * STEPS].bitcast(I32).rearrange("p (a k) -> p a k", a=2)
        small_row = late[0:1, 2 * STEPS:2 * STEPS + C_STEPS]
        xc = late[:, 0:CHT * KC * P].rearrange("p (n c) -> p n c", n=CHT)
        table = late[:, CHT * KC * P:].rearrange("p (n f) -> p n f", f=ROW)
        small = sb("small", [P, 16])
        small_i = sb("small_i", [P, 2], I32)
        end_idx = sb("end_idx", [P, 64], I32)
        histo = sb("histo", [P, 3, 65])
        digit_axis = sb("digit_axis", [P, P])
        last_row = sb("last_row", [P, P])
        edge_idx = sb("edge_idx", [P, TG], I32)
        starts = sb("starts", [P, TG + 1])
        inside = sb("inside", [P, TG + 1])
        stats = sb("stats", [P, NBP, 6])
        mv = sb("mv", [P, NBP, 2])
        std = sb("std", [P, NBP])
        rstd = sb("rstd", [P, NBP])
        nmr = sb("nmr", [P, NBP])
        brow = sb("brow", [1, D])
        wg = sb("wg", [P, KC, ROW])
        att_w = sb("att_w", [P, KC, FEAT])
        att = sb("att", [P, 2, FEAT])
        gpar = sb("gpar", [P, 3, FEAT])
        weights = sb("weights", [P, EXP * (KC * HID + FC * D)])
        w1s = weights[:, 0:EXP * KC * HID].rearrange("p (e k f) -> p e k f", e=EXP, k=KC)
        w2s = weights[:, EXP * KC * HID:].rearrange("p (e k f) -> p e k f", e=EXP, k=FC)
        b1s = sb("b1s", [P, EXP, FC])
        b2s = sb("b2s", [1, EXP, D])
        tails_t = sb("tails_t", [NS, 4, P])
        run_m = sb("run_m", [NS, P + 1])
        run_s = sb("run_s", [NS, P + 1])
        run_e = sb("run_e", [NS, 2, P])
        gate = sb("gate", [P, EXP, NB])
        BANK_NODES = 512 // NC
        SPILL_PARTS = [(a, min(a + BANK_NODES, NB), at) for a, at in zip(range(0, NB, BANK_NODES), (6, 7, 0))]
        head_node = sb("head_node", [P, 2])
        head_i = sb("head_i", [P, 3], I32)
        ps = ctx.enter_context(nc.psum_tensor("ps", [P, 8 * 512], F32))
        bank = lambda b: ps[:, b * 512:(b + 1) * 512]
        ps_step = [bank(2 + j)[:, 0:D] for j in range(PRING)]
        ps_hist = bank(6)[:, 0:64]
        ps_tab = bank(7)

        S = {}

        def s(name):
            if name not in S:
                S[name] = sem(name)
            return S[name]

        raw_in, x_in, w_in, w2_in = s("raw_in"), s("x_in"), s("w_in"), s("w2_in")
        raw2_in = s("raw2_in")
        consts = s("consts")
        vec = s("vec")
        sort_ready, turned, turn_copied = s("sort_ready"), s("turned"), s("turn_copied")
        half_copied, digits_in = s("half_copied"), s("digits_in")
        var_ready, std_ready, norm1_ready = s("var_ready"), s("std_ready"), s("norm1_ready")
        wt_turned, wt_copied = s("wt_turned"), s("wt_copied")
        xn_ready, xn_turned, xT_ready, h_done, h_copied = (s("xn_ready"), s("xn_turned"), s("xT_ready"),
                                                           s("h_done"), s("h_copied"))
        h_stored = [s("h_stored0"), s("h_stored1")]
        sums_ready, count_done, steps_ready, steps_done, tab_ready = (
            s("sums_ready"), s("count_done"), s("steps_ready"), s("steps_done"), s("tab_ready"))
        pairs_ready, pairs_stored = s("pairs_ready"), s("pairs_stored")
        idx_in = [s(f"idx_in{j}") for j in range(RING)]
        rows_in = [s(f"rows_in{j}") for j in range(RING)]
        onehot_ready, step_done, step_added = s("onehot_ready"), s("step_done"), s("step_added")
        digit_ready, digit_done = s("digit_ready"), s("digit_done")
        keys2_ready, keys2_stored, keys2_in = s("keys2_ready"), s("keys2_stored"), s("keys2_in")
        hist_copied, hist_summed = s("hist_copied"), s("hist_summed")
        xn2_ready, xn2_turned, xT2_ready, g_done, g_copied = (s("xn2_ready"), s("xn2_turned"), s("xT2_ready"),
                                                              s("g_done"), s("g_copied"))
        xT_stored = [s("xT_stored0"), s("xT_stored1")]
        wg_ready = s("wg_ready")
        table_ready, table_stored = s("table_ready"), s("table_stored")
        slot_ready, gathers_begun = s("slot_ready"), s("gathers_begun")
        gat_in = [s(f"gat_in{g}") for g in range(GG)]
        xc_in, up_done, act_done, down_done, y_copied = (s("xc_in"), s("up_done"), s("act_done"),
                                                         s("down_done"), s("y_copied"))
        y_stored = [s("y_stored0"), s("y_stored1")]
        head_in, block_steps, block_expo, block_exp, block_summed = (
            s("head_in"), s("block_steps"), s("block_expo"), s("block_exp"), s("block_summed"))
        block_stored = [s(f"block_stored{g}") for g in range(GG)]
        tails_ready, tails_turned, run_expo, run_exp, runs_ready, runs_turned = (
            s("tails_ready"), s("tails_turned"), s("run_expo"), s("run_exp"), s("runs_ready"), s("runs_turned"))
        spill_ready, spill_done, node_sums_in = s("spill_ready"), s("spill_done"), s("node_sums_in")
        share_expo, share_exp = s("share_expo"), s("share_exp")
        rvar_ready, rstd_in, d_ready, dexp_ready = s("rvar_ready"), s("rstd_in"), s("d_ready"), s("dexp_ready")
        stats_in, fin_step, fin_out = s("stats_in"), s("fin_step"), s("fin_out")
        x_summed, mean_ready, x_squared, var1_ready = s("x_summed"), s("mean_ready"), s("x_squared"), s("var1_ready")

        PAIR = 2 * EXP * D
        fin_slot = ([weights[:, q * PAIR:(q + 1) * PAIR] for q in range(EXP * (KC * HID + FC * D) // PAIR)]
                    + [flat[:, q * PAIR:(q + 1) * PAIR] for q in range(RING * WIN * D // PAIR)])
        fin_slot = [a.rearrange("p (t e c) -> p t e c", t=2, e=EXP) for a in fin_slot]
        FR = len(fin_slot)
        PAIRS = NB // 2
        assert PAIRS % FR == 0 and NB % 2 == 1
        fin_in = [s(f"fin_in{j}") for j in range(FR)]

        UNITS = NBP // 2
        C_TURNS = len(TURN_OF["chunk"])
        FIRST_TURNS = 2
        LAYER_PARTS = ((2, 2, 1, 1), (2, 4, 3, 0), (4, 6, 4, 1), (6, 8, 6, 1), (8, 10, 7, 0), (10, UNITS // 2, 11, NBP))
        assert C_TURNS == FIRST_TURNS + 2 * len(LAYER_PARTS)
        LAY_AT = {len(CHUNK_STEPS) - 7 + 2 * stage: stage for stage in range(4)}
        FIRST_LAY_AT = {len(CHUNK_STEPS) - 3 + stage: stage for stage in range(3)}
        chunk_side = []
        for at, st in enumerate(CHUNK_STEPS):
            if at in LAY_AT:
                chunk_side.append(("lay", LAY_AT[at]))
            chunk_side.append(("chunk", st))
        chunk_side.append(("pairs", None))
        side = chunk_side + [("keys", None)] + [("route", st) for st in ROUTE_STEPS] + [("save", None), ("flags", None)]
        weight = {"chunk": 1.2, "lay": 1.5, "pairs": 4.0, "keys": 6.0, "route": 2.3, "save": 9.0, "flags": 8.0}
        share = sum(weight[kind] for kind, _ in side) / (ITERS - 6)
        assert sum(weight[kind] for kind, _ in chunk_side) < share * (C_ITERS - 2)
        BURSTS, at, spent = [], 0, 0.0
        for n in range(1, ITERS):
            take = at
            while take < len(side) and (spent < share * n or n == ITERS - 1):
                spent += weight[side[take][0]]
                take += 1
            BURSTS.append((side[at:take], n))
            at = take
        assert at == len(side)

        block = ctx.enter_context(nc.Block())

        @block.sync
        def _(sp):
            sp.dma_start(rows_raw, src.rearrange("(p t) -> p t", p=E1_P)).then_inc(raw_in, 16)
            sp.dma_start(cols_raw, dst.rearrange("(p t) -> p t", p=E1_P)).then_inc(raw_in, 16)
            sp.wait_ge(consts, 1)
            n3 = nodes.rearrange("p (n c) -> p n c", c=D)
            sp.dma_start(n3[:, 0:NB - 1, :], x[0:(NB - 1) * P, :].rearrange("(n p) c -> p n c", p=P)).then_inc(x_in, 16)
            sp.dma_start(n3[0:TAIL, NB - 1, :], x[(NB - 1) * P:N, :]).then_inc(x_in, 16)
            sp.dma_start(wraw[:, :, :], gnn_W.rearrange("(k p) c -> p k c", p=P)).then_inc(w_in, 16)
            sp.dma_start(brow[:, :], gnn_b.rearrange("(a c) -> a c", a=1)).then_inc(w_in, 16)
            e2 = edge_index.rearrange("a (p t) -> a p t", p=P)
            sp.dma_start(r_src, e2[0]).then_inc(raw2_in, 16)
            sp.dma_start(r_dst, e2[1]).then_inc(raw2_in, 16)
            sp.dma_start(wg[:, :, 0:FEAT], W_gat.rearrange("(k p) f -> p k f", p=P)).then_inc(w2_in, 16)
            for q, a in enumerate((att_src, att_dst)):
                sp.dma_start(att[:, q, :], a.rearrange("(o h) e -> o (h e)", o=1).to_broadcast([P, FEAT])).then_inc(w2_in, 16)
            for q, a in enumerate((b_gat, ln_gamma, ln_beta)):
                sp.dma_start(gpar[:, q, :], a.rearrange("(o f) -> o f", o=1).to_broadcast([P, FEAT])).then_inc(w2_in, 16)
            for e in range(EXP):
                sp.dma_start(w1s[:, e, :, :], W1[e].rearrange("(k p) f -> p k f", p=P)).then_inc(w2_in, 16)
                sp.dma_start(w2s[:, e, :, :], W2[e].rearrange("(k p) f -> p k f", p=P)).then_inc(w2_in, 16)
                sp.dma_start(b1s[:, e, :], b1[e].rearrange("(f p) -> p f", p=P), allow_slow_non_contiguous=True).then_inc(w2_in, 16)
            sp.dma_start(b2s[:, :, :], b2.rearrange("(o e) c -> o e c", o=1)).then_inc(w2_in, 16)
            h_u = h_d.rearrange("(u t p) c -> p u t c", t=2, p=P)

            def store_h(u, par):
                sp.wait_ge(h_copied, u + 1)
                sp.dma_start(h_u[:, bass.ds(u, 1), :, :].rearrange("p o t c -> p (o t) c"),
                             hst[:, par, :].rearrange("p (t c) -> p t c", t=2)).then_inc(h_stored[par], 16)

            with sp.Fori(0, UNITS // 2) as i:
                for par in range(2):
                    store_h(2 * i + par, par)
            store_h(UNITS - 1, 0)
            sp.wait_ge(pairs_stored, 16)
            sp.wait_ge(tab_ready, 1)

            def load_step(i, j, first):
                if not first:
                    sp.wait_ge(step_done, i * RING + j + 1 - RING)
                at = sp.value_load(step_tab[0:1, 0, bass.ds(i * RING + j, 1)], min_val=0, max_val=CHUNKS * P * CHUNK_W - G)
                sp.dma_start(idx_slot[:, j, :, :], pairs_d[bass.ds(at, G), :].rearrange("(p t) w -> p t w", p=P)).then_inc(idx_in[j], 16)

            for j in range(RING):
                load_step(0, j, True)
            with sp.Fori(1, C_ITERS) as i:
                for j in range(RING):
                    load_step(i, j, False)
            sp.wait_ge(pairs_stored, 32)
            sp.wait_ge(tab_ready, 2)
            with sp.Fori(C_ITERS, ITERS) as i:
                for j in range(RING):
                    load_step(i, j, False)
            def store_xT(u, par):
                sp.wait_ge(xT2_ready, u + 1)
                sp.dma_start(xT_d[:, bass.ds(2 * u, 2), :], xT[:, par, :].rearrange("p (t c) -> p t c", t=2)).then_inc(xT_stored[par], 16)

            with sp.Fori(0, UNITS // 2) as i:
                for par in range(2):
                    store_xT(2 * i + par, par)
            store_xT(UNITS - 1, 0)
            sp.wait_ge(table_ready, 1)
            sp.dma_start(tab_d.rearrange("(n p) f -> p n f", p=P), table[:, :, :]).then_inc(table_stored, 16)
            for par in range(2):
                sp.wait_ge(xT_stored[par], 16 * (UNITS // 2 + 1 - par))

            def load_chunk(start, tiles):
                sp.dma_start(xc[:, 0:tiles, :], xT_d[:, bass.ds(start, tiles), :]).then_inc(xc_in, 16)

            def expert_outputs(i, start, tiles, next_start, blocks):
                for e in range(EXP):
                    if e == EXP - 1 and next_start is not None:
                        sp.wait_ge(up_done, (i + 1) * EXP * FC)
                        load_chunk(next_start, CHT)
                    sp.wait_ge(y_copied, EXP * i + e + 1)
                    sp.dma_start(y_d[bass.ds(start * P, tiles * P), e, :].rearrange("(n p) c -> p n c", p=P),
                                 yst[:, e % 2, 0:tiles, :]).then_inc(y_stored[e % 2], 16)
                    if blocks and e < GG:
                        k = (i - 1) * GG + e
                        sp.wait_ge(block_summed, k + 1)
                        sp.dma_start(sums_d.rearrange("(p t) f -> p t f", p=P)[:, bass.ds(k * GW, GW), :],
                                     edge_ring[:, e, :, :]).then_inc(block_stored[e], 16)

            load_chunk(NCH * CHT, REST)
            expert_outputs(0, NCH * CHT, REST, 0, False)
            with sp.Fori(1, NCH) as i:
                expert_outputs(i, (i - 1) * CHT, CHT, i * CHT, True)
            expert_outputs(NCH, (NCH - 1) * CHT, CHT, None, True)
            for e in range(2):
                sp.wait_ge(y_stored[e], 16 * (NCH + 1) * EXP // 2)

            def load_final(q, j):
                sp.dma_start(fin_slot[j].rearrange("p t e c -> p t (e c)"),
                             y_d[bass.ds(q * 2 * P, 2 * P), :, :].rearrange("(t p) e c -> p t (e c)", p=P)).then_inc(fin_in[j], 16)

            def store_final(q):
                sp.wait_ge(fin_step, 2 * EXP * (q + 1))
                sp.dma_start(out[bass.ds(q * 2 * P, 2 * P), :].rearrange("(t p) c -> p t c", p=P),
                             nodes[:, bass.ds(q * 2 * D, 2 * D)].rearrange("p (t c) -> p t c", t=2)).then_inc(fin_out, 16)

            for j in range(FR):
                load_final(j, j)
            with sp.Fori(0, PAIRS // FR - 1) as i:
                for j in range(FR):
                    store_final(i * FR + j)
                    load_final((i + 1) * FR + j, j)
            for j in range(FR):
                store_final(PAIRS - FR + j)
                if j == 0:
                    sp.dma_start(fin_slot[0][0:TAIL, 0, :, :], y_d[(NB - 1) * P:N, :, :]).then_inc(fin_in[0], 16)
            sp.wait_ge(fin_step, (2 * PAIRS + 1) * EXP)
            sp.dma_start(out[(NB - 1) * P:N, :], nodes[0:TAIL, (NB - 1) * D:NB * D]).then_inc(fin_out, 16)
            sp.wait_ge(fin_out, 16 * (PAIRS + 1))

        @block.gpsimd
        def _(pool):
            nc.gpsimd.memset(nodes[:, (NB - 1) * D:NBP * D], 0.0).then_inc(consts, 1)
            nc.gpsimd.memset(ident[:, :], 0.0).then_inc(consts, 1)
            nc.gpsimd.memset(tri[:, :], 1.0).then_inc(consts, 1)
            pool.wait_ge(consts, 3)
            nc.gpsimd.affine_select(out=ident[:, :], in_=ident[:, :], compare_op=ALU.not_equal, fill=1.0, base=0,
                                    pattern=[[-1, P]], channel_multiplier=1).then_inc(consts, 1)
            nc.gpsimd.affine_select(out=tri[:, :], in_=tri[:, :], compare_op=ALU.is_ge, fill=0.0, base=0,
                                    pattern=[[1, P]], channel_multiplier=-1).then_inc(consts, 1)
            nc.gpsimd.memset(ones[:, :], 1.0).then_inc(consts, 1)
            nc.gpsimd.memset(zero_bf[:, :], 0.0).then_inc(consts, 1)
            nc.gpsimd.iota(iota_i[:, :], [[0, 8]], base=0, channel_multiplier=1).then_inc(consts, 1)
            nc.gpsimd.iota(iota_c[:, :], [[1, P]], base=0, channel_multiplier=0,
                           allow_small_or_imprecise_dtypes=True).then_inc(consts, 1)
            nc.gpsimd.iota(thr[:, :], [[-P, NBP]], base=0, channel_multiplier=0,
                           allow_small_or_imprecise_dtypes=True).then_inc(consts, 1)
            nc.gpsimd.iota(step_iota[:, :], [[1, C_STEPS]], base=0, channel_multiplier=0,
                           allow_small_or_imprecise_dtypes=True).then_inc(consts, 1)
            nc.gpsimd.iota(mark_iota[:, :], [[1, MARKS]], base=0, channel_multiplier=MARKS).then_inc(consts, 1)
            nc.gpsimd.iota(node_iota[:, :], [[P, 64]], base=0, channel_multiplier=1,
                           allow_small_or_imprecise_dtypes=True).then_inc(consts, 1)
            pool.wait_ge(x_summed, NBP)
            nc.gpsimd.tensor_scalar(nmr[:, :], mv[:, :, 0], -1.0 / D, None, ALU.mult).then_inc(mean_ready, 1)
            pool.wait_ge(x_squared, NBP)
            nc.gpsimd.tensor_scalar(mv[:, :, 1], mv[:, :, 1], 1.0 / D, EPS, ALU.mult, ALU.add).then_inc(var1_ready, 1)
            for t in range(2):
                pool.wait_ge(h_stored[t], 16 * (UNITS // 2 + 1 - t))

            def gather_step(i, j, first):
                pool.wait_ge(idx_in[j], 16 * i + 16)
                if not first:
                    pool.wait_ge(step_done, i * RING + j + 1 - RING)
                pool.sem_inc(gathers_begun, 1)
                for t in range(WIN):
                    nc.gpsimd.indirect_dma_start(
                        gathered[:, j, t, :], None, h_d[:, :],
                        bass.IndirectOffsetOnAxis(ap=idx_slot[:, j, t, 1:2].bitcast(I32), axis=0)).then_inc(rows_in[j], 16)

            for j in range(RING):
                gather_step(0, j, True)
            with pool.Fori(1, ITERS) as i:
                for j in range(RING):
                    gather_step(i, j, False)
            pool.wait_ge(table_stored, 16)
            pool.wait_ge(slot_ready, 1)
            nc.gpsimd.indirect_dma_start(
                head_row, None, tab_d[:, :], bass.IndirectOffsetOnAxis(ap=head_i[:, 0:1], axis=0)).then_inc(head_in, 16)

            def gather_block(i, g, first):
                pool.wait_ge(slot_ready, GG * i + g + 2)
                if not first:
                    pool.wait_ge(block_stored[g], 16 * i)
                pool.sem_inc(gathers_begun, 1)
                for q in range(GW):
                    nc.gpsimd.indirect_dma_start(
                        edge_ring[:, g, q, :], None, tab_d[:, :],
                        bass.IndirectOffsetOnAxis(ap=gat_slot[:, g, q:q + 1], axis=0)).then_inc(gat_in[g], 16)

            for g in range(GG):
                gather_block(0, g, True)
            with pool.Fori(1, NCH) as i:
                for g in range(GG):
                    gather_block(i, g, False)
            for g in range(GG):
                pool.wait_ge(block_stored[g], 16 * NCH)
            for n in range(NB):
                nc.gpsimd.indirect_dma_start(
                    nsum[:, n, :], None, sums_d[:, :],
                    bass.IndirectOffsetOnAxis(ap=end_idx[:, n:n + 1], axis=0)).then_inc(node_sums_in, 16)
        @block.scalar
        def _(act):
            act.wait_ge(wt_turned, 1)
            nc.scalar.activation(wt.rearrange("p k c -> p (k c)"), bank(7), ACT.Copy).then_inc(wt_copied, 1)
            turns_done = [0, 0]

            def turn_copies(net):
                bufs, halves = (chunkbuf, 1) if net == "chunk" else (routebuf, 2)
                of = TURN_OF[net]
                to = bufs[1 - of[turns_done[0] % len(of) if net == "chunk" else turns_done[0] - CHUNKS * C_TURNS]]
                turns_done[0] += 1
                for b in range(halves):
                    act.wait_ge(turned, turns_done[1] + 1)
                    nc.scalar.activation(to[:, b * 1024:b * 1024 + 512], bank(0), ACT.Copy).then_inc(turn_copied, 1)
                    turns_done[1] += 2

            act.wait_ge(x_in, 32)
            act.wait_ge(consts, 3)

            def node_sum(b, t, to, fun, counted, bias, first):
                if not first:
                    act.wait_ge(counted, b - 1)
                nc.scalar.activation(unread[:, t % 2, :], nodes[:, bass.ds(b * D, D)], fun, bias=bias,
                                     accum_out=mv[:, bass.ds(b, 1), to:to + 1].rearrange("p a b -> p (a b)")).then_inc(counted, 1)

            for part, (fun, counted) in enumerate(((ACT.Identity, x_summed), (ACT.Square, x_squared))):
                if part:
                    act.wait_ge(mean_ready, 1)
                    act.wait_ge(x_summed, NBP)
                bias = lambda b: nmr[:, bass.ds(b, 1)] if part else 0.0
                for b in range(2):
                    node_sum(b, b, part, fun, counted, bias(b), True)
                with act.Fori(0, (NBP - 2) // 8) as i:
                    for t in range(8):
                        b = i * 8 + t + 2
                        node_sum(b, t, part, fun, counted, bias(b), False)
            for _ in range(FIRST_TURNS):
                turn_copies("chunk")
            act.wait_ge(var1_ready, 1)
            nc.scalar.activation(std[:, :], mv[:, :, 1], ACT.Sqrt).then_inc(std_ready, 1)
            act.wait_ge(norm1_ready, 1)

            def normalise(u, par, first):
                if not first:
                    act.wait_ge(xn_turned, u - 1)
                for t in range(2):
                    last = nc.scalar.activation(xn[:, par, t * D:(t + 1) * D], nodes[:, bass.ds((2 * u + t) * D, D)],
                                                ACT.Identity, scale=rstd[:, bass.ds(2 * u + t, 1)],
                                                bias=nmr[:, bass.ds(2 * u + t, 1)])
                last.then_inc(xn_ready, 1)

            def copy_xT(u, par, first):
                act.wait_ge(xn_turned, u + 1)
                if not first:
                    act.wait_ge(h_done, u - 1)
                nc.scalar.activation(xT[:, par, :], bank(4 + par), ACT.Copy).then_inc(xT_ready, 1)

            def copy_h(u, par, first):
                act.wait_ge(h_done, u + 1)
                if not first:
                    act.wait_ge(h_stored[par], 8 * (u - par))
                nc.scalar.activation(hst[:, par, :], bank(6 + par), ACT.Copy).then_inc(h_copied, 1)

            act.wait_ge(raw_in, 32)
            act.wait_ge(consts, 14)

            def count_signs(q):
                c, b = divmod(q, NBP)
                if q:
                    act.wait_ge(sums_ready, q)
                nc.scalar.activation(junk[0:E1_P, :], rows_raw[:, c * C_W:(c + 1) * C_W], ACT.Sign,
                                     bias=thr[0:E1_P, b:b + 1],
                                     accum_out=signsum[0:E1_P, c, b:b + 1]).then_inc(sums_ready, 1)

            normalise(0, 0, True)
            normalise(1, 1, True)
            copy_xT(0, 0, True)
            normalise(2, 0, False)
            copy_xT(1, 1, True)
            copy_h(0, 0, True)
            normalise(3, 1, False)
            copy_xT(2, 0, False)
            copy_h(1, 1, True)
            signs_done = [0]

            def signs(most):
                for q in range(signs_done[0], min(signs_done[0] + most, NBP)):
                    count_signs(q)
                    signs_done[0] += 1

            for a, b, between, after in LAYER_PARTS:
                if a < b:
                    with act.Fori(a, b) as i:
                        for par in range(2):
                            u = 2 * i + par
                            normalise(u, par, False)
                            copy_xT(u - 1, 1 - par, False)
                            copy_h(u - 2, par, False)
                if b == UNITS // 2:
                    normalise(UNITS - 1, 0, False)
                    copy_xT(UNITS - 2, 1, False)
                    signs(1)
                    copy_h(UNITS - 3, 0, False)
                    copy_xT(UNITS - 1, 0, False)
                    signs(2)
                    copy_h(UNITS - 2, 1, False)
                    signs(1)
                    copy_h(UNITS - 1, 0, False)
                turn_copies("chunk")
                signs(between)
                turn_copies("chunk")
                signs(after)

            def store_pairs(c):
                act.wait_ge(pairs_ready, c + 1)
                act.dma_start(pairs_d[c * P * CHUNK_W:(c + 1) * P * CHUNK_W, :].rearrange("(p t) w -> p (t w)", p=P),
                              pairs.rearrange("p t w -> p (t w)")).then_inc(pairs_stored, 16)

            def reload_keys():
                act.wait_ge(keys2_ready, 1)
                act.dma_start(keys2_d.rearrange("(p t) -> p t", p=P), routebuf[ROUTE_IN].bitcast(I32)).then_inc(keys2_stored, 16)
                act.wait_ge(keys2_stored, 16)
                halo = bass.AP(tensor=keys2_d.tensor, offset=0, ap=[[TG, P], [1, TG + 1]])
                act.dma_start(key2, halo).then_inc(keys2_in, 16)

            def digits(i, first):
                for q in range(HQ):
                    if not first:
                        act.wait_ge(digit_done, (i - 1) * HQ + q + 1)
                    nc.scalar.activation(oh_hi[:, q, :], digit_axis[:, 0:64], ACT.Sign, bias=dig_hi[:, bass.ds(i * HQ + q, 1)])
                    nc.scalar.activation(oh_lo[:, q, :], digit_axis[:, :], ACT.Sign, bias=dig_lo[:, bass.ds(i * HQ + q, 1)]).then_inc(digit_ready, 1)

            store_pairs(0)
            act.wait_ge(digits_in, 1)
            digits(0, True)
            for q in range(NBP, 2 * NBP):
                count_signs(q)
            for entries, i in BURSTS:
                for kind, entry in entries:
                    if kind == "pairs":
                        store_pairs(1)
                    elif kind == "save":
                        reload_keys()
                    elif kind in ("chunk", "route") and entry[0] == "turn":
                        turn_copies(kind)
                digits(i, False)
            act.wait_ge(var_ready, 1)
            nc.scalar.activation(std[:, :], mv[:, :, 1], ACT.Sqrt).then_inc(std_ready, 1)

            def copy_xT2(u, par, first):
                act.wait_ge(xn2_turned, u + 1)
                if not first:
                    act.wait_ge(g_done, u - 1)
                    act.wait_ge(xT_stored[par], 8 * (u - par))
                nc.scalar.activation(xT[:, par, :], bank(4 + par), ACT.Copy).then_inc(xT2_ready, 1)

            for par in range(2):
                copy_xT2(par, par, True)
            with act.Fori(1, UNITS // 2) as i:
                for par in range(2):
                    copy_xT2(2 * i + par, par, False)
            copy_xT2(UNITS - 1, 0, False)

            def expert_chunk(i, tiles, first, blocks):
                for e in range(EXP):
                    for f in range(FC):
                        act.wait_ge(up_done, (i * EXP + e) * FC + f + 1)
                        if not (first and e < 2):
                            act.wait_ge(down_done, i * EXP + e - 1)
                        nc.scalar.activation(hidden[:, e % 2, f, 0:tiles * P], bank(f % 2)[:, 0:tiles * P], ACT.Gelu,
                                             bias=b1s[:, e, f:f + 1]).then_inc(act_done, 1)
                    act.wait_ge(down_done, i * EXP + e + 1)
                    if not (first and e < 2):
                        act.wait_ge(y_stored[e % 2], 16 * (2 * i + e // 2))
                    nc.scalar.activation(yst[:, e % 2, 0:tiles, :].rearrange("p n c -> p (n c)"),
                                         ps[:, 1024:1024 + tiles * D], ACT.Copy).then_inc(y_copied, 1)
                    if blocks and e < GG:
                        act.wait_ge(block_expo, (i - 1) * GG + e + 1)
                        nc.scalar.activation(expo, expo, ACT.Exp).then_inc(block_exp, 1)

            expert_chunk(0, REST, True, False)
            with act.Fori(1, NCH + 1) as i:
                expert_chunk(i, CHT, False, True)
            act.wait_ge(run_expo, 1)
            nc.scalar.activation(run_e[:, :, :], run_e[:, :, :], ACT.Exp).then_inc(run_exp, 1)
            act.wait_ge(share_expo, 1)
            nc.scalar.activation(shares, shares, ACT.Exp).then_inc(share_exp, 1)
            act.wait_ge(rvar_ready, 1)
            nc.scalar.activation(nv[1], nv[1], ACT.Sqrt).then_inc(rstd_in, 1)
            act.wait_ge(d_ready, 1)
            nc.scalar.activation(nv[13], nv[12], ACT.Exp).then_inc(dexp_ready, 1)

        @block.tensor
        def _(pe):
            pe.wait_ge(consts, 4)
            pe.wait_ge(w_in, 32)
            for k in range(KC):
                for m in range(KC):
                    last = nc.tensor.transpose(bank(7)[:, (k * KC + m) * P:(k * KC + m + 1) * P],
                                               wraw[:, m, k * P:(k + 1) * P], ident[:, :])
            last.then_inc(wt_turned, 1)
            pe.wait_ge(wt_copied, 1)
            pe.wait_ge(consts, 6)

            def turn_x(u, par, ready, turned_x, first, until):
                pe.wait_ge(ready, u + 1)
                if not first:
                    pe.wait_ge(until, u - 1)
                for t in range(2 * KC):
                    last = nc.tensor.transpose(bank(4 + par)[:, t * P:(t + 1) * P], xn[:, par, t * P:(t + 1) * P], ident[:, :])
                last.then_inc(turned_x, 1)

            def multiply_h(u, par, first):
                pe.wait_ge(xT_ready, u + 1)
                if not first:
                    pe.wait_ge(h_copied, u - 1)
                for t in range(2):
                    o = bank(6 + par)[:, t * D:(t + 1) * D]
                    for k in range(KC):
                        at = (t * KC + k) * P
                        nc.tensor.matmul(o, xT[:, par, at:at + P], wt[:, k, :], start=(k == 0), stop=False)
                    last = nc.tensor.matmul(o, ones[0:1, :], brow[0:1, :], start=False, stop=True)
                last.then_inc(h_done, 1)

            turns_done = [0]
            copies_done = [0, 0]

            def turn(net):
                bufs, halves = (chunkbuf, 1) if net == "chunk" else (routebuf, 2)
                of = TURN_OF[net]
                frm = bufs[of[turns_done[0] % len(of) if net == "chunk" else turns_done[0] - CHUNKS * C_TURNS]]
                turns_done[0] += 1
                pe.wait_ge(sort_ready, turns_done[0])
                for half in range(halves):
                    for b in range(2):
                        if half and b == 0:
                            pe.wait_ge(turn_copied, copies_done[0] + 1)
                        if half and b == 1:
                            pe.wait_ge(half_copied, copies_done[1] + 1)
                        for q in range(4):
                            at = (8 * half + 4 * b + q) * P
                            last = nc.tensor.transpose(bank(b)[:, q * P:(q + 1) * P], frm[:, at:at + P], ident[:, :])
                        last.then_inc(turned, 1)
                copies_done[0] += halves
                copies_done[1] += halves - 1

            for _ in range(FIRST_TURNS):
                turn("chunk")
            turn_x(0, 0, xn_ready, xn_turned, True, None)
            turn_x(1, 1, xn_ready, xn_turned, True, None)
            multiply_h(0, 0, True)
            turn_x(2, 0, xn_ready, xn_turned, False, xT_ready)
            multiply_h(1, 1, True)
            turn_x(3, 1, xn_ready, xn_turned, False, xT_ready)
            multiply_h(2, 0, False)
            for a, b, _, _ in LAYER_PARTS:
                if a < b:
                    with pe.Fori(a, b) as i:
                        for par in range(2):
                            u = 2 * i + par
                            turn_x(u, par, xn_ready, xn_turned, False, xT_ready)
                            multiply_h(u - 1, 1 - par, False)
                if b == UNITS // 2:
                    turn_x(UNITS - 1, 0, xn_ready, xn_turned, False, xT_ready)
                    multiply_h(UNITS - 2, 1, False)
                    multiply_h(UNITS - 1, 0, False)
                turn("chunk")
                turn("chunk")

            def lay_steps(c, stage):
                if stage == 0:
                    pe.wait_ge(sums_ready, (c + 1) * NBP)
                    nc.tensor.matmul(ps_tab[0:NB, 0:1], signsum[0:E1_P, c, 0:NB], ones[0:E1_P, 0:1], start=True, stop=True)
                    nc.tensor.matmul(ps_tab[0:NB, 1:2], signsum[0:E1_P, c, 1:NBP], ones[0:E1_P, 0:1], start=True, stop=True).then_inc(count_done, 1)
                elif stage == 1:
                    pe.wait_ge(steps_ready, 3 * c + 1)
                    nc.tensor.matmul(ps_tab[0:NB, 2:3], tri[0:NB, 0:NB], small[0:NB, 3:4], start=True, stop=True).then_inc(count_done, 1)
                elif stage == 2:
                    pe.wait_ge(steps_ready, 3 * c + 2)
                    nc.tensor.matmul(ps_tab[:, 0:C_STEPS], ones[0:NB, :], block_over[0:NB, :], start=True, stop=True).then_inc(steps_done, 1)
                else:
                    pe.wait_ge(steps_ready, 3 * c + 3)
                    nc.tensor.matmul(ps_tab[0:1, 0:C_STEPS], small[0:NB, 5:6], block_over[0:NB, :], start=True, stop=True).then_inc(steps_done, 1)

            pe.wait_ge(h_copied, UNITS)
            for stage in range(4):
                lay_steps(0, stage)
            pe.wait_ge(consts, 7)
            nc.tensor.matmul(ps_hist, zero_bf[:, :], zero_bf[:, 0:64], start=True, stop=False)

            def step(i, j, first):
                pe.wait_ge(onehot_ready, i * RING + j + 1)
                pe.wait_ge(rows_in[j], 32 * i + 32)
                if not (first and j < PRING):
                    pe.wait_ge(step_added, i * RING + j + 1 - PRING)
                for t in range(WIN):
                    last = nc.tensor.matmul(ps_step[j % PRING], onehot[:, j, t, :], gathered[:, j, t, :],
                                            start=(t == 0), stop=(t == WIN - 1))
                last.then_inc(step_done, 1)

            def digits(i):
                for q in range(HQ):
                    pe.wait_ge(digit_ready, i * HQ + q + 1)
                    nc.tensor.matmul(ps_hist, oh_lo[:, q, :], oh_hi[:, q, :], start=False, stop=False).then_inc(digit_done, 1)

            for j in range(RING):
                step(0, j, True)
            digits(0)
            for entries, i in BURSTS:
                for kind, entry in entries:
                    if kind == "lay":
                        lay_steps(1, entry)
                    elif kind in ("chunk", "route") and entry[0] == "turn":
                        turn(kind)
                for j in range(RING):
                    step(i, j, False)
                digits(i)
            nc.tensor.matmul(ps_hist, zero_bf[:, :], zero_bf[:, 0:64], start=False, stop=True).then_inc(digit_done, 1)
            pe.wait_ge(hist_copied, 1)
            nc.tensor.matmul(ps_tab[:, 0:64], last_row[:, :], histo[:, 0, 1:65], start=True, stop=True).then_inc(hist_summed, 1)
            pe.wait_ge(w2_in, 16 * (7 + 3 * EXP))

            pe.wait_ge(wg_ready, 1)

            def multiply_g(u, par, first):
                pe.wait_ge(xT2_ready, u + 1)
                if not first:
                    pe.wait_ge(g_copied, u - 1)
                for t in range(2):
                    for k in range(KC):
                        at = (t * KC + k) * P
                        last = nc.tensor.matmul(bank(6 + par)[:, t * ROW:(t + 1) * ROW], xT[:, par, at:at + P], wg[:, k, :],
                                                start=(k == 0), stop=(k == KC - 1))
                last.then_inc(g_done, 1)

            turn_x(0, 0, xn2_ready, xn2_turned, True, None)
            turn_x(1, 1, xn2_ready, xn2_turned, True, None)
            multiply_g(0, 0, True)
            turn_x(2, 0, xn2_ready, xn2_turned, False, xT2_ready)
            multiply_g(1, 1, True)
            turn_x(3, 1, xn2_ready, xn2_turned, False, xT2_ready)
            multiply_g(2, 0, False)
            with pe.Fori(2, UNITS // 2) as i:
                for par in range(2):
                    u = 2 * i + par
                    turn_x(u, par, xn2_ready, xn2_turned, False, xT2_ready)
                    multiply_g(u - 1, 1 - par, False)
            turn_x(UNITS - 1, 0, xn2_ready, xn2_turned, False, xT2_ready)
            multiply_g(UNITS - 2, 1, False)
            multiply_g(UNITS - 1, 0, False)

            def expert_chunk(i, tiles, first):
                T = tiles * P
                pe.wait_ge(xc_in, 16 * i + 16)
                for e in range(EXP):
                    for f in range(FC):
                        if not (first and e == 0 and f < 2):
                            pe.wait_ge(act_done, (i * EXP + e) * FC + f - 1)
                        for k in range(KC):
                            last = nc.tensor.matmul(bank(f % 2)[:, 0:T], w1s[:, e, k, f * P:(f + 1) * P],
                                                    xc[:, 0:tiles, k * P:(k + 1) * P], start=(k == 0), stop=(k == KC - 1))
                        last.then_inc(up_done, 1)
                    pe.wait_ge(act_done, (i * EXP + e + 1) * FC)
                    if not (first and e == 0):
                        pe.wait_ge(y_copied, i * EXP + e)
                    for n in range(tiles):
                        y = ps[:, 1024 + n * D:1024 + (n + 1) * D]
                        for f in range(FC):
                            nc.tensor.matmul(y, hidden[:, e % 2, f, n * P:(n + 1) * P], w2s[:, e, f, :], start=(f == 0), stop=False)
                        last = nc.tensor.matmul(y, ones[0:1, :], b2s[0:1, e, :], start=False, stop=True)
                    last.then_inc(down_done, 1)

            expert_chunk(0, REST, True)
            with pe.Fori(1, NCH + 1) as i:
                expert_chunk(i, CHT, False)
            pe.wait_ge(tails_ready, 1)
            for q in range(4):
                last = nc.tensor.transpose(bank(4)[0:NS, q * P:(q + 1) * P], tails[:, q, :], ident[:, :])
            last.then_inc(tails_turned, 1)
            pe.wait_ge(runs_ready, 1)
            nc.tensor.transpose(bank(5)[:, 0:NS], run_s[:, 0:P], ident[0:NS, 0:NS])
            nc.tensor.transpose(bank(5)[:, NS:2 * NS], run_m[:, 0:P], ident[0:NS, 0:NS]).then_inc(runs_turned, 1)
            pe.wait_ge(spill_ready, 1)
            for a, b, at in SPILL_PARTS:
                last = nc.tensor.matmul(bank(at)[:, 0:(b - a) * NC], spill_lo, spill_hi[:, a:b, :].rearrange("p n f -> p (n f)"),
                                        start=True, stop=True)
            last.then_inc(spill_done, 1)

        @block.vector
        def _(dve):
            V = nc.vector
            n = [0]

            def done(ins):
                n[0] += 1
                ins.then_inc(vec, 1)
                dve.wait_ge(vec, n[0])

            turns_done = [0, 0]

            def sort_step(net, which):
                kind, cur, *what = which
                bufs = chunkbuf if net == "chunk" else routebuf
                frm, to = bufs[cur], bufs[1 - cur]
                if kind == "flip":
                    a, b = what
                    if b is None:
                        done(V.tensor_scalar(to, frm, sign[:, a:a + 1], None, ALU.mult))
                    else:
                        done(V.tensor_scalar(to, frm, sign[:, a:a + 1], sign[:, b:b + 1], ALU.mult, ALU.mult))
                elif kind == "pair":
                    d, mirror = what
                    f4 = frm.rearrange("p (b s d) -> p b s d", s=2, d=d)
                    t4 = to.rearrange("p (b s d) -> p b s d", s=2, d=d)
                    lo, hi, tlo, thi = f4[:, :, 0, :], f4[:, :, 1, :], t4[:, :, 0, :], t4[:, :, 1, :]
                    if mirror:
                        hi, thi = hi[:, :, ::-1], thi[:, :, ::-1]
                    V.tensor_tensor(tlo, lo, hi, ALU.min)
                    done(V.tensor_tensor(thi, lo, hi, ALU.max))
                else:
                    halves = 1 if net == "chunk" else 2
                    dve.sem_inc(sort_ready, 1)
                    for half in range(halves):
                        dve.wait_ge(turned, turns_done[0] + 2)
                        turns_done[0] += 2
                        last = V.tensor_copy(to[:, half * 1024 + 512:(half + 1) * 1024], bank(1))
                        if half < halves - 1:
                            last.then_inc(half_copied, 1)
                    done(last)
                    turns_done[1] += halves
                    dve.wait_ge(turn_copied, turns_done[1])

            def layer_stats():
                PER = 10
                with dve.Fori(0, NBP // PER) as i:
                    for b in range(PER):
                        V.bn_stats(stats[:, bass.ds(i * PER + b, 1), :].rearrange("p o s -> p (o s)"),
                                   nodes[:, bass.ds((i * PER + b) * D, D)]).then_inc(stats_in, 1)
                dve.wait_ge(stats_in, NBP)
                for b in range(NBP):
                    last = V.bn_aggr(mv[:, b, :], stats[:, b, :])
                done(last)
                done(V.tensor_scalar_add(mv[:, :, 1], mv[:, :, 1], EPS))
                dve.sem_inc(var_ready, 1)

            dve.wait_ge(raw_in, 32)
            dve.wait_ge(consts, 13)
            for k in range(7):
                V.tensor_scalar(bits[:, k:k + 1], iota_i[:, k:k + 1], k, 1, ALU.logical_shift_right, ALU.bitwise_and)
            done(V.memset(bits[:, 7:8], 0))
            V.tensor_scalar(sign[:, :], bits[:, :], -2.0, 1.0, ALU.mult, ALU.add)
            V.tensor_scalar_add(thr[:, :], thr[:, :], 0.5).then_inc(consts, 1)

            def chunk_keys(c):
                k0, k1 = chunkbuf[0].bitcast(I32), chunkbuf[1].bitcast(I32)
                cols = slice(c * C_W, (c + 1) * C_W)
                V.memset(k0, KEY_BIAS | 0x63FFE000)
                done(V.scalar_tensor_tensor(out=k1[0:E1_P, 0:C_W], in0=rows_raw[:, cols], scalar=13, in1=cols_raw[:, cols],
                                            op0=ALU.logical_shift_left, op1=ALU.bitwise_or))
                done(V.tensor_scalar(k0[0:E1_P, 0:C_W], k1[0:E1_P, 0:C_W], KEY_BIAS, None, ALU.bitwise_or))

            def chunk_pairs(c):
                srt, oth = chunkbuf[CHUNK_IN].bitcast(I32), chunkbuf[1 - CHUNK_IN].bitcast(I32)
                if c:
                    dve.wait_ge(pairs_stored, 16 * c)
                done(V.tensor_scalar(oth, srt, 13, FIELD, ALU.logical_shift_right, ALU.bitwise_and))
                V.tensor_copy(pairs[:, :, 0], oth)
                done(V.tensor_scalar(srt, srt, FIELD, None, ALU.bitwise_and))
                done(V.tensor_scalar_min(pairs_i[:, :, 1], srt, N - 1))
                dve.sem_inc(pairs_ready, 1)

            def lay_steps(c, stage):
                k = slice(c * C_STEPS, (c + 1) * C_STEPS)
                if stage == 0:
                    dve.wait_ge(count_done, 2 * c + 1)
                    done(V.tensor_scalar(small[0:NB, 0:2], ps_tab[0:NB, 0:2], -0.5, 0.5 * C_E, ALU.mult, ALU.add))
                    done(V.tensor_tensor(small[0:NB, 2:3], small[0:NB, 1:2], small[0:NB, 0:1], ALU.subtract))
                    done(V.tensor_scalar_add(small_i[0:NB, 0:1], small[0:NB, 2:3], float(G - 1)))
                    done(V.tensor_scalar(small_i[0:NB, 1:2], small_i[0:NB, 0:1], G.bit_length() - 1, None, ALU.logical_shift_right))
                    done(V.tensor_copy(small[0:NB, 3:4], small_i[0:NB, 1:2]))
                    dve.sem_inc(steps_ready, 1)
                    done(V.scalar_tensor_tensor(out=small[0:NB, 5:6], in0=small[0:NB, 3:4], scalar=-float(G), in1=small[0:NB, 2:3],
                                                op0=ALU.mult, op1=ALU.add))
                elif stage == 1:
                    if c:
                        dve.wait_ge(pairs_stored, 16 * c)
                    dve.wait_ge(count_done, 2 * c + 2)
                    done(V.tensor_copy(small[0:NB, 4:5], ps_tab[0:NB, 2:3]))
                    done(V.tensor_scalar(block_over[0:NB, :], step_iota[0:NB, :], small[0:NB, 4:5], None, ALU.is_ge))
                    dve.sem_inc(steps_ready, 1)
                elif stage == 2:
                    dve.wait_ge(steps_done, 2 * c + 1)
                    V.tensor_scalar(block_base[:, k], ps_tab[:, 0:C_STEPS], float(P), None, ALU.mult)
                    done(V.tensor_scalar(step_tab[0:1, 1, k], ps_tab[0:1, 0:C_STEPS], float(D), None, ALU.mult))
                    dve.sem_inc(steps_ready, 1)
                else:
                    dve.wait_ge(steps_done, 2 * c + 2)
                    done(V.scalar_tensor_tensor(out=small_row, in0=step_iota[0:1, :], scalar=float(G),
                                                in1=ps_tab[0:1, 0:C_STEPS], op0=ALU.mult, op1=ALU.add))
                    done(V.tensor_scalar_add(step_tab[0:1, 0, k], small_row, float(c * P * CHUNK_W)))
                    dve.sem_inc(tab_ready, 1)

            chunk_keys(0)
            AFTER_FIRST_TURNS = [at for at, which in enumerate(CHUNK_STEPS) if which[0] == "turn"][FIRST_TURNS - 1] + 1
            for at, which in enumerate(CHUNK_STEPS):
                if at == AFTER_FIRST_TURNS:
                    dve.wait_ge(std_ready, 1)
                    done(V.reciprocal(rstd[:, :], std[:, :]))
                    V.tensor_tensor(nmr[:, :], nmr[:, :], rstd[:, :], ALU.mult).then_inc(norm1_ready, 1)
                if at == AFTER_FIRST_TURNS + 12:
                    dve.wait_ge(raw2_in, 32)
                    V.tensor_scalar(dig_hi[:, 0:E2_W].bitcast(I32), r_dst, 7, None, ALU.logical_shift_right)
                    V.tensor_scalar(dig_lo[:, 0:E2_W].bitcast(I32), r_dst, P - 1, None, ALU.bitwise_and)
                    V.memset(dig_hi[:, E2_W:HCOLS], -63.0)
                    done(V.memset(dig_lo[:, E2_W:HCOLS], -float(P - 1)))
                    V.tensor_scalar(dig_hi[:, 0:E2_W], dig_hi[:, 0:E2_W].bitcast(I32), -1.0, None, ALU.mult)
                    V.tensor_scalar(dig_lo[:, 0:E2_W], dig_lo[:, 0:E2_W].bitcast(I32), -1.0, None, ALU.mult)
                    V.tensor_scalar(last_row[:, :], ones[:, :], ident[:, P - 1:P], None, ALU.mult)
                    V.tensor_scalar_add(digit_axis[:, :], iota_c[:, :], 0.5).then_inc(digits_in, 1)
                if at in FIRST_LAY_AT:
                    lay_steps(0, FIRST_LAY_AT[at])
                sort_step("chunk", which)
            lay_steps(0, 3)
            chunk_pairs(0)

            def route_keys():
                s0 = routebuf[0].bitcast(I32)
                V.memset(s0, KEY_BIAS | 0x63FFDFFF)
                done(V.scalar_tensor_tensor(out=r_src, in0=r_dst, scalar=14, in1=r_src,
                                            op0=ALU.logical_shift_left, op1=ALU.bitwise_or))
                V.tensor_scalar(s0[:, 0:E2_W], r_src, KEY_BIAS | 0x2000, None, ALU.bitwise_or)
                dve.wait_ge(pairs_stored, 16 * CHUNKS)
                done(V.scalar_tensor_tensor(out=mark_tmp, in0=mark_iota[:, :], scalar=14, in1=mark_iota[:, :],
                                            op0=ALU.logical_shift_left, op1=ALU.bitwise_or))
                done(V.tensor_scalar(s0[:, E2_W:E2_W + MARKS], mark_tmp, KEY_BIAS, None, ALU.bitwise_or))

            def route_flags():
                dve.wait_ge(keys2_in, 16)
                V.tensor_scalar(head_i[:, 1:2], key2[:, 0:1], 14 + 7, 63, ALU.logical_shift_right, ALU.bitwise_and)
                V.tensor_scalar(head_i[:, 2:3], key2[:, 0:1], 14, P - 1, ALU.logical_shift_right, ALU.bitwise_and)
                V.tensor_scalar(head_i[:, 0:1], key2[:, 0:1], 14, FIELD, ALU.logical_shift_right, ALU.bitwise_and)
                done(V.tensor_scalar(edge_idx[:, :], key2[:, 0:TG], FIELD, None, ALU.bitwise_and))
                V.tensor_copy(head_node[:, :], head_i[:, 1:3])
                V.tensor_scalar_min(head_i[:, 0:1], head_i[:, 0:1], N - 1)
                V.tensor_scalar_min(edge_idx[:, :], edge_idx[:, :], N - 1)
                done(V.tensor_scalar(key2, key2, 13, 1, ALU.logical_shift_right, ALU.bitwise_and))
                V.tensor_copy(inside[:, :], key2)
                done(V.tensor_scalar(starts[:, :], key2, -1.0, 1.0, ALU.mult, ALU.add))

            def attention_weights():
                dve.wait_ge(w2_in, 16 * (7 + 3 * EXP))
                for q in range(2):
                    done(V.tensor_tensor(att_w[:, :, :], wg[:, :, 0:FEAT], att[:, q, :].unsqueeze(1).to_broadcast([P, KC, FEAT]), ALU.mult))
                    last = V.tensor_reduce(wg[:, :, FEAT + q * HEADS:FEAT + (q + 1) * HEADS],
                                           att_w[:, :, :].rearrange("p k (h e) -> p k h e", h=HEADS), axis=AX.X, op=ALU.add)
                    if q == 0:
                        done(last)
                last.then_inc(wg_ready, 1)

            def spread(i, j, first):
                dve.wait_ge(idx_in[j], 16 * i + 16)
                if not first:
                    dve.wait_ge(step_done, i * RING + j + 1 - RING)
                V.scalar_tensor_tensor(out=onehot[:, j, :, :], in0=iota_c[:, :].unsqueeze(1).to_broadcast([P, WIN, P]),
                                       scalar=block_base[:, bass.ds(i * RING + j, 1)],
                                       in1=idx_slot[:, j, :, 0].unsqueeze(2).to_broadcast([P, WIN, P]),
                                       op0=ALU.add, op1=ALU.is_equal).then_inc(onehot_ready, 1)

            def add_step(k, j, first):
                dve.wait_ge(step_done, k + 1)
                if not first:
                    dve.wait_ge(step_added, k)
                col = dve.value_load(step_tab[0:1, 1, bass.ds(k, 1)], min_val=0, max_val=NB * D)
                V.tensor_tensor(nodes[:, bass.ds(col, D)], nodes[:, bass.ds(col, D)], ps_step[j % PRING], ALU.add).then_inc(step_added, 1)

            for j in range(RING):
                spread(0, j, True)
                if j >= PRING:
                    add_step(j - PRING, j, j == PRING)
            chunk_keys(1)
            for entries, i in BURSTS:
                for kind, entry in entries:
                    if kind == "lay":
                        lay_steps(1, entry)
                    elif kind == "pairs":
                        chunk_pairs(1)
                    elif kind == "keys":
                        route_keys()
                    elif kind == "save":
                        dve.sem_inc(keys2_ready, 1)
                    elif kind == "flags":
                        route_flags()
                        attention_weights()
                    else:
                        sort_step(kind, entry)
                for j in range(RING):
                    spread(i, j, False)
                    add_step(i * RING + j - PRING, j, False)
            for k in range(STEPS - PRING, STEPS):
                add_step(k, k % PRING, False)
            dve.wait_ge(step_added, STEPS)
            layer_stats()
            dve.wait_ge(digit_done, HCOLS + 1)
            counts, last_counts, ends_at = histo[:, 0, :], histo[:, 1, :], histo[:, 2, 0:64]
            done(V.tensor_copy(counts[:, 1:65], ps_hist))
            V.tensor_scalar(counts[:, 0:1], counts[:, 64:65], -1.0, None, ALU.mult).then_inc(hist_copied, 1)
            dve.wait_ge(hist_summed, 1)
            done(V.tensor_copy(last_counts[:, 1:65], ps_tab[:, 0:64]))
            dve.wait_ge(std_ready, 2)
            done(V.reciprocal(rstd[:, :], std[:, :]))

            def normalise(u, par, first):
                if not first:
                    dve.wait_ge(xn2_turned, u - 1)
                for t in range(2):
                    last = V.tensor_scalar(xn[:, par, t * D:(t + 1) * D], nodes[:, bass.ds((2 * u + t) * D, D)],
                                           mv[:, bass.ds(2 * u + t, 1), 0:1].rearrange("p a b -> p (a b)"),
                                           rstd[:, bass.ds(2 * u + t, 1)], ALU.subtract, ALU.mult)
                last.then_inc(xn2_ready, 1)

            def copy_g(u, par):
                dve.wait_ge(g_done, u + 1)
                V.tensor_copy(table[:, bass.ds(2 * u, 2), :],
                              bank(6 + par)[:, 0:2 * ROW].rearrange("p (t f) -> p t f", t=2)).then_inc(g_copied, 1)

            normalise(0, 0, True)
            normalise(1, 1, True)
            normalise(2, 0, False)
            copy_g(0, 0)
            normalise(3, 1, False)
            copy_g(1, 1)
            with dve.Fori(2, UNITS // 2) as i:
                for par in range(2):
                    normalise(2 * i + par, par, False)
                    copy_g(2 * i + par - 2, par)
            normalise(UNITS - 1, 0, False)
            copy_g(UNITS - 3, 0)
            copy_g(UNITS - 2, 1)
            copy_g(UNITS - 1, 0)
            dve.wait_ge(g_copied, UNITS)
            dve.sem_inc(table_ready, 1)

            dve.sem_inc(slot_ready, 1)
            for g in range(GG):
                V.tensor_copy(gat_slot[:, g, :], edge_idx[:, g * GW:(g + 1) * GW]).then_inc(slot_ready, 1)
            done(V.tensor_scalar(last_counts[:, 0:1], last_counts[:, 64:65], -1.0, None, ALU.mult))
            done(V.tensor_tensor(counts, counts, last_counts, ALU.add))
            done(V.tensor_tensor(ends_at, counts[:, 1:65], counts[:, 0:64], ALU.subtract))
            done(V.tensor_scalar(last_counts, last_counts, last_counts[:, 64:65], 0.5, ALU.add, ALU.mult))
            done(V.scalar_tensor_tensor(out=ends_at, in0=ends_at, scalar=0.25, in1=last_counts[:, 0:64], op0=ALU.mult, op1=ALU.add))
            V.tensor_tensor(end_idx[:, :], ends_at, node_iota[:, :], ALU.add)
            V.tensor_reduce(small[:, 0:1], starts[:, 0:TG], axis=AX.X, op=ALU.max)
            done(V.tensor_reduce(small[:, 1:2], starts[:, 1:TG + 1], axis=AX.X, op=ALU.max))
            V.tensor_scalar(small[:, 2:3], small[:, 0:1], NEG, None, ALU.mult)
            V.tensor_scalar(small[:, 3:4], small[:, 0:1], -1.0, 1.0, ALU.mult, ALU.add)
            done(V.tensor_tensor(small[:, 4:5], inside[:, 0:1], small[:, 1:2], ALU.mult))
            V.tensor_scalar(tails[:, 2, :], ones[:, 0:NS], small[:, 2:3], None, ALU.mult)
            V.tensor_scalar(tails[:, 3, :], ones[:, 0:NS], small[:, 3:4], None, ALU.mult)
            V.tensor_scalar(spill_lo, iota_c[:, :], head_node[:, 1:2], None, ALU.is_equal)
            V.memset(carry_sum, 0.0)
            V.memset(m_run[:, 0, :], NEG)
            V.memset(run_m[:, 0:1], NEG)
            V.memset(run_s[:, 0:1], 0.0)
            dve.wait_ge(head_in, 16)
            done(V.tensor_copy(carry_dst, head_row[:, FEAT + HEADS:ROW]))
            over_heads = lambda a: a.unsqueeze(2).to_broadcast([P, GW, HEADS])

            def router_block(i, g, more):
                k = i * GG + g
                waits = [0]

                def after(ins):
                    waits[0] += 1
                    ins.then_inc(block_steps, 1)
                    dve.wait_ge(block_steps, k * BLOCK_WAITS + waits[0])

                rows = edge_ring[:, g, :, :]
                dve.wait_ge(gat_in[g], (i + 1) * (16 * GW))
                if more:
                    V.tensor_copy(gat_slot[:, g, :], edge_idx[:, bass.ds((k + GG) * GW, GW)]).then_inc(slot_ready, 1)
                V.tensor_copy(b_first, starts[:, bass.ds(k * GW, GW)])
                V.tensor_scalar(b_reset, starts[:, bass.ds(k * GW, GW)], NEG, None, ALU.mult)
                after(V.tensor_copy(b_in, inside[:, bass.ds(k * GW, GW)]))
                after(V.tensor_tensor(rows[:, :, FEAT + HEADS:ROW], rows[:, :, FEAT + HEADS:ROW], over_heads(b_first), ALU.mult))
                for h in range(HEADS):
                    last = V.tensor_tensor_scan(e_blk[:, :, h], b_in, rows[:, :, FEAT + HEADS + h], carry_dst[:, h:h + 1], ALU.mult, ALU.add)
                after(last)
                after(V.tensor_copy(carry_dst, e_blk[:, GW - 1, :]))
                after(V.tensor_tensor(e_blk, e_blk, rows[:, :, FEAT:FEAT + HEADS], ALU.add))
                after(V.scalar_tensor_tensor(out=e_blk, in0=e_blk, scalar=0.2, in1=e_blk, op0=ALU.mult, op1=ALU.max))
                for h in range(HEADS):
                    last = V.tensor_tensor_scan(m_run[:, 1:GW + 1, h], b_reset, e_blk[:, :, h], m_run[:, 0, h:h + 1], ALU.add, ALU.max)
                after(last)
                V.tensor_tensor(expo[:, :, 0:HEADS], e_blk, m_run[:, 1:GW + 1, :], ALU.subtract)
                V.tensor_tensor(expo[:, :, HEADS:2 * HEADS], m_run[:, 0:GW, :], m_run[:, 1:GW + 1, :], ALU.subtract).then_inc(block_expo, 1)
                dve.wait_ge(block_exp, k + 1)
                V.tensor_copy(rows[:, :, NS:ROW], m_run[:, 1:GW + 1, :])
                V.tensor_copy(m_run[:, 0, :], m_run[:, GW, :])
                for h in range(HEADS):
                    V.tensor_tensor(rows[:, :, h * EXP:(h + 1) * EXP], rows[:, :, h * EXP:(h + 1) * EXP],
                                    expo[:, :, h].unsqueeze(2).to_broadcast([P, GW, EXP]), ALU.mult)
                V.tensor_copy(rows[:, :, FEAT:NS], expo[:, :, 0:HEADS])
                after(V.scalar_tensor_tensor(out=keep, in0=expo[:, :, HEADS:2 * HEADS], scalar=1.0, in1=over_heads(b_in),
                                             op0=ALU.min, op1=ALU.mult))
                for f in range(NS):
                    head = f // EXP if f < FEAT else f - FEAT
                    last = V.tensor_tensor_scan(rows[:, :, f], keep[:, :, head], rows[:, :, f], carry_sum[:, f:f + 1], ALU.mult, ALU.add)
                after(last)
                V.tensor_copy(carry_sum, rows[:, GW - 1, 0:NS]).then_inc(block_summed, 1)
                assert waits[0] == BLOCK_WAITS

            with dve.Fori(0, NCH - 1) as i:
                for g in range(GG):
                    router_block(i, g, True)
            for g in range(GG):
                router_block(NCH - 1, g, False)

            dve.wait_ge(block_summed, GG * NCH)
            V.tensor_copy(tails[:, 0, :], carry_sum)
            for h in range(HEADS):
                V.tensor_copy(tails[:, 1, h * EXP:(h + 1) * EXP], m_run[:, 0, h:h + 1].to_broadcast([P, EXP]))
            V.tensor_copy(tails[:, 1, FEAT:NS], m_run[:, 0, :]).then_inc(tails_ready, 1)
            dve.wait_ge(tails_turned, 1)
            done(V.tensor_copy(tails_t[:, :, :].rearrange("p a c -> p (a c)"), bank(4)[0:NS, :]))
            done(V.tensor_tensor_scan(run_m[:, 1:P + 1], tails_t[:, 2, :], tails_t[:, 1, :], NEG, ALU.add, ALU.max))
            V.tensor_tensor(run_e[:, 0, :], tails_t[:, 1, :], run_m[:, 1:P + 1], ALU.subtract)
            V.tensor_tensor(run_e[:, 1, :], run_m[:, 0:P], run_m[:, 1:P + 1], ALU.subtract).then_inc(run_expo, 1)
            dve.wait_ge(run_exp, 1)
            V.tensor_tensor(tails_t[:, 0, :], tails_t[:, 0, :], run_e[:, 0, :], ALU.mult)
            done(V.scalar_tensor_tensor(out=tails_t[:, 3, :], in0=run_e[:, 1, :], scalar=1.0, in1=tails_t[:, 3, :], op0=ALU.min, op1=ALU.mult))
            V.tensor_tensor_scan(run_s[:, 1:P + 1], tails_t[:, 3, :], tails_t[:, 0, :], 0.0, ALU.mult, ALU.add).then_inc(runs_ready, 1)
            dve.wait_ge(runs_turned, 1)
            V.tensor_scalar(row_vals[:, 0:NS], bank(5)[:, 0:NS], small[:, 4:5], None, ALU.mult)
            V.tensor_scalar(row_vals[:, NS:NS + HEADS], bank(5)[:, NS + FEAT:2 * NS], small[:, 4:5], None, ALU.mult)
            done(V.tensor_copy(row_vals[:, NS + HEADS:NC], small[:, 4:5]))
            V.scalar_tensor_tensor(out=spill_hi, in0=iota_c[:, 0:NB].unsqueeze(2).to_broadcast([P, NB, NC]), scalar=head_node[:, 0:1],
                                   in1=row_vals.unsqueeze(1).to_broadcast([P, NB, NC]),
                                   op0=ALU.is_equal, op1=ALU.mult).then_inc(spill_ready, 1)
            dve.wait_ge(spill_done, 1)
            for a, b, at in SPILL_PARTS:
                last = V.tensor_copy(carried[:, a:b, :].rearrange("p n f -> p (n f)"), bank(at)[:, 0:(b - a) * NC])
            done(last)
            done(V.tensor_scalar(den[:, :, 0], carried[:, :, NC - 1], -1.0, -NEG, ALU.add, ALU.mult))
            done(V.tensor_tensor(m_carried, carried[:, :, NS:NS + HEADS], den[:, :, 0].unsqueeze(2).to_broadcast([P, NB, HEADS]), ALU.add))

            dve.wait_ge(node_sums_in, 16 * NB)
            n4 = lambda a: a.rearrange("p (n h e) -> p n h e", h=HEADS, e=EXP)
            n3 = lambda a: a.rearrange("p (n f) -> p n f", f=FEAT)
            over_n = lambda a: a.unsqueeze(1).to_broadcast([P, NB, FEAT])
            over_f = lambda a: a.unsqueeze(2).to_broadcast([P, NB, FEAT])
            done(V.tensor_tensor(m_node, nsum[:, :, NS:ROW], m_carried, ALU.max))
            V.tensor_tensor(shares[:, 0, :, :], nsum[:, :, NS:ROW], m_node, ALU.subtract)
            V.tensor_tensor(shares[:, 1, :, :], m_carried, m_node, ALU.subtract).then_inc(share_expo, 1)
            dve.wait_ge(share_exp, 1)
            for part, val in enumerate((nsum, carried)):
                for h in range(HEADS):
                    V.tensor_tensor(val[:, :, h * EXP:(h + 1) * EXP], val[:, :, h * EXP:(h + 1) * EXP],
                                    shares[:, part, :, h].unsqueeze(2).to_broadcast([P, NB, EXP]), ALU.mult)
                last = V.tensor_tensor(val[:, :, FEAT:NS], val[:, :, FEAT:NS], shares[:, part, :, :], ALU.mult)
            done(last)
            done(V.tensor_tensor(nsum[:, :, 0:NS], nsum[:, :, 0:NS], carried[:, :, 0:NS], ALU.add))
            done(V.tensor_scalar_add(den, nsum[:, :, FEAT:NS], 1e-16))
            done(V.reciprocal(den, den))
            for h in range(HEADS):
                last = V.tensor_tensor(n4(nw[0])[:, :, h, :], nsum[:, :, h * EXP:(h + 1) * EXP],
                                       den[:, :, h].unsqueeze(2).to_broadcast([P, NB, EXP]), ALU.mult)
            done(last)
            done(V.tensor_tensor(n3(nw[0]), n3(nw[0]), over_n(gpar[:, 0, :]), ALU.add))
            done(V.tensor_reduce(nv[0], n3(nw[0]), axis=AX.X, op=ALU.add))
            done(V.tensor_scalar(nv[0], nv[0], 1.0 / FEAT, None, ALU.mult))
            done(V.tensor_tensor(n3(nw[1]), n3(nw[0]), over_f(nv[0]), ALU.subtract))
            done(V.tensor_tensor(nw[2], nw[1], nw[1], ALU.mult))
            done(V.tensor_reduce(nv[1], n3(nw[2]), axis=AX.X, op=ALU.add))
            V.tensor_scalar(nv[1], nv[1], 1.0 / FEAT, EPS, ALU.mult, ALU.add).then_inc(rvar_ready, 1)
            dve.wait_ge(rstd_in, 1)
            done(V.reciprocal(nv[2], nv[1]))
            done(V.tensor_tensor(n3(nw[1]), n3(nw[1]), over_f(nv[2]), ALU.mult))
            done(V.tensor_tensor(n3(nw[1]), n3(nw[1]), over_n(gpar[:, 1, :]), ALU.mult))
            done(V.tensor_tensor(n3(nw[1]), n3(nw[1]), over_n(gpar[:, 2, :]), ALU.add))
            for e in range(EXP):
                last = V.tensor_reduce(score[e], n4(nw[1])[:, :, :, e], axis=AX.X, op=ALU.add)
            done(last)
            for e in range(EXP):
                V.tensor_scalar(score[e], score[e], 1.0 / HEADS, None, ALU.mult)
                last = V.memset(rank[e], float(EXP - 1 - e))
            done(last)
            for a in range(EXP):
                for b in range(a + 1, EXP):
                    done(V.tensor_tensor(nv[0], score[a], score[b], ALU.is_ge))
                    V.tensor_tensor(rank[b], rank[b], nv[0], ALU.add)
                    done(V.tensor_tensor(rank[a], rank[a], nv[0], ALU.subtract))
            V.tensor_tensor(nv[0], score[0], score[1], ALU.max)
            done(V.tensor_tensor(nv[1], score[2], score[3], ALU.max))
            done(V.tensor_tensor(nv[0], nv[0], nv[1], ALU.max))
            done(V.scalar_tensor_tensor(out=nv[12], in0=rank[0], scalar=1.0, in1=score[0], op0=ALU.is_equal, op1=ALU.mult))
            for e in range(1, EXP):
                done(V.scalar_tensor_tensor(out=nv[1], in0=rank[e], scalar=1.0, in1=score[e], op0=ALU.is_equal, op1=ALU.mult))
                done(V.tensor_tensor(nv[12], nv[12], nv[1], ALU.add))
            V.tensor_tensor(nv[12], nv[12], nv[0], ALU.subtract).then_inc(d_ready, 1)
            dve.wait_ge(dexp_ready, 1)
            done(V.tensor_scalar_add(nv[0], nv[13], 1.0))
            done(V.reciprocal(nv[0], nv[0]))
            done(V.tensor_tensor(nv[1], nv[13], nv[0], ALU.mult))
            for e in range(EXP):
                done(V.scalar_tensor_tensor(out=nv[2], in0=rank[e], scalar=0.0, in1=nv[0], op0=ALU.is_equal, op1=ALU.mult))
                done(V.scalar_tensor_tensor(out=gate[:, e, :], in0=rank[e], scalar=1.0, in1=nv[1], op0=ALU.is_equal, op1=ALU.mult))
                done(V.tensor_tensor(gate[:, e, :], gate[:, e, :], nv[2], ALU.add))

            def combine(q, j, n_in, rows, tiles):
                dve.wait_ge(fin_in[j], 16 * n_in)
                for e in range(EXP):
                    for t in range(tiles):
                        if e:
                            dve.wait_ge(fin_step, q * 2 * EXP + (e - 1) * tiles + t + 1)
                        x1 = nodes[0:rows, bass.ds((2 * q + t) * D, D)]
                        V.scalar_tensor_tensor(out=x1, in0=fin_slot[j][0:rows, t, e, :], scalar=gate[0:rows, e, bass.ds(2 * q + t, 1)],
                                               in1=x1, op0=ALU.mult, op1=ALU.add).then_inc(fin_step, 1)

            with dve.Fori(0, PAIRS // FR) as i:
                for j in range(FR):
                    combine(i * FR + j, j, i + 1, P, 2)
            combine(PAIRS, 0, PAIRS // FR + 1, TAIL, 1)


_INS = ["x", "src", "dst", "L0_gnn_W", "L0_gnn_b", "L0_ffn_W_gat", "L0_ffn_att_src", "L0_ffn_att_dst", "L0_ffn_b_gat",
        "L0_ffn_ln_gamma", "L0_ffn_ln_beta", "L0_ffn_W1", "L0_ffn_b1", "L0_ffn_W2", "L0_ffn_b2", "L0_ffn_edge_index"]


def kernel(**inputs):
    import numpy as _np
    import concourse.bacc as _bacc
    from concourse import mybir as _mybir
    from concourse.bass_utils import run_bass_kernel_spmd as _run

    nc = _bacc.Bacc("TRN2", target_bir_lowering=False, num_devices=1)
    arrays, args = {}, []
    for name in _INS:
        a = _np.ascontiguousarray(inputs[name])
        arrays[f"in_{name}"] = a
        args.append(nc.dram_tensor(f"in_{name}", a.shape, _mybir.dt.from_np(a.dtype), kind="ExternalInput").ap())
    shape = inputs["x"].shape
    out = nc.dram_tensor("out_0", shape, _mybir.dt.float32, kind="ExternalOutput").ap()
    gnn_ffn_kernel(nc, *args, out)
    r = _run(nc, [arrays], core_ids=[0])
    return r.results[0]["out_0"]
```
